# Optimizing a Trainium2 kernel written in Bass

```python
import numpy as np
import jax
import jax.numpy as jnp

def _softmax(x, axis=-1):
    return jax.nn.softmax(x, axis=axis)

def _gelu(x):
    return jax.nn.gelu(x, approximate=True)

def _silu(x):
    return jax.nn.silu(x)

def _sigmoid(x):
    return jax.nn.sigmoid(x)

def _layernorm(x, axis=-1, eps=1e-05):
    m = jnp.mean(x, axis=axis, keepdims=True)
    v = jnp.var(x, axis=axis, keepdims=True)
    return (x - m) / jnp.sqrt(v + eps)

def _scatter_add(tgt, idx, src, axis=0):
    return tgt.at[idx].add(src)

def _segment_sum(src, seg, n):
    return jax.ops.segment_sum(src, seg, n)
kernel_name = 'mk_flamingo_gated_d2_seqx_r4_f70459'

def setup_inputs(seed: int=0):
    np.random.seed(seed)
    _w = jnp.asarray

    def _rec_inputs():
        import jax
        import jax.numpy as jnp
        _rk = jax.random.key(seed)
        x = 7.22e-05 + 1 * jax.random.normal(jax.random.fold_in(_rk, 1), (4, 512, 256), jnp.float32)
        _lenS = 512 - jax.random.randint(jax.random.fold_in(_rk, 7), (4,), 0, max(1, 512 // 4) + 1, jnp.int32)
        _lenS2 = 64 - jax.random.randint(jax.random.fold_in(_rk, 8), (4,), 0, max(1, 64 // 4) + 1, jnp.int32)
        _ctx_768P = jax.random.normal(jax.random.fold_in(_rk, 11), (4, 16, 192), jnp.float32)
        _ctx_768c = jax.random.dirichlet(jax.random.fold_in(_rk, 511), 0.3 * jnp.ones((16,), jnp.float32), (4, 64))
        _ctx_768t = jnp.einsum('bsk,bkd->bsd', _ctx_768c, _ctx_768P)
        _ctx_768t = _ctx_768t * jax.lax.rsqrt(jnp.mean(jnp.square(_ctx_768t)) + 1e-12) * 0.953939
        ctx_768 = -0.000191848 + 0.999787 * (_ctx_768t + 0.3 * jax.random.normal(jax.random.fold_in(_rk, 611), (4, 64, 192), jnp.float32))
        _g = jax.random.normal(jax.random.fold_in(_rk, 9001), (2, 2), jnp.float32)
        _g = jnp.sign(_g) * jnp.maximum(jnp.abs(_g), 1.0) + (_g == 0) * 1.0
        g_xattn = _g[0]
        g_ffn = _g[1]
        return (x, ctx_768, g_xattn, g_ffn)
    x, ctx_768, g_xattn, g_ffn = _rec_inputs()

    def _L0_xattn_setup():
        import jax, jax.numpy as jnp
        import numpy as np
        NUM_HEADS = 16
        CLAMP = 10000.0
        key = jax.random.key(seed)
        ks = jax.random.split(key, 8)
        B, Nq, Nkv, Cq, Ckv = (4, 512, 512, 256, 192)
        s_q = 1.0 / np.sqrt(Cq)
        s_kv = 1.0 / np.sqrt(Ckv)
        return {'query': jax.random.normal(ks[0], (B, Nq, Cq), jnp.float32), 'key_value': jax.random.normal(ks[1], (B, Nkv, Ckv), jnp.float32), 'Wq': jax.random.normal(ks[2], (Cq, Cq), jnp.float32) * s_q, 'bq': jnp.zeros((Cq,), jnp.float32), 'Wk': jax.random.normal(ks[3], (Ckv, Cq), jnp.float32) * s_kv, 'bk': jnp.zeros((Cq,), jnp.float32), 'Wv': jax.random.normal(ks[4], (Ckv, Cq), jnp.float32) * s_kv, 'bv': jnp.zeros((Cq,), jnp.float32), 'Wo': jax.random.normal(ks[5], (Cq, Cq), jnp.float32) * s_q, 'bo': jnp.zeros((Cq,), jnp.float32)}
    _L0_xattn_all = _L0_xattn_setup()
    _L0_xattn_in = {k: v for k, v in _L0_xattn_all.items() if k in ('Wq', 'bq', 'Wk', 'bk', 'Wv', 'bv', 'Wo', 'bo')}
    del _L0_xattn_all

    def _L0_ffn_setup():
        import jax, jax.numpy as jnp
        import numpy as np
        E = 8
        K = 2
        DIM = 256
        DFF = 512

        def _moe(x, Wg, bg, w1, w2):
            B, S, D = x.shape
            t = x.reshape(-1, D)
            logits = t @ Wg.T + bg
            probs = jax.nn.softmax(logits, axis=-1)
            topw, topi = jax.lax.top_k(probs, K)
            topw = topw / jnp.sum(topw, axis=-1, keepdims=True)
            combine = jnp.sum(jax.nn.one_hot(topi, E, dtype=t.dtype) * topw[..., None], axis=1)

            def body(acc, packed):
                w1e, w2e, ce = packed
                h = t @ w1e.T
                gate, up = jnp.split(h, 2, axis=-1)
                a = jax.nn.silu(gate) * up
                o = a @ w2e.T
                return (acc + ce[:, None] * o, None)
            out, _ = jax.lax.scan(body, jnp.zeros_like(t), (w1, w2, combine.T))
            return out.reshape(B, S, D)
        key = jax.random.key(seed)
        ks = jax.random.split(key, 5)
        B, S = (4, 512)
        x = jax.random.normal(ks[0], (B, S, DIM), dtype=jnp.float32)
        Wg = jax.random.normal(ks[1], (E, DIM), dtype=jnp.float32) * 0.02
        bg = jax.random.normal(ks[2], (E,), dtype=jnp.float32) * 0.02
        w1 = jax.random.normal(ks[3], (E, DFF, DIM), dtype=jnp.float32) * 0.02
        w2 = jax.random.normal(ks[4], (E, DIM, DFF // 2), dtype=jnp.float32) * 0.02
        return {'x': x, 'Wg': Wg, 'bg': bg, 'w1': w1, 'w2': w2}
    _L0_ffn_all = _L0_ffn_setup()
    _L0_ffn_in = {k: v for k, v in _L0_ffn_all.items() if k in ('Wg', 'bg', 'w1', 'w2')}
    del _L0_ffn_all

    def _L1_xattn_setup():
        import jax, jax.numpy as jnp
        import numpy as np
        N_HEADS = 16
        D_HEAD = 64
        key = jax.random.key(seed)
        ks = jax.random.split(key, 7)
        B, SQ, SKV = (2, 512, 512)
        D_MODEL, D_COND, D_ATTN = (256, 192, N_HEADS * D_HEAD)
        return {'x': jax.random.normal(ks[0], (B, SQ, D_MODEL), jnp.float32), 'cond': jax.random.normal(ks[1], (B, SKV, D_COND), jnp.float32), 'w_q': jax.random.normal(ks[2], (D_MODEL, D_ATTN), jnp.float32) * D_MODEL ** (-0.5), 'w_k': jax.random.normal(ks[3], (D_COND, D_ATTN), jnp.float32) * D_COND ** (-0.5), 'w_v': jax.random.normal(ks[4], (D_COND, D_ATTN), jnp.float32) * D_COND ** (-0.5), 'w_out': jax.random.normal(ks[5], (D_ATTN, D_MODEL), jnp.float32) * D_ATTN ** (-0.5), 'b_out': jnp.zeros((D_MODEL,), jnp.float32)}
    _L1_xattn_all = _L1_xattn_setup()
    _L1_xattn_in = {k: v for k, v in _L1_xattn_all.items() if k in ('w_q', 'w_k', 'w_v', 'w_out', 'b_out')}
    del _L1_xattn_all

    def _L1_ffn_setup():
        import jax, jax.numpy as jnp
        import numpy as np
        D_MODEL = 256
        M = 64
        INNER = 16
        key = jax.random.key(seed)
        ks = jax.random.split(key, 9)

        def init(k, shape, fan_in):
            bound = 1.0 / np.sqrt(fan_in)
            return jax.random.uniform(k, shape, jnp.float32, -bound, bound)
        x = jax.random.normal(ks[0], (16, 1024, D_MODEL), dtype=jnp.float32)
        Win = init(ks[1], (D_MODEL, M), D_MODEL)
        bin_ = init(ks[2], (M,), D_MODEL)
        W1 = init(ks[3], (M, INNER), 1)
        b1 = init(ks[4], (M, INNER), 1)
        W2 = init(ks[5], (M, INNER), INNER)
        b2 = init(ks[6], (M,), INNER)
        Wout = init(ks[7], (M, D_MODEL), M)
        bout = init(ks[8], (D_MODEL,), M)
        return {'x': x, 'Win': Win, 'bin_': bin_, 'W1': W1, 'b1': b1, 'W2': W2, 'b2': b2, 'Wout': Wout, 'bout': bout}
    _L1_ffn_all = _L1_ffn_setup()
    _L1_ffn_in = {k: v for k, v in _L1_ffn_all.items() if k in ('Win', 'bin_', 'W1', 'b1', 'W2', 'b2', 'Wout', 'bout')}
    del _L1_ffn_all
    return {'x': x, 'ctx_768': ctx_768, 'g_xattn': g_xattn, 'g_ffn': g_ffn, 'L0_xattn_Wq': _L0_xattn_in['Wq'], 'L0_xattn_bq': _L0_xattn_in['bq'], 'L0_xattn_Wk': _L0_xattn_in['Wk'], 'L0_xattn_bk': _L0_xattn_in['bk'], 'L0_xattn_Wv': _L0_xattn_in['Wv'], 'L0_xattn_bv': _L0_xattn_in['bv'], 'L0_xattn_Wo': _L0_xattn_in['Wo'], 'L0_xattn_bo': _L0_xattn_in['bo'], 'L0_ffn_Wg': _L0_ffn_in['Wg'], 'L0_ffn_bg': _L0_ffn_in['bg'], 'L0_ffn_w1': _L0_ffn_in['w1'], 'L0_ffn_w2': _L0_ffn_in['w2'], 'L1_xattn_w_q': _L1_xattn_in['w_q'], 'L1_xattn_w_k': _L1_xattn_in['w_k'], 'L1_xattn_w_v': _L1_xattn_in['w_v'], 'L1_xattn_w_out': _L1_xattn_in['w_out'], 'L1_xattn_b_out': _L1_xattn_in['b_out'], 'L1_ffn_Win': _L1_ffn_in['Win'], 'L1_ffn_bin_': _L1_ffn_in['bin_'], 'L1_ffn_W1': _L1_ffn_in['W1'], 'L1_ffn_b1': _L1_ffn_in['b1'], 'L1_ffn_W2': _L1_ffn_in['W2'], 'L1_ffn_b2': _L1_ffn_in['b2'], 'L1_ffn_Wout': _L1_ffn_in['Wout'], 'L1_ffn_bout': _L1_ffn_in['bout']}

def reference(x, ctx_768, g_xattn, g_ffn, L0_xattn_Wq, L0_xattn_bq, L0_xattn_Wk, L0_xattn_bk, L0_xattn_Wv, L0_xattn_bv, L0_xattn_Wo, L0_xattn_bo, L0_ffn_Wg, L0_ffn_bg, L0_ffn_w1, L0_ffn_w2, L1_xattn_w_q, L1_xattn_w_k, L1_xattn_w_v, L1_xattn_w_out, L1_xattn_b_out, L1_ffn_Win, L1_ffn_bin_, L1_ffn_W1, L1_ffn_b1, L1_ffn_W2, L1_ffn_b2, L1_ffn_Wout, L1_ffn_bout):
    import jax
    import jax.numpy as jnp

    def _L0_xattn_ref(query, key_value, Wq, bq, Wk, bk, Wv, bv, Wo, bo):
        import jax, jax.numpy as jnp
        import numpy as np
        NUM_HEADS = 16
        CLAMP = 10000.0
        B, Nq, Cq = query.shape
        Nkv = key_value.shape[1]
        H = NUM_HEADS
        D = Cq // H
        scale = D ** (-0.5)
        q = (query @ Wq + bq).reshape(B, Nq, H, D).transpose(0, 2, 1, 3)
        k = (key_value @ Wk + bk).reshape(B, Nkv, H, D).transpose(0, 2, 1, 3)
        v = (key_value @ Wv + bv).reshape(B, Nkv, H, D).transpose(0, 2, 1, 3)
        attn = jnp.einsum('bhqd,bhkd->bhqk', q, k) * scale
        attn = jnp.clip(attn, -CLAMP, CLAMP)
        attn = jax.nn.softmax(attn, axis=-1)
        attn = jnp.where(jnp.any(jnp.isnan(attn)), jnp.asarray(1.0 / Nkv, attn.dtype), attn)
        x = jnp.einsum('bhqk,bhkd->bqhd', attn, v).reshape(B, Nq, Cq)
        return x @ Wo + bo

    def _L0_ffn_ref(x, Wg, bg, w1, w2):
        import jax, jax.numpy as jnp
        import numpy as np
        E = 8
        K = 2
        DIM = 256
        DFF = 512

        def _moe(x, Wg, bg, w1, w2):
            B, S, D = x.shape
            t = x.reshape(-1, D)
            logits = t @ Wg.T + bg
            probs = jax.nn.softmax(logits, axis=-1)
            topw, topi = jax.lax.top_k(probs, K)
            topw = topw / jnp.sum(topw, axis=-1, keepdims=True)
            combine = jnp.sum(jax.nn.one_hot(topi, E, dtype=t.dtype) * topw[..., None], axis=1)

            def body(acc, packed):
                w1e, w2e, ce = packed
                h = t @ w1e.T
                gate, up = jnp.split(h, 2, axis=-1)
                a = jax.nn.silu(gate) * up
                o = a @ w2e.T
                return (acc + ce[:, None] * o, None)
            out, _ = jax.lax.scan(body, jnp.zeros_like(t), (w1, w2, combine.T))
            return out.reshape(B, S, D)
        return _moe(x, Wg, bg, w1, w2)

    def _L1_xattn_ref(x, cond, w_q, w_k, w_v, w_out, b_out):
        import jax, jax.numpy as jnp
        import numpy as np
        N_HEADS = 16
        D_HEAD = 64
        B, SQ, _ = x.shape
        SKV = cond.shape[1]
        scale = D_HEAD ** (-0.5)
        q = (x @ w_q).reshape(B, SQ, N_HEADS, D_HEAD)
        k = (cond @ w_k).reshape(B, SKV, N_HEADS, D_HEAD)
        v = (cond @ w_v).reshape(B, SKV, N_HEADS, D_HEAD)
        attn = jnp.einsum('bqhd,bkhd->bhqk', q, k) * scale
        attn = jax.nn.softmax(attn, axis=-1)
        out = jnp.einsum('bhqk,bkhd->bqhd', attn, v).reshape(B, SQ, N_HEADS * D_HEAD)
        return out @ w_out + b_out

    def _L1_ffn_ref(x, Win, bin_, W1, b1, W2, b2, Wout, bout):
        import jax, jax.numpy as jnp
        import numpy as np
        D_MODEL = 256
        M = 64
        INNER = 16
        s = jnp.einsum('btd,dm->btm', x, Win) + bin_
        h = jax.nn.relu(s[..., None] * W1 + b1)
        g = jnp.einsum('btmh,mh->btm', h, W2) + b2
        out = jnp.einsum('btm,md->btd', g, Wout) + bout
        return out
    x = x + jnp.tanh(g_xattn[0]) * _L0_xattn_ref(_layernorm(x, axis=-1), ctx_768, L0_xattn_Wq, L0_xattn_bq, L0_xattn_Wk, L0_xattn_bk, L0_xattn_Wv, L0_xattn_bv, L0_xattn_Wo, L0_xattn_bo)
    x = x + jnp.tanh(g_ffn[0]) * _L0_ffn_ref(_layernorm(x, axis=-1), L0_ffn_Wg, L0_ffn_bg, L0_ffn_w1, L0_ffn_w2)
    x = x + jnp.tanh(g_xattn[1]) * _L1_xattn_ref(_layernorm(x, axis=-1), ctx_768, L1_xattn_w_q, L1_xattn_w_k, L1_xattn_w_v, L1_xattn_w_out, L1_xattn_b_out)
    x = x + jnp.tanh(g_ffn[1]) * _L1_ffn_ref(_layernorm(x, axis=-1), L1_ffn_Win, L1_ffn_bin_, L1_ffn_W1, L1_ffn_b1, L1_ffn_W2, L1_ffn_b2, L1_ffn_Wout, L1_ffn_bout)
    return x

_drawn_inputs = setup_inputs


def setup_inputs(seed=0):
    import zlib

    import numpy as np

    out = dict(_drawn_inputs(seed))
    spreads = {'g_ffn': (-1.0, 0.6),
     'L0_xattn_bq': (0.0, 0.464),
     'L0_xattn_bk': (0.0, 2.0),
     'L0_xattn_bv': (0.0, 0.1),
     'L0_xattn_bo': (0.0, 0.1),
     'L1_xattn_b_out': (0.0, 0.432)}
    factors = {'L0_ffn_Wg': 8.0,
     'L0_ffn_bg': 8.0,
     'L0_ffn_w1': 7.323,
     'L0_ffn_w2': 7.344,
     'L1_ffn_bin_': 64.0,
     'L1_ffn_Win': 4.904,
     'L1_ffn_W1': 4.792,
     'L1_ffn_b2': 3.633,
     'L1_ffn_bout': 4.754,
     'L1_ffn_b1': 2.682}
    for name, (base, spread) in spreads.items():
        noise = np.random.default_rng([zlib.crc32(name.encode()), seed]).standard_normal(out[name].shape)
        drawn = base * np.exp(spread * noise) if base else spread * noise
        out[name] = jnp.asarray(drawn.astype(out[name].dtype))
    for name, factor in factors.items():
        out[name] = (out[name] * factor).astype(out[name].dtype)
    return out
```

```python
from contextlib import ExitStack

import numpy as np

import concourse.bass as bass
from concourse import mybir

ALU = mybir.AluOpType
ACT = mybir.ActivationFunctionType
AX = mybir.AxisListType
F32 = mybir.dt.float32
F32R = mybir.dt.float32r
I32 = mybir.dt.int32
U32 = mybir.dt.uint32
ds = bass.ds

P = 128
B, S, C = 4, 512, 256
KV, CK = 64, 192
KP = CK // 2
NTOK = B * S
TILES = NTOK // P
TPB = S // P
KC = C // P
H = 16
PAIRS = H // 2
D0 = C // H
D1 = 64
HK = H * KV
CLAMP = 10000.0
EPS = 1e-5
NE, TOPK = 8, 2
FF = 256
ITEMS = TOPK * NTOK // P + NE
SLOTS = ITEMS * P
M1, INNER = 64, 16
VW = D0 + 1
PASSES = 3

ROWS = [("ident", P), ("tri", P), ("mask", P // D0), ("rev", NE), ("item", ITEMS), ("ones", P),
        ("bq", KC), ("bk", KC), ("bv", C), ("bo", C), ("bg", NE), ("gx", 2), ("gf", 2), ("bout1", C),
        ("fbin", 1), ("fw1", INNER // 2), ("fb1", INNER // 2), ("fw2", INNER // 2), ("fb2", 1), ("fbout", C),
        ("scan", P), ("place", P), ("token", TILES)]
COL, _o = {}, 0
for _n, _w in ROWS:
    COL[_n] = (_o, _o + _w)
    _o += _w
NCOL = _o


def split3(hi_l, lo_l, hi_r, lo_r):
    return ((hi_l, hi_r), (lo_l, hi_r), (hi_l, lo_r))


def live(t):
    return not isinstance(t, int) or 0 <= t < TILES


def staged(eng, body, first, steady, after, last):
    for i in range(first, steady):
        body(i, i % 2)
    with eng.Fori(steady // 2, after // 2) as turn:
        body(2 * turn, 0)
        body(2 * turn + 1, 1)
    for i in range(after, last):
        body(i, i % 2)


def gated_blocks(nc, x, ctxt, wq0, wk0, wv0, wo0, wg, w1, w2, wqt1, wk1, wv1, wo1, fwin, fwout, rows, out):
    top = ExitStack()
    with top:
        def sbuf(name, shape, dt=F32):
            return top.enter_context(nc.sbuf_tensor(name, shape, dt))

        xres = sbuf("xres", [P, TILES, C])
        cst = sbuf("cst", [P, NCOL])
        gates = sbuf("gates", [P, 4])
        mhalf = sbuf("mhalf", [P, 1])
        slots = sbuf("slots", [P, TOPK, TILES], U32)
        wsel = sbuf("wsel", [P, TOPK, TILES])
        xn_dram = nc.dram_tensor("normed_tokens", [NTOK, C], F32).ap()
        ys_dram = nc.dram_tensor("expert_out", [SLOTS, C], F32).ap()

        def c(name):
            return cst[:, COL[name][0]:COL[name][1]]

        with ExitStack() as ffn:
            w1l = ffn.enter_context(nc.sbuf_tensor("ffn0_w1_lo", [P, NE * KC, 2 * FF], F32R))
            w2l = ffn.enter_context(nc.sbuf_tensor("ffn0_w2_lo", [P, NE * 2, C], F32R))
            w_in = ffn.enter_context(nc.semaphore("ffn0_w_in"))
            lg = ffn.enter_context(nc.sbuf_tensor("ffn0_logits", [P, TILES * NE], F32))
            attention0(nc, c, x, ctxt, wq0, wk0, wv0, wo0, rows, xres, xn_dram, cst, gates, mhalf, wg, w1, w2, w1l, w2l, w_in, lg)
            experts(nc, c, w1l, w2l, w_in, lg, xn_dram, ys_dram, gates, slots, wsel)
        attention1(nc, c, ctxt, wqt1, wk1, wv1, wo1, ys_dram, xres, gates, mhalf, slots, wsel)
        mlp1(nc, c, fwin, fwout, xres, gates, mhalf, out)


def attention0(nc, c, x, ctxt, wq0, wk0, wv0, wo0, rows, xres, xn_dram, cst, gates, mhalf, wg, w1, w2, w1l, w2l, w_in, lg):
    with ExitStack() as keep:
        def sbuf(name, shape, dt=F32, on=keep):
            return on.enter_context(nc.sbuf_tensor(f"a0_{name}", shape, dt))

        bkh, bkl = (sbuf(f"blockk_{s}", [P, B, KC, 8 * KV], F32R) for s in ("hi", "lo"))
        bvh, bvl = (sbuf(f"blockv_{s}", [P, B * PAIRS, 2 * VW], F32R) for s in ("hi", "lo"))
        wqh, wql = (sbuf(f"wq_{s}", [P, KC, C], F32R) for s in ("hi", "lo"))
        woh, wol = (sbuf(f"wo_{s}", [P, KC, C], F32R) for s in ("hi", "lo"))
        bos = sbuf("bo_scaled", [P, C])
        wghl = sbuf("wg_hi_lo", [P, KC, 2 * NE], F32R)
        mean, rstd = sbuf("ln_mean_var", [P, TILES, 2]), sbuf("ln_rstd", [P, TILES])
        prepare0(nc, c, x, ctxt, wq0, wk0, wv0, wo0, rows, xres, cst, gates, mhalf,
                 bkh, bkl, bvh, bvl, wqh, wql, woh, wol, bos, wg, wghl, mean, rstd, w1, w2, w1l, w2l, w_in)
        attend0(nc, c, xres, xn_dram, mhalf, bkh, bkl, bvh, bvl, wqh, wql, woh, wol, bos, wghl, mean, rstd, lg)


def prepare0(nc, c, x, ctxt, wq0, wk0, wv0, wo0, rows, xres, cst, gates, mhalf,
             bkh, bkl, bvh, bvl, wqh, wql, woh, wol, bos, wg, wghl, mean, rstd, w1, w2, w1l, w2l, w_in):
    with ExitStack() as ctx:
        def sbuf(name, shape, dt=F32):
            return ctx.enter_context(nc.sbuf_tensor(f"kv0_{name}", shape, dt))

        def sem(name):
            return ctx.enter_context(nc.semaphore(f"kv0_{name}"))

        ctr, cth, ctl = sbuf("ctx_raw", [KP, 2, B * KV]), sbuf("ctx_hi", [KP, 2, B * KV], F32R), sbuf("ctx_lo", [KP, 2, B * KV], F32R)
        dch, dcl = sbuf("ctx2_hi", [KP, 2, B, 2, KV], F32R), sbuf("ctx2_lo", [KP, 2, B, 2, KV], F32R)
        wkr, wkh, wkl = sbuf("wk_raw", [KP, 2, C]), sbuf("wk_hi", [KP, 2, C], F32R), sbuf("wk_lo", [KP, 2, C], F32R)
        wvr, wvh, wvl = sbuf("wv_raw", [KP, 2, C]), sbuf("wv_hi", [KP, 2, C], F32R), sbuf("wv_lo", [KP, 2, C], F32R)
        wqr, wor, wos = sbuf("wq_raw", [P, KC, C]), sbuf("wo_raw", [P, KC, C]), sbuf("wo_scaled", [P, KC, C])
        kf, vf = sbuf("k_full", [P, KC, B * KV]), sbuf("v_full", [P, B, C])
        kh, kl = sbuf("k_hi", [P, KC, B * KV]), sbuf("k_lo", [P, KC, B * KV])
        wgr = sbuf("wg_raw", [P, KC, NE])
        st, ve = sbuf("ln_stats", [P, TILES, 6]), sbuf("ln_var_eps", [P, TILES])
        psk = ctx.enter_context(nc.psum_tensor("kv0_psk", [P, KC, 512], F32))
        psv = ctx.enter_context(nc.psum_tensor("kv0_psv", [P, 2, 512], F32))

        cst_in, ctx_in, wk_in, wv_in, wq_in, wo_in = (sem(n) for n in (
            "cst_in", "ctx_in", "wk_in", "wv_in", "wq_in", "wo_in"))
        x_in = [sem(f"x_in{b}") for b in range(B)]
        gate_done, his, los = sem("gate_done"), sem("his"), sem("los")
        k_ready, v_ready, k_full, v_full = sem("k_ready"), sem("v_ready"), sem("k_full"), sem("v_full")
        kv_hi, kv_lo, wo_scaled = sem("kv_hi"), sem("kv_lo"), sem("wo_scaled_done")
        cleared, block_done, wg_in, wg_hi, wg_lo = (sem(n) for n in ("cleared", "block_done", "wg_in", "wg_hi_done", "wg_lo_done"))
        lnst, lnmv, lnve, lnrs = (sem(n) for n in ("ln_stats_done", "ln_mv_done", "ln_ve_done", "ln_rstd_done"))

        weights = [(ctr, cth, ctl, ctx_in), (wkr, wkh, wkl, wk_in), (wvr, wvh, wvl, wv_in),
                   (wqr, wqh, wql, wq_in), (wos, woh, wol, wo_scaled)]

        with nc.Block() as block:
            @block.sync
            def _(sp):
                sp.dma_start(ctr[:], ctxt.rearrange("(k p) n -> p k n", p=KP)).then_inc(ctx_in, 16)
                sp.dma_start(wkr[:], wk0.rearrange("(k p) n -> p k n", p=KP)).then_inc(wk_in, 16)
                sp.dma_start(cst[:], rows).then_inc(cst_in, 16)
                sp.dma_start(wvr[:], wv0.rearrange("(k p) n -> p k n", p=KP)).then_inc(wv_in, 16)
                sp.dma_start(wqr[:], wq0.rearrange("(k p) n -> p k n", p=P)).then_inc(wq_in, 16)
                sp.dma_start(wor[:], wo0.rearrange("(k p) n -> p k n", p=P)).then_inc(wo_in, 16)
                for b in range(B):
                    sp.dma_start(xres[:, b * TPB:(b + 1) * TPB, :],
                                 x[b].rearrange("(t p) c -> p t c", p=P)).then_inc(x_in[b], 16)
                sp.dma_start(wgr[:], wg.rearrange("(k p) e -> p k e", p=P)).then_inc(wg_in, 16)
                for e in range(NE):
                    sp.dma_start(w1l[:, e * KC:(e + 1) * KC, :].bitcast(F32), w1[e].rearrange("(k p) f -> p k f", p=P)).then_inc(w_in, 16)
                    sp.dma_start(w2l[:, e * 2:(e + 1) * 2, :].bitcast(F32), w2[e].rearrange("(k p) f -> p k f", p=P)).then_inc(w_in, 16)

            @block.gpsimd
            def _(pool):
                pool.memset(mhalf[:], -0.5)
                pool.memset(bvh[:].bitcast(F32), 0.0).then_inc(cleared, 1)
                pool.memset(bvl[:].bitcast(F32), 0.0).then_inc(cleared, 1)
                pool.wait_ge(cleared, 2)
                pool.memset(bvh[0:KV, :, D0:VW].bitcast(F32), 1.0).then_inc(cleared, 1)
                pool.memset(bvh[KV:P, :, VW + D0:2 * VW].bitcast(F32), 1.0).then_inc(cleared, 1)
                pool.wait_ge(cleared, 4)
                for g in range(KC):
                    pool.wait_ge(kv_lo, g + 1)
                    pool.wait_ge(cst_in, 16)
                    pool.tensor_tensor(bkl[:, :, g, :].rearrange("p b (h k) -> p b h k", k=KV),
                                       kl[:, g, :].rearrange("p (b o k) -> p b o k", o=1, k=KV).broadcast_to([P, B, 8, KV]),
                                       c("mask").rearrange("p (o h q) -> p o h q", o=1, q=1).broadcast_to([P, B, 8, KV]),
                                       ALU.mult).then_inc(block_done, 1)
                pool.wait_ge(lnve, 1)
                pool.tensor_tensor(rstd[:], ve[:], mhalf[:].broadcast_to([P, TILES]), ALU.pow).then_inc(lnrs, 1)

            @block.scalar
            def _(act):
                for raw, hi, _, loaded in weights[:2]:
                    act.wait_ge(loaded, 16)
                    act.copy(hi[:], raw[:]).then_inc(his, 1)
                act.wait_ge(cst_in, 16)
                act.activation(gates[:, 0:2], c("gx"), ACT.Tanh).then_inc(gate_done, 1)
                act.activation(gates[:, 2:4], c("gf"), ACT.Tanh).then_inc(gate_done, 1)
                for raw, hi, _, loaded in weights[2:]:
                    act.wait_ge(loaded, 1 if loaded is wo_scaled else 16)
                    act.copy(hi[:], raw[:]).then_inc(his, 1)
                for g in range(KC):
                    act.wait_ge(k_full, g + 1)
                    act.copy(kh[:, g, :].bitcast(F32R), kf[:, g, :]).then_inc(kv_hi, 1)
                act.wait_ge(cleared, 4)
                for h in range(2):
                    act.wait_ge(v_full, 2)
                    act.copy(bvh[h * KV:(h + 1) * KV, :, h * VW:h * VW + D0],
                             vf[h * KV:(h + 1) * KV].rearrange("p b (j h d) -> p (b j) h d", h=2, d=D0)[:, :, h, :]).then_inc(kv_hi, 1)
                act.wait_ge(wg_in, 16)
                act.copy(wghl[:, :, 0:NE], wgr[:]).then_inc(wg_hi, 1)

            @block.vector
            def _(dve):
                for n, (raw, hi, lo, _) in enumerate(weights):
                    if raw is wos:
                        dve.wait_ge(wo_in, 16)
                        dve.wait_ge(gate_done, 2)
                        dve.tensor_scalar(wos[:], wor[:], gates[:, 0:1], None, ALU.mult).then_inc(wo_scaled, 1)
                        dve.tensor_scalar(bos[:], c("bo"), gates[:, 0:1], None, ALU.mult)
                        dve.wait_ge(wo_scaled, 1)
                    dve.wait_ge(his, n + 1)
                    dve.tensor_tensor(lo[:], raw[:], hi[:].bitcast(F32), ALU.subtract).then_inc(los, 1)
                    if raw is ctr:
                        dve.wait_ge(los, 1)
                        for src, dst in ((cth, dch), (ctl, dcl)):
                            for h in range(2):
                                dve.tensor_copy(dst[:, :, :, h, :].rearrange("p k b n -> p k b n"),
                                                src[:].rearrange("p k (b n) -> p k b n", b=B)).then_inc(los, 1)
                for g in range(KC):
                    dve.wait_ge(k_ready, g + 1)
                    dve.wait_ge(cst_in, 16)
                    dve.tensor_scalar(kf[:, g, :], psk[:, g, 0:B * KV], c("bk")[:, g:g + 1], D0 ** -0.5,
                                      ALU.add, ALU.mult).then_inc(k_full, 1)
                for v2 in range(2):
                    dve.wait_ge(v_ready, v2 + 1)
                    dve.tensor_tensor(vf[:, 2 * v2:2 * v2 + 2, :], psv[:, v2, :].rearrange("p (b c) -> p b c", b=2),
                                      c("bv").rearrange("p (o c) -> p o c", o=1).broadcast_to([P, 2, C]), ALU.add).then_inc(v_full, 1)
                for g in range(KC):
                    dve.wait_ge(kv_hi, g + 1)
                    dve.tensor_tensor(kl[:, g, :], kf[:, g, :], kh[:, g, :], ALU.subtract).then_inc(kv_lo, 1)
                    dve.tensor_tensor(bkh[:, :, g, :].rearrange("p b (h k) -> p b h k", k=KV),
                                      kh[:, g, :].rearrange("p (b o k) -> p b o k", o=1, k=KV).broadcast_to([P, B, 8, KV]),
                                      c("mask").rearrange("p (o h q) -> p o h q", o=1, q=1).broadcast_to([P, B, 8, KV]),
                                      ALU.mult).then_inc(block_done, 1)
                dve.wait_ge(cleared, 4)
                for h in range(2):
                    dve.wait_ge(kv_hi, KC + h + 1)
                    rs = slice(h * KV, (h + 1) * KV)
                    dve.tensor_tensor(bvl[rs, :, h * VW:h * VW + D0],
                                      vf[rs].rearrange("p b (j h d) -> p (b j) h d", h=2, d=D0)[:, :, h, :],
                                      bvh[rs, :, h * VW:h * VW + D0].bitcast(F32), ALU.subtract).then_inc(block_done, 1)
                for t in range(TILES):
                    dve.wait_ge(x_in[t // TPB], 16)
                    dve.bn_stats(st[:, t, :], xres[:, t, :]).then_inc(lnst, 1)
                for t in range(TILES):
                    dve.wait_ge(lnst, t + 1)
                    dve.bn_aggr(mean[:, t, :], st[:, t, :]).then_inc(lnmv, 1)
                dve.wait_ge(lnmv, TILES)
                dve.tensor_scalar(ve[:], mean[:, :, 1], EPS, None, ALU.add).then_inc(lnve, 1)
                dve.wait_ge(wg_hi, 1)
                dve.tensor_tensor(wghl[:, :, NE:2 * NE], wgr[:], wghl[:, :, 0:NE].bitcast(F32), ALU.subtract).then_inc(wg_lo, 1)

            @block.tensor
            def _(pe):
                pe.wait_ge(los, 1 + 4 + 1)
                for g in range(KC):
                    n = 0
                    for k in range(2):
                        m = slice(g * P, (g + 1) * P)
                        for l, r in split3(wkh[:, k, m], wkl[:, k, m], cth[:, k, :], ctl[:, k, :]):
                            mm = nc.tensor.matmul(psk[:, g, 0:B * KV], l, r, start=(n == 0), stop=(n == 2 * PASSES - 1))
                            n += 1
                    mm.then_inc(k_ready, 1)
                pe.wait_ge(los, 1 + 4 + 2)
                for v2 in range(2):
                    for b in (2 * v2, 2 * v2 + 1):
                        n = 0
                        for k in range(2):
                            lh, ll = (t[:, k, b].rearrange("p h n -> p (h n)") for t in (dch, dcl))
                            for l, r in split3(lh, ll, wvh[:, k, :], wvl[:, k, :]):
                                mm = nc.tensor.matmul(psv[:, v2, (b % 2) * C:(b % 2 + 1) * C], l, r,
                                                      start=(n == 0), stop=(n == 2 * PASSES - 1))
                                n += 1
                    mm.then_inc(v_ready, 1)


def attend0(nc, c, xres, xn_dram, mhalf, bkh, bkl, bvh, bvl, wqh, wql, woh, wol, bos, wghl, mean, rstd, lg):
    with ExitStack() as ctx:
        def sbuf(name, shape, dt=F32):
            return ctx.enter_context(nc.sbuf_tensor(f"att0_{name}", shape, dt))

        def sem(name):
            return ctx.enter_context(nc.semaphore(f"att0_{name}"))

        def bank(name, n=1):
            return ctx.enter_context(nc.psum_tensor(f"att0_{name}", [P, n, 512], F32))

        st, mv = sbuf("ln_stats", [P, 2, 6]), sbuf("ln_mean_var", [P, 2, 2])
        ve, rs = sbuf("ln_var_eps", [P, 2]), sbuf("ln_rstd", [P, 2])
        xn = sbuf("xn", [P, 2, 2, C])
        xh, xl = sbuf("xt_hi", [P, 2, 2, C], F32R), sbuf("xt_lo", [P, 2, 2, C], F32R)
        qf = sbuf("q_full", [P, 2, C])
        qh, ql = sbuf("qt_hi", [P, 2, C], F32R), sbuf("qt_lo", [P, 2, C], F32R)
        sc = sbuf("scores", [P, 2, HK])
        mx = sbuf("score_max", [P, 2, H])
        ph, pl = sbuf("pt_hi", [P, 2, HK], F32R), sbuf("pt_lo", [P, 2, HK], F32R)
        rc = sbuf("recip", [P, 2, H])
        on = sbuf("o_norm", [P, 2, C])
        oh, ol = sbuf("ot_hi", [P, 2, C], F32R), sbuf("ot_lo", [P, 2, C], F32R)
        ps_s, ps_p = bank("ps_scores", 2), bank("ps_pt", 2)
        ps_o, ps_x, ps_q, ps_m = bank("ps_pv"), bank("ps_xt"), bank("ps_q"), bank("ps_oy")

        (xt_ready, q_ready, s_ready, pt_ready, pv_ready, ot_ready, y_ready) = (sem(n) for n in (
            "xt_ready", "q_ready", "scores_ready", "pt_ready", "pv_ready", "ot_ready", "y_ready"))
        (xhi, qhi, expd, phi, ohi) = (sem(n) for n in ("xt_hi_done", "q_hi_done", "exp_done", "pt_hi_done", "ot_hi_done"))
        (copied,) = (sem("scores_copied"),)
        (xlo, qsum, clipd, maxd, plo, recd, normd, olo, resd) = (sem(n) for n in (
            "xt_lo_done", "q_biased", "clipped", "max_done", "pt_lo_done", "recip_done", "o_normed", "ot_lo_done", "residual_done"))
        lnve, lndone, lnrs = sem("ln_next_ve"), [sem("ln_out"), sem("ln_next_out")], sem("ln_next_rstd")
        logits, lg_part = sem("logits_ready"), sem("lg_part")
        stored = [sem("xn_next_stored0"), sem("xn_next_stored1")]
        (cent, qlo, xbias) = (sem(n) for n in ("centred", "q_lo_done", "bias_added"))
        ident = c("ident")
        NEXT = 7

        def halves(u):
            return slice(0 if live(u) else 1, 2 if live(u - NEXT) else 1)

        def transposing(u):
            return live(u) or live(u - NEXT)

        with nc.Block() as block:
            @block.sync
            def _(sp):
                def store(t, p):
                    sp.wait_ge(lndone[1], t + 1)
                    sp.dma_start(xn_dram[ds(t * P, P), :], xn[:, (p + NEXT) % 2, 1, :]).then_inc(stored[p], 16)

                def body(i, par):
                    if live(i - 4):
                        store(i - 4, par % 2)
                staged(sp, body, 4, 6, 12, TILES + 4)
                for p in range(2):
                    sp.wait_ge(stored[p], 16 * TILES // 2)

            @block.tensor
            def _(pe):
                def route_logits(t, p):
                    pe.wait_ge(xlo, t + NEXT + 1)
                    steps = ((xh, 0, 2), (xl, 0, 1), (xl, 1, 1), (xh, 1, 2))
                    for n, (lhs, k, w) in enumerate(steps):
                        mm = nc.tensor.matmul(ps_q[:, 0, ds(t * 2 * NE + C, w * NE)], lhs[:, (p + NEXT) % 2, 1, k * P:(k + 1) * P],
                                              wghl[:, k, 0:w * NE], start=(n == 0), stop=(n == len(steps) - 1))
                    mm.then_inc(logits, 1)

                def scores(t, p):
                    pe.wait_ge(qlo, t + 1)
                    if not isinstance(t, int) or t > 0:
                        pe.wait_ge(copied, t)
                    for g in range(KC):
                        gs = slice(g * P, (g + 1) * P)
                        rh, rl = (w[:, ds(t // TPB, 1), g, :].rearrange("p o n -> p (o n)") for w in (bkh, bkl))
                        for n, (l, r) in enumerate(split3(qh[:, p, gs], ql[:, p, gs], rh, rl)):
                            mm = nc.tensor.matmul(ps_s[:, g, :], l, r, start=(n == 0), stop=(n == PASSES - 1))
                    mm.then_inc(s_ready, 1)

                def transpose_probs(t, p):
                    pe.wait_ge(expd, t + 1)
                    for j in range(PAIRS):
                        mm = nc.tensor.transpose(ps_p[:, j // 4, (j % 4) * P:(j % 4 + 1) * P],
                                                 sc[:, p, j * P:(j + 1) * P], ident)
                        if j % 4 == 3:
                            mm.then_inc(pt_ready, 1)

                def transpose_x(u, p):
                    if live(u):
                        pe.wait_ge(lndone[0], u + 1)
                    if live(u - NEXT):
                        pe.wait_ge(lndone[1], u - NEXT + 1)
                    for h in range(2)[halves(u)]:
                        for k in range(KC):
                            mm = nc.tensor.transpose(ps_x[:, 0, h * C + k * P:h * C + (k + 1) * P], xn[:, p, h, k * P:(k + 1) * P], ident)
                    mm.then_inc(xt_ready, 1)

                def transpose_o(t, p):
                    pe.wait_ge(normd, t + 1)
                    if not isinstance(t, int) or t > 0:
                        pe.wait_ge(resd, t)
                    for k in range(KC):
                        mm = nc.tensor.transpose(ps_m[:, 0, k * P:(k + 1) * P], on[:, p, k * P:(k + 1) * P], ident)
                    mm.then_inc(ot_ready, 1)

                def weighted_values(t, p):
                    pe.wait_ge(plo, 2 * t + 2)
                    for j in range(PAIRS):
                        js = slice(j * P, (j + 1) * P)
                        rh, rl = (w[:, ds(t // TPB * PAIRS + j, 1), :].rearrange("p o n -> p (o n)") for w in (bvh, bvl))
                        for n, (l, r) in enumerate(split3(ph[:, p, js], pl[:, p, js], rh, rl)):
                            mm = nc.tensor.matmul(ps_o[:, 0, j * 2 * VW:(j + 1) * 2 * VW], l, r,
                                                  start=(n == 0), stop=(n == PASSES - 1))
                    mm.then_inc(pv_ready, 1)

                def queries(t, p):
                    pe.wait_ge(xlo, t + 1)
                    for m in range(KC):
                        ms, n = slice(m * P, (m + 1) * P), 0
                        for k in range(KC):
                            ks = slice(k * P, (k + 1) * P)
                            for l, r in split3(wqh[:, k, ms], wql[:, k, ms], xh[:, p, 0, ks], xl[:, p, 0, ks]):
                                mm = nc.tensor.matmul(ps_q[:, 0, ms], l, r, start=(n == 0), stop=(n == KC * PASSES - 1))
                                n += 1
                    mm.then_inc(q_ready, 1)

                def project(t, p):
                    pe.wait_ge(olo, t + 1)
                    n = 0
                    for k in range(KC):
                        ks = slice(k * P, (k + 1) * P)
                        for l, r in split3(oh[:, p, ks], ol[:, p, ks], woh[:, k, :], wol[:, k, :]):
                            mm = nc.tensor.matmul(ps_m[:, 0, C:2 * C], l, r, start=(n == 0), stop=(n == KC * PASSES - 1))
                            n += 1
                    mm.then_inc(y_ready, 1)

                def body(i, par):
                    for stage, d in ((transpose_probs, -2), (scores, 0), (transpose_x, 2), (transpose_o, -3),
                                     (weighted_values, -2), (route_logits, -5), (queries, 2), (project, -3)):
                        if live(i + d) or stage is transpose_x and transposing(i + d):
                            stage(i + d, (par + d) % 2)
                staged(pe, body, -2, 6, 12, TILES + 5)

            @block.scalar
            def _(act):
                def copy_scores(t, p):
                    act.wait_ge(s_ready, t + 1)
                    if not isinstance(t, int) or t > 1:
                        act.wait_ge(pt_ready, 2 * t - 2)
                    act.copy(sc[:, p, :].rearrange("p (a n) -> p a n", a=2), ps_s[:]).then_inc(copied, 1)

                def x_high(t, p):
                    act.wait_ge(xt_ready, t + 1)
                    hs = halves(t)
                    act.copy(xh[:, p, hs, :], ps_x[:, 0, :].rearrange("p (h c) -> p h c", h=2)[:, hs, :]).then_inc(xhi, 1)

                def probs_high(t, p):
                    for half in range(2):
                        act.wait_ge(pt_ready, 2 * t + half + 1)
                        act.copy(ph[:, p, half * 512:(half + 1) * 512], ps_p[:, half, :]).then_inc(phi, 1)

                def o_high(t, p):
                    act.wait_ge(ot_ready, t + 1)
                    act.copy(oh[:, p, :], ps_m[:, 0, 0:C]).then_inc(ohi, 1)

                def q_high(t, p):
                    act.wait_ge(qsum, t + 1)
                    act.copy(qh[:, p, :], qf[:, p, :]).then_inc(qhi, 1)

                def exponential(t, p):
                    act.wait_ge(cent, t + 1)
                    act.activation(sc[:, p, :], sc[:, p, :], ACT.Exp).then_inc(expd, 1)

                def body(i, par):
                    for stage, d in ((exponential, -1), (probs_high, -2), (copy_scores, 0), (x_high, 2), (o_high, -3),
                                     (q_high, 2)):
                        if live(i + d) or stage is x_high and transposing(i + d):
                            stage(i + d, (par + d) % 2)
                staged(act, body, -2, 6, 12, TILES + 5)

            @block.gpsimd
            def _(pool):
                def rstd_next(t, p):
                    pool.wait_ge(lnve, t + 1)
                    pool.tensor_tensor(rs[:, p:p + 1], ve[:, p:p + 1], mhalf[:], ALU.pow).then_inc(lnrs, 1)

                def centre(t, p):
                    pool.wait_ge(maxd, t + 1)
                    s3 = sc[:, p, :].rearrange("p (h k) -> p h k", k=KV)
                    pool.tensor_tensor(s3, s3, mx[:, p, :].rearrange("p (h o) -> p h o", o=1).broadcast_to([P, H, KV]),
                                       ALU.subtract).then_inc(cent, 1)
                    xt = xres[:, ds(t, 1), :].rearrange("p o c -> p (o c)")
                    pool.tensor_tensor(xt, xt, bos[:], ALU.add).then_inc(xbias, 1)

                def q_low(t, p):
                    pool.wait_ge(qhi, t + 1)
                    pool.tensor_tensor(ql[:, p, :], qf[:, p, :], qh[:, p, :].bitcast(F32), ALU.subtract).then_inc(qlo, 1)

                def body(i, par):
                    for stage, d in ((centre, 0), (q_low, 2), (rstd_next, -3)):
                        if live(i + d):
                            stage(i + d, (par + d) % 2)
                staged(pool, body, -2, 6, 12, TILES + 3)

            @block.vector
            def _(dve):
                def tile_of(t):
                    return xres[:, ds(t, 1), :].rearrange("p o c -> p (o c)")

                def stats_next(t, p):
                    dve.drain()
                    dve.bn_stats(st[:, p, :], tile_of(t))
                    dve.drain()
                    dve.bn_aggr(mv[:, p, :], st[:, p, :])
                    dve.drain()
                    dve.tensor_scalar(ve[:, p:p + 1], mv[:, p, 1:2], EPS, None, ALU.add).then_inc(lnve, 1)

                def normed(t, p):
                    dve.tensor_scalar(xn[:, p, 0, :], tile_of(t), mean[:, ds(t, 1), 0:1].rearrange("p a b -> p (a b)"),
                                      rstd[:, ds(t, 1)], ALU.subtract, ALU.mult).then_inc(lndone[0], 1)

                def normed_next(t, p):
                    dve.wait_ge(lnrs, t + 1)
                    if not isinstance(t, int) or t > 1:
                        dve.wait_ge(stored[p], (t // 2) * 16)
                    dve.tensor_scalar(xn[:, (p + NEXT) % 2, 1, :], tile_of(t), mv[:, p, 0:1], rs[:, p:p + 1], ALU.subtract, ALU.mult).then_inc(lndone[1], 1)

                def clip_and_max(t, p):
                    dve.wait_ge(copied, t + 1)
                    dve.tensor_scalar(sc[:, p, :], sc[:, p, :], CLAMP, -CLAMP, ALU.min, ALU.max).then_inc(clipd, 1)
                    dve.wait_ge(clipd, t + 1)
                    dve.tensor_reduce(mx[:, p, :], sc[:, p, :].rearrange("p (h k) -> p h k", k=KV), AX.X, ALU.max).then_inc(maxd, 1)

                def probs_low(t, p):
                    for half in range(2):
                        hs = slice(half * 512, (half + 1) * 512)
                        dve.wait_ge(phi, 2 * t + half + 1)
                        dve.tensor_tensor(pl[:, p, hs], ps_p[:, half, :], ph[:, p, hs].bitcast(F32), ALU.subtract).then_inc(plo, 1)

                def x_low(t, p):
                    dve.wait_ge(xhi, t + 1)
                    hs = halves(t)
                    dve.tensor_tensor(xl[:, p, hs, :], ps_x[:, 0, :].rearrange("p (h c) -> p h c", h=2)[:, hs, :],
                                      xh[:, p, hs, :].bitcast(F32), ALU.subtract).then_inc(xlo, 1)

                def o_low(t, p):
                    dve.wait_ge(ohi, t + 1)
                    dve.tensor_tensor(ol[:, p, :], ps_m[:, 0, 0:C], oh[:, p, :].bitcast(F32), ALU.subtract).then_inc(olo, 1)

                def q_bias(t, p):
                    dve.wait_ge(q_ready, t + 1)
                    dve.tensor_tensor(qf[:, p, :].rearrange("p (m n) -> p m n", m=KC), ps_q[:, 0, 0:C].rearrange("p (m n) -> p m n", m=KC),
                                      c("bq").rearrange("p (m o) -> p m o", o=1).broadcast_to([P, KC, P]), ALU.add).then_inc(qsum, 1)

                def normalise_o(t, p):
                    dve.wait_ge(pv_ready, t + 1)
                    o3 = ps_o[:, 0, 0:H * VW].rearrange("p (h v) -> p h v", v=VW)
                    dve.reciprocal(rc[:, p, :], o3[:, :, D0]).then_inc(recd, 1)
                    dve.wait_ge(recd, t + 1)
                    dve.tensor_tensor(on[:, p, :].rearrange("p (h d) -> p h d", d=D0), o3[:, :, 0:D0],
                                      rc[:, p, :].rearrange("p (h o) -> p h o", o=1).broadcast_to([P, H, D0]), ALU.mult).then_inc(normd, 1)

                def residual(t, p):
                    dve.wait_ge(y_ready, t + 1)
                    dve.wait_ge(xbias, t + 1)
                    xt = xres[:, ds(t, 1), :].rearrange("p o c -> p (o c)")
                    dve.tensor_tensor(xt, ps_m[:, 0, C:2 * C], xt, ALU.add).then_inc(resd, 1)

                def body(i, par):
                    for stage, d in ((probs_low, -2), (clip_and_max, 0), (x_low, 2), (o_low, -3), (normed_next, -4),
                                     (q_bias, 2), (normed, 3), (normalise_o, -2), (residual, -3), (stats_next, -3)):
                        if live(i + d) or stage is x_low and transposing(i + d):
                            stage(i + d, (par + d) % 2)
                staged(dve, body, -3, 6, 12, TILES + 5)
                dve.wait_ge(logits, TILES)
                parts = ps_q[:, 0, C:2 * C].rearrange("p (t w e) -> p t w e", w=2, e=NE)
                lg3 = lg[:].rearrange("p (t e) -> p t e", e=NE)
                dve.tensor_tensor(lg3, parts[:, :, 0, :], c("bg").rearrange("p (o e) -> p o e", o=1).broadcast_to([P, TILES, NE]),
                                  ALU.add).then_inc(lg_part, 1)
                dve.wait_ge(lg_part, 1)
                dve.tensor_tensor(lg3, parts[:, :, 1, :], lg3, ALU.add)


def experts(nc, c, w1l, w2l, w_in, lg, xn_dram, ys_dram, gates, slots, wsel):
    with ExitStack() as ctx:
        def sbuf(name, shape, dt=F32):
            return ctx.enter_context(nc.sbuf_tensor(f"ffn0_{name}", shape, dt))

        w1h, w2h = sbuf("w1_hi", [P, NE * KC, 2 * FF], F32R), sbuf("w2_hi", [P, NE * 2, C], F32R)
        eid = sbuf("item_expert", [P, ITEMS], I32)
        token = sbuf("token_of_slot", [P, ITEMS], U32)
        route(nc, c, w1h, w1l, w2h, w2l, w_in, eid, token, lg, gates, slots, wsel)
        run_experts(nc, c, w1h, w1l, w2h, w2l, eid, token, xn_dram, ys_dram)


def route(nc, c, w1h, w1l, w2h, w2l, w_in, eid, token, lg0, gates, slots, wsel):
    with ExitStack() as ctx:
        def sbuf(name, shape, dt=F32):
            return ctx.enter_context(nc.sbuf_tensor(f"route_{name}", shape, dt))

        def sem(name):
            return ctx.enter_context(nc.semaphore(f"route_{name}"))

        TE, NB = TILES * NE, TOPK * TILES
        CHUNK = 8
        lg = [lg0, sbuf("logits1", [P, TE])]
        key = [sbuf(f"key{n}", [P, TE]) for n in range(2)]
        oneh = [sbuf(f"onehot{n}", [P, TE]) for n in range(2)]
        top = [sbuf(f"top{n}", [P, TILES]) for n in range(2)]
        kmax = [sbuf(f"keymax{n}", [P, TILES]) for n in range(2)]
        maskr = sbuf("chosen", [P, TE], F32R)
        trir, onesr = sbuf("tri_r", [P, P], F32R), sbuf("ones_r", [P, P], F32R)
        tot, incl, base, slot, tmp = (sbuf(n, [P, TE]) for n in ("totals_et", "inclusive", "base", "slot", "slot_picked"))
        cnt = sbuf("counts", [P, NE]); cnti = sbuf("counts_int", [P, NE], I32); ntl = sbuf("tiles_of_expert", [P, NE])
        endt, startt = sbuf("end_tile", [P, NE]), sbuf("start_slot", [P, NE])
        ge = sbuf("item_past_end", [P, ITEMS, NE]); eidf = sbuf("item_expert_f", [P, ITEMS])
        d21, ez, zp1, inv = (sbuf(n, [P, TILES]) for n in ("gap", "gap_exp", "denominator", "inverse"))
        slotf = sbuf("slot_f", [P, NB])
        sloti, itemf, placef = sbuf("slot_item_int", [P, NB], I32), sbuf("slot_item", [P, NB]), sbuf("slot_place", [P, NB])
        is_item, tok_item = sbuf("is_item", [P, NB, ITEMS]), sbuf("token_in_item", [P, NB, ITEMS], F32R)
        is_place = sbuf("is_place", [P, NB, P], F32R)
        ps_r = ctx.enter_context(nc.psum_tensor("route_ps_rank", [P, 512], F32))
        ps_c = ctx.enter_context(nc.psum_tensor("route_ps_totals", [P, 512], F32))
        ps_t = ctx.enter_context(nc.psum_tensor("route_ps_token", [P, 512], F32))

        whi, wlo = sem("w_hi_done"), sem("w_lo_done")
        step, gap, gexp, chosen, rank, placed, inverted = (sem(n) for n in (
            "route_step", "gap_ready", "gap_exp_done", "chosen_ready", "rank_ready", "placed", "inverted"))

        def te(a):
            return a.rearrange("p (t e) -> p t e", e=NE)

        def over_e(a):
            return a.rearrange("p (t o) -> p t o", o=1).broadcast_to([P, TILES, NE])

        def over_t(a):
            return a.rearrange("p (o e) -> p o e", o=1).broadcast_to([P, TILES, NE])

        with nc.Block() as block:
            @block.tensor
            def _(pe):
                pe.wait_ge(chosen, 1)
                nc.tensor.matmul(ps_r[:, 0:TE], trir[:], maskr[:], start=True, stop=True)
                nc.tensor.matmul(ps_c[:, 0:TE], onesr[:], maskr[:], start=True, stop=True).then_inc(rank, 1)
                for n in range(NB):
                    if n % CHUNK == 0:
                        pe.wait_ge(placed, n // CHUNK + 1)
                    mm = nc.tensor.matmul(ps_t[:, 0:ITEMS], is_place[:, n, :], tok_item[:, n, :], start=(n == 0), stop=(n == NB - 1))
                mm.then_inc(inverted, 1)

            @block.scalar
            def _(act):
                act.wait_ge(w_in, 32 * NE)
                for e in range(NE):
                    if e == 2:
                        act.wait_ge(gap, 1)
                        act.activation(ez[:], d21[:], ACT.Exp).then_inc(gexp, 1)
                    act.copy(w1h[:, e * KC:(e + 1) * KC, :], w1l[:, e * KC:(e + 1) * KC, :].bitcast(F32)).then_inc(whi, 1)
                    act.copy(w2h[:, e * 2:(e + 1) * 2, :], w2l[:, e * 2:(e + 1) * 2, :].bitcast(F32)).then_inc(whi, 1)

            @block.gpsimd
            def _(pool):
                for e in range(NE):
                    for n, (hi, lo, w) in enumerate(((w1h, w1l, KC), (w2h, w2l, 2))):
                        es = slice(e * w, (e + 1) * w)
                        pool.wait_ge(whi, 2 * e + n + 1)
                        pool.tensor_tensor(lo[:, es, :], lo[:, es, :].bitcast(F32), hi[:, es, :].bitcast(F32), ALU.subtract).then_inc(wlo, 1)

            @block.vector
            def _(dve):
                steps = [0]

                def link(ins):
                    steps[0] += 1
                    ins.then_inc(step, 1)
                    dve.wait_ge(step, steps[0])

                dve.tensor_copy(trir[:], c("tri"))
                dve.tensor_copy(onesr[:], c("ones"))
                for n in range(TOPK):
                    link(dve.tensor_reduce(top[n][:], te(lg[n][:]), AX.X, ALU.max))
                    link(dve.tensor_tensor(te(key[n][:]), te(lg[n][:]), over_e(top[n][:]), ALU.is_equal))
                    link(dve.tensor_tensor(te(key[n][:]), te(key[n][:]), over_t(c("rev")), ALU.mult))
                    link(dve.tensor_reduce(kmax[n][:], te(key[n][:]), AX.X, ALU.max))
                    link(dve.tensor_tensor(te(oneh[n][:]), over_t(c("rev")), over_e(kmax[n][:]), ALU.is_equal))
                    if n == 0:
                        link(dve.scalar_tensor_tensor(out=lg[1][:], in0=oneh[0][:], scalar=-3e38, in1=lg[0][:], op0=ALU.mult, op1=ALU.add))
                dve.tensor_tensor(maskr[:], oneh[0][:], oneh[1][:], ALU.add).then_inc(chosen, 1)
                dve.tensor_tensor(d21[:], top[1][:], top[0][:], ALU.subtract).then_inc(gap, 1)
                dve.wait_ge(rank, 1)
                link(dve.tensor_copy(tot[:].rearrange("p (e t) -> p t e", e=NE), te(ps_c[:, 0:TE])))
                link(dve.tensor_tensor_scan(incl[:], c("scan"), tot[:], 0.0, ALU.mult, ALU.add))
                link(dve.tensor_scalar(cnt[:], incl[:].rearrange("p (e t) -> p e t", e=NE)[:, :, TILES - 1], float(P - 1), None, ALU.add))
                link(dve.tensor_copy(cnti[:], cnt[:]))
                link(dve.tensor_single_scalar(cnti[:], cnti[:], 7, ALU.arith_shift_right))
                link(dve.tensor_copy(ntl[:], cnti[:]))
                link(dve.tensor_tensor_scan(endt[:], c("ones")[:, 0:NE], ntl[:], 0.0, ALU.mult, ALU.add))
                link(dve.tensor_tensor(startt[:], endt[:], ntl[:], ALU.subtract))
                link(dve.tensor_scalar(startt[:], startt[:], float(P), None, ALU.mult))
                link(dve.tensor_tensor(incl[:], incl[:], tot[:], ALU.subtract))
                link(dve.tensor_tensor(te(base[:]), incl[:].rearrange("p (e t) -> p t e", e=NE), over_t(startt[:]), ALU.add))
                link(dve.tensor_tensor(slot[:], ps_r[:, 0:TE], base[:], ALU.add))
                for n in range(TOPK):
                    link(dve.tensor_tensor(tmp[:], slot[:], oneh[n][:], ALU.mult))
                    link(dve.tensor_reduce(slotf[:, n * TILES:(n + 1) * TILES], te(tmp[:]), AX.X, ALU.add))
                dve.tensor_copy(slots[:].rearrange("p k t -> p (k t)"), slotf[:])
                link(dve.tensor_copy(sloti[:], slotf[:]))
                link(dve.tensor_single_scalar(sloti[:], sloti[:], 7, ALU.arith_shift_right))
                link(dve.tensor_copy(itemf[:], sloti[:]))
                link(dve.scalar_tensor_tensor(out=placef[:], in0=itemf[:], scalar=-float(P), in1=slotf[:], op0=ALU.mult, op1=ALU.add))
                link(dve.tensor_tensor(is_item[:], c("item").rearrange("p (o j) -> p o j", o=1).broadcast_to([P, NB, ITEMS]),
                                       itemf[:].rearrange("p (n o) -> p n o", o=1).broadcast_to([P, NB, ITEMS]), ALU.is_equal))
                for k in range(TOPK):
                    ks = slice(k * TILES, (k + 1) * TILES)
                    link(dve.tensor_tensor(tok_item[:, ks, :], is_item[:, ks, :],
                                           c("token").rearrange("p (t o) -> p t o", o=1).broadcast_to([P, TILES, ITEMS]), ALU.mult))
                for n in range(0, NB, CHUNK):
                    dve.tensor_tensor(is_place[:, n:n + CHUNK, :], c("place").rearrange("p (o r) -> p o r", o=1).broadcast_to([P, CHUNK, P]),
                                      placef[:, n:n + CHUNK].rearrange("p (n o) -> p n o", o=1).broadcast_to([P, CHUNK, P]),
                                      ALU.is_equal).then_inc(placed, 1)
                link(dve.tensor_tensor(ge[:], c("item").rearrange("p (j o) -> p j o", o=1).broadcast_to([P, ITEMS, NE]),
                                       endt[:].rearrange("p (o e) -> p o e", o=1).broadcast_to([P, ITEMS, NE]), ALU.is_ge))
                link(dve.tensor_reduce(eidf[:], ge[:], AX.X, ALU.add))
                link(dve.tensor_scalar(eidf[:], eidf[:], float(NE - 1), None, ALU.min))
                dve.tensor_copy(eid[:], eidf[:])
                dve.wait_ge(inverted, 1)
                dve.tensor_copy(token[:], ps_t[:, 0:ITEMS])
                dve.wait_ge(gexp, 1)
                link(dve.tensor_scalar(zp1[:], ez[:], 1.0, None, ALU.add))
                link(dve.reciprocal(inv[:], zp1[:]))
                link(dve.tensor_scalar(wsel[:, 0, :], inv[:], gates[:, 2:3], None, ALU.mult))
                dve.tensor_tensor(wsel[:, 1, :], wsel[:, 0, :], ez[:], ALU.mult)


def run_experts(nc, c, w1h, w1l, w2h, w2l, eid, token, xn_dram, ys_dram):
    with ExitStack() as ctx:
        def sbuf(name, shape, dt=F32):
            return ctx.enter_context(nc.sbuf_tensor(f"moe_{name}", shape, dt))

        def sem(name):
            return ctx.enter_context(nc.semaphore(f"moe_{name}"))

        xg = sbuf("gathered_tile", [P, 2, C])
        xh, xl = sbuf("xt_hi", [P, 2, C], F32R), sbuf("xt_lo", [P, 2, C], F32R)
        sg, act_a = sbuf("silu_gate", [P, 2, FF]), sbuf("hidden", [P, 2, FF])
        ah, al = sbuf("at_hi", [P, 2, FF], F32R), sbuf("at_lo", [P, 2, FF], F32R)
        yo = sbuf("expert_tile", [P, 2, C])
        ps_x = ctx.enter_context(nc.psum_tensor("moe_ps_xt", [P, 2, 512], F32))
        ps_h = ctx.enter_context(nc.psum_tensor("moe_ps_h", [P, 2, 512], F32))
        ps_a = ctx.enter_context(nc.psum_tensor("moe_ps_at", [P, 2, 512], F32))
        ps_y = ctx.enter_context(nc.psum_tensor("moe_ps_y", [P, 2, 512], F32))
        x_in = [sem("x_in0"), sem("x_in1")]
        y_out = [sem("y_out0"), sem("y_out1")]
        (xt_ready, xhi, xlo, h_ready, silud, hidden, at_ready, ahi, alo, y_ready, y_copied) = (sem(n) for n in (
            "xt_ready", "xt_hi_done", "xt_lo_done", "h_ready", "silu_done", "hidden_done", "at_ready", "at_hi_done",
            "at_lo_done", "y_ready", "y_copied"))

        def exists(j):
            return not isinstance(j, int) or 0 <= j < ITEMS

        def later(j, n=0):
            return not isinstance(j, int) or j > n

        def turns(eng, stages, first, last):
            def body(i, par):
                for stage, d in stages:
                    if exists(i + d):
                        stage(i + d, (par + d) % 2)
            staged(eng, body, first, 6, ITEMS - 4, last)

        with nc.Block() as block:
            @block.sync
            def _(sp):
                def store(j, p):
                    sp.wait_ge(y_copied, j + 1)
                    sp.dma_start(ys_dram[ds(j * P, P), :], yo[:, p, :]).then_inc(y_out[p], 16)
                turns(sp, ((store, -1),), 0, ITEMS + 1)
                for p in range(2):
                    sp.wait_ge(y_out[p], 16 * ITEMS // 2)

            @block.gpsimd
            def _(pool):
                for j in range(ITEMS):
                    if j >= 2:
                        pool.wait_ge(xt_ready, j - 1)
                    pool.indirect_dma_start(xg[:, j % 2, :], None, xn_dram,
                                            bass.IndirectOffsetOnAxis(ap=token[:, j:j + 1], axis=0)).then_inc(x_in[j % 2], 16)

            @block.tensor
            def _(pe):
                expert_down = [pe.alloc_register(f"expert_down{q}") for q in range(2)]
                expert = [pe.alloc_register(f"expert{q}") for q in range(2)]

                def transpose_x(j, p):
                    pe.wait_ge(x_in[p], (j // 2 + 1) * 16)
                    for k in range(KC):
                        mm = nc.tensor.transpose(ps_x[:, p, k * P:(k + 1) * P], xg[:, p, k * P:(k + 1) * P], c("ident"))
                    mm.then_inc(xt_ready, 1)

                def load_expert(j, p):
                    if later(j, 1):
                        pe.reg_load(expert[p], eid[0:1, ds(j, 1)])

                def gate_up(j, p):
                    e, n = pe.snap(expert[p], min_val=0, max_val=NE - 1), 0
                    pe.reg_mov(expert_down[p], expert[p])
                    pe.wait_ge(xlo, j + 1)
                    for k in range(KC):
                        rh, rl = (w[:, ds(e * KC + k, 1), :].rearrange("p o f -> p (o f)") for w in (w1h, w1l))
                        for l, r in split3(xh[:, p, k * P:(k + 1) * P], xl[:, p, k * P:(k + 1) * P], rh, rl):
                            mm = nc.tensor.matmul(ps_h[:, p, :], l, r, start=(n == 0), stop=(n == KC * PASSES - 1))
                            n += 1
                    mm.then_inc(h_ready, 1)

                def transpose_a(j, p):
                    pe.wait_ge(hidden, j + 1)
                    for k in range(2):
                        mm = nc.tensor.transpose(ps_a[:, p, k * P:(k + 1) * P], act_a[:, p, k * P:(k + 1) * P], c("ident"))
                    mm.then_inc(at_ready, 1)

                def down(j, p):
                    e, n = pe.snap(expert_down[p], min_val=0, max_val=NE - 1), 0
                    pe.wait_ge(alo, j + 1)
                    if later(j, 1):
                        pe.wait_ge(y_copied, j - 1)
                    for k in range(2):
                        rh, rl = (w[:, ds(e * 2 + k, 1), :].rearrange("p o f -> p (o f)") for w in (w2h, w2l))
                        for l, r in split3(ah[:, p, k * P:(k + 1) * P], al[:, p, k * P:(k + 1) * P], rh, rl):
                            mm = nc.tensor.matmul(ps_y[:, p, 0:C], l, r, start=(n == 0), stop=(n == 2 * PASSES - 1))
                            n += 1
                    mm.then_inc(y_ready, 1)
                for j in range(2):
                    pe.reg_load(expert[j], eid[0:1, j:j + 1])
                turns(pe, ((transpose_a, -1), (gate_up, 0), (load_expert, 1), (transpose_x, 2), (down, -1)), -2, ITEMS + 1)

            @block.scalar
            def _(act):
                def x_high(j, p):
                    act.wait_ge(xt_ready, j + 1)
                    act.copy(xh[:, p, :], ps_x[:, p, 0:C]).then_inc(xhi, 1)

                def a_high(j, p):
                    act.wait_ge(at_ready, j + 1)
                    act.copy(ah[:, p, :], ps_a[:, p, 0:FF]).then_inc(ahi, 1)

                def silu(j, p):
                    act.wait_ge(h_ready, j + 1)
                    act.activation(sg[:, p, :], ps_h[:, p, 0:FF], ACT.Silu).then_inc(silud, 1)

                def y_copy(j, p):
                    act.wait_ge(y_ready, j + 1)
                    if later(j, 1):
                        act.wait_ge(y_out[p], (j // 2) * 16)
                    act.copy(yo[:, p, :], ps_y[:, p, 0:C]).then_inc(y_copied, 1)
                turns(act, ((a_high, -1), (silu, 0), (x_high, 2), (y_copy, -1)), -2, ITEMS + 1)

            @block.vector
            def _(dve):
                def x_low(j, p):
                    dve.wait_ge(xhi, j + 1)
                    dve.tensor_tensor(xl[:, p, :], ps_x[:, p, 0:C], xh[:, p, :].bitcast(F32), ALU.subtract).then_inc(xlo, 1)

                def a_low(j, p):
                    dve.wait_ge(ahi, j + 1)
                    dve.tensor_tensor(al[:, p, :], ps_a[:, p, 0:FF], ah[:, p, :].bitcast(F32), ALU.subtract).then_inc(alo, 1)

                def times_up(j, p):
                    dve.wait_ge(silud, j + 1)
                    dve.tensor_tensor(act_a[:, p, :], ps_h[:, p, FF:2 * FF], sg[:, p, :], ALU.mult).then_inc(hidden, 1)
                turns(dve, ((a_low, -1), (times_up, 0), (x_low, 2)), -2, ITEMS + 1)


def attention1(nc, c, ctxt, wqt1, wk1, wv1, wo1, ys_dram, xres, gates, mhalf, slots, wsel):
    with ExitStack() as keep:
        def sbuf(name, shape, dt=F32):
            return keep.enter_context(nc.sbuf_tensor(f"a1_{name}", shape, dt))

        ah, al = (sbuf(f"a_{s}", [P, KC, B, HK], F32R) for s in ("hi", "lo"))
        bh, bl = (sbuf(f"b_{s}", [P, B, PAIRS, C], F32R) for s in ("hi", "lo"))
        bos = sbuf("bo_scaled", [P, C])
        prepare1(nc, c, ctxt, wqt1, wk1, wv1, wo1, ys_dram, xres, gates, slots, wsel, ah, al, bh, bl, bos)
        attend1(nc, c, xres, mhalf, ah, al, bh, bl, bos)


def prepare1(nc, c, ctxt, wqt1, wk1, wv1, wo1, ys_dram, xres, gates, slots, wsel, ah, al, bh, bl, bos):
    with ExitStack() as ctx:
        def sbuf(name, shape, dt=F32):
            return ctx.enter_context(nc.sbuf_tensor(f"kv1_{name}", shape, dt))

        def sem(name):
            return ctx.enter_context(nc.semaphore(f"kv1_{name}"))

        DEPTH = 2
        yg = sbuf("gathered", [P, DEPTH, TOPK, C])
        ctr, cth, ctl = sbuf("ctx_raw", [KP, 2, B * KV]), sbuf("ctx_hi", [KP, 2, B * KV], F32R), sbuf("ctx_lo", [KP, 2, B * KV], F32R)
        wk, wv, wq, wo = ([sbuf(f"{n}_raw", [q, 2, 2 * P]), sbuf(f"{n}_hi", [q, 2, 2 * P], F32R), sbuf(f"{n}_lo", [q, 2, 2 * P], F32R)]
                          for n, q in (("wk", KP), ("wv", KP), ("wq", P), ("wo", P)))
        wos = sbuf("wo_gated", [P, 2, C])
        kbh, kbl, vbh, vbl = (sbuf(n, [P, 2, B * P], F32R) for n in ("kblock_hi", "kblock_lo", "vblock_hi", "vblock_lo"))
        ps_kv = ctx.enter_context(nc.psum_tensor("kv1_ps_kv", [P, 2, 512], F32))
        ps_a = ctx.enter_context(nc.psum_tensor("kv1_ps_a", [P, 2, 512], F32))
        ps_b = ctx.enter_context(nc.psum_tensor("kv1_ps_b", [P, 2, 512], F32))
        ctx_in = sem("ctx_in")
        w_in = [sem("w_in0"), sem("w_in1")]
        g_in = [sem(f"gathered{n}") for n in range(DEPTH)]
        (ctxhi, ctxlo, gated, whi, wlo, cleared, kv_ready, kvhi, kvlo, a_ready, ahi, alo, b_ready, bhi, blo, comb) = (sem(n) for n in (
            "ctx_hi_done", "ctx_lo_done", "wo_gated_done", "w_hi_done", "w_lo_done", "cleared", "kv_ready", "kv_hi_done",
            "kv_lo_done", "a_ready", "a_hi_done", "a_lo_done", "b_ready", "b_hi_done", "b_lo_done", "combined"))

        with nc.Block() as block:
            @block.sync
            def _(sp):
                sp.dma_start(ctr[:], ctxt.rearrange("(k p) n -> p k n", p=KP)).then_inc(ctx_in, 16)
                for j in range(PAIRS):
                    p, cols = j % 2, slice(j * P, (j + 1) * P)
                    if j >= 2:
                        sp.wait_ge(wlo, 4 * (j - 1))
                    sp.dma_start(wk[0][:, p, :].rearrange("p (k n) -> p k n", k=2),
                                 wk1[:, cols].rearrange("(k p) n -> p k n", p=KP)).then_inc(w_in[p], 16)
                    sp.dma_start(wv[0][:, p, :].rearrange("p (k n) -> p k n", k=2),
                                 wv1[:, cols].rearrange("(k p) n -> p k n", p=KP)).then_inc(w_in[p], 16)
                    sp.dma_start(wq[0][:, p, :], wqt1[cols, :]).then_inc(w_in[p], 16)
                    sp.dma_start(wo[0][:, p, :], wo1[cols, :]).then_inc(w_in[p], 16)

            @block.gpsimd
            def _(pool):
                for n, t in enumerate((kbh, kbl, vbh, vbl)):
                    pool.memset(t[:].bitcast(F32), 0.0).then_inc(cleared, 1)
                for t in range(TILES):
                    if t >= DEPTH:
                        pool.wait_ge(comb, 2 * (t - DEPTH + 1))
                    for n in range(TOPK):
                        pool.indirect_dma_start(yg[:, t % DEPTH, n, :], None, ys_dram,
                                                bass.IndirectOffsetOnAxis(ap=slots[:, n, t:t + 1], axis=0)).then_inc(g_in[t % DEPTH], 16)

            @block.scalar
            def _(act):
                act.wait_ge(ctx_in, 16)
                act.copy(cth[:], ctr[:]).then_inc(ctxhi, 1)
                act.wait_ge(cleared, 4)

                def weights_high(j):
                    p = j % 2
                    act.wait_ge(w_in[p], 64 * (j // 2 + 1))
                    if j >= 2:
                        act.wait_ge(b_ready, j - 1)
                    for n, w in enumerate((wk, wv, wq)):
                        act.copy(w[1][:, p, :], w[0][:, p, :]).then_inc(whi, 1)
                    act.wait_ge(gated, j + 1)
                    act.copy(wo[1][:, p, :], wos[:, p, :]).then_inc(whi, 1)

                for j in range(PAIRS):
                    p = j % 2
                    if j == 0:
                        weights_high(0)
                    if j + 1 < PAIRS:
                        weights_high(j + 1)
                    for n, (hi, scale) in enumerate(((kbh, D1 ** -0.5), (vbh, 1.0))):
                        act.wait_ge(kv_ready, 2 * j + n + 1)
                        for h in range(2):
                            rows = slice(h * D1, (h + 1) * D1)
                            act.activation(hi[rows, p, :].rearrange("p (b h k) -> p b h k", b=B, h=2)[:, :, h, :],
                                           ps_kv[rows, n, 0:B * KV].rearrange("p (b k) -> p b k", b=B), ACT.Copy,
                                           scale=scale).then_inc(kvhi, 1)
                    for m in range(KC):
                        act.wait_ge(a_ready, 2 * j + m + 1)
                        act.copy(ah[:, m, :, j * P:(j + 1) * P], ps_a[:, m, :].rearrange("p (b n) -> p b n", b=B)).then_inc(ahi, 1)
                    act.wait_ge(b_ready, j + 1)
                    act.copy(bh[:, :, j, :].rearrange("p (a b) c -> p a b c", a=2), ps_b[:].rearrange("p a (b c) -> p a b c", b=2)).then_inc(bhi, 1)

            @block.vector
            def _(dve):
                dve.tensor_scalar(bos[:], c("bout1"), gates[:, 1:2], None, ALU.mult)
                dve.wait_ge(ctxhi, 1)
                dve.tensor_tensor(ctl[:], ctr[:], cth[:].bitcast(F32), ALU.subtract).then_inc(ctxlo, 1)
                dve.wait_ge(cleared, 4)

                def weights_low(j):
                    p = j % 2
                    dve.wait_ge(w_in[p], 64 * (j // 2 + 1))
                    if j >= 2:
                        dve.wait_ge(b_ready, j - 1)
                    dve.tensor_scalar(wos[:, p, :], wo[0][:, p, :], gates[:, 1:2], None, ALU.mult).then_inc(gated, 1)
                    for n, w in enumerate((wk, wv, wq)):
                        dve.wait_ge(whi, 4 * j + n + 1)
                        dve.tensor_tensor(w[2][:, p, :], w[0][:, p, :], w[1][:, p, :].bitcast(F32), ALU.subtract).then_inc(wlo, 1)
                    dve.wait_ge(whi, 4 * j + 4)
                    dve.tensor_tensor(wo[2][:, p, :], wos[:, p, :], wo[1][:, p, :].bitcast(F32), ALU.subtract).then_inc(wlo, 1)

                def combine(t):
                    dve.wait_ge(g_in[t % DEPTH], 16 * TOPK * (t // DEPTH + 1))
                    for n in range(TOPK):
                        if n:
                            dve.wait_ge(comb, 2 * t + 1)
                        dve.scalar_tensor_tensor(out=xres[:, t, :], in0=yg[:, t % DEPTH, n, :], scalar=wsel[:, n, t:t + 1],
                                                 in1=xres[:, t, :], op0=ALU.mult, op1=ALU.add).then_inc(comb, 1)

                for j in range(PAIRS):
                    p = j % 2
                    if j == 0:
                        weights_low(0)
                    if j + 1 < PAIRS:
                        weights_low(j + 1)
                    for n, (hi, lo, scale) in enumerate(((kbh, kbl, D1 ** -0.5), (vbh, vbl, 1.0))):
                        for h in range(2):
                            dve.wait_ge(kvhi, 4 * j + 2 * n + 2)
                            rows = slice(h * D1, (h + 1) * D1)

                            def block_of(a):
                                return a[rows, p, :].rearrange("p (b h k) -> p b h k", b=B, h=2)[:, :, h, :]
                            dve.scalar_tensor_tensor(out=block_of(lo), in0=ps_kv[rows, n, 0:B * KV].rearrange("p (b k) -> p b k", b=B),
                                                     scalar=scale, in1=block_of(hi).bitcast(F32), op0=ALU.mult,
                                                     op1=ALU.subtract).then_inc(kvlo, 1)
                    combine(2 * j)
                    for m in range(KC):
                        dve.wait_ge(ahi, 2 * j + m + 1)
                        dve.tensor_tensor(al[:, m, :, j * P:(j + 1) * P], ps_a[:, m, :].rearrange("p (b n) -> p b n", b=B),
                                          ah[:, m, :, j * P:(j + 1) * P].bitcast(F32), ALU.subtract).then_inc(alo, 1)
                    combine(2 * j + 1)
                    dve.wait_ge(bhi, j + 1)
                    for q in range(2):
                        dve.tensor_tensor(bl[:, 2 * q:2 * q + 2, j, :], ps_b[:, q, :].rearrange("p (b c) -> p b c", b=2),
                                          bh[:, 2 * q:2 * q + 2, j, :].bitcast(F32), ALU.subtract).then_inc(blo, 1)

            @block.tensor
            def _(pe):
                pe.wait_ge(ctxlo, 1)

                def keys_values(j):
                    p = j % 2
                    pe.wait_ge(wlo, 4 * j + 4)
                    if j >= 1:
                        pe.wait_ge(kvlo, 4 * j)
                    for n, w in enumerate((wk, wv)):
                        q = 0
                        for k in range(2):
                            for l, r in split3(w[1][:, p, k * P:(k + 1) * P], w[2][:, p, k * P:(k + 1) * P], cth[:, k, :], ctl[:, k, :]):
                                mm = nc.tensor.matmul(ps_kv[:, n, 0:B * KV], l, r, start=(q == 0), stop=(q == 2 * PASSES - 1))
                                q += 1
                        mm.then_inc(kv_ready, 1)

                keys_values(0)
                for j in range(PAIRS):
                    p = j % 2
                    pe.wait_ge(kvlo, 4 * j + 4)
                    for m in range(KC):
                        if j >= 1:
                            pe.wait_ge(alo, 2 * (j - 1) + m + 1)
                        ms = slice(m * P, (m + 1) * P)
                        for n, (l, r) in enumerate(split3(wq[1][:, p, ms], wq[2][:, p, ms], kbh[:, p, :], kbl[:, p, :])):
                            mm = nc.tensor.matmul(ps_a[:, m, :], l, r, start=(n == 0), stop=(n == PASSES - 1))
                        mm.then_inc(a_ready, 1)
                    if j + 1 < PAIRS:
                        keys_values(j + 1)
                    if j >= 1:
                        pe.wait_ge(blo, 2 * j)
                    for b in range(B):
                        bs = slice(b * P, (b + 1) * P)
                        for n, (l, r) in enumerate(split3(vbh[:, p, bs], vbl[:, p, bs], wo[1][:, p, :], wo[2][:, p, :])):
                            mm = nc.tensor.matmul(ps_b[:, b // 2, (b % 2) * C:(b % 2 + 1) * C], l, r, start=(n == 0), stop=(n == PASSES - 1))
                    mm.then_inc(b_ready, 1)


def attend1(nc, c, xres, mhalf, ah, al, bh, bl, bos):
    with ExitStack() as ctx:
        def sbuf(name, shape, dt=F32):
            return ctx.enter_context(nc.sbuf_tensor(f"att1_{name}", shape, dt))

        def sem(name):
            return ctx.enter_context(nc.semaphore(f"att1_{name}"))

        def bank(name, *n):
            return ctx.enter_context(nc.psum_tensor(f"att1_{name}", [P, *n, 512], F32))

        st, mv = sbuf("ln_stats", [P, 2, 6]), sbuf("ln_mean_var", [P, 2, 2])
        ve, rs = sbuf("ln_var_eps", [P, 2]), sbuf("ln_rstd", [P, 2])
        xn = sbuf("xn", [P, 2, C])
        xh, xl = sbuf("xt_hi", [P, 2, C], F32R), sbuf("xt_lo", [P, 2, C], F32R)
        sc = sbuf("scores", [P, 2, HK])
        mx, sm, rc = (sbuf(n, [P, 2, H]) for n in ("score_max", "exp_sum", "recip"))
        ph, pl = sbuf("pt_hi", [P, HK], F32R), sbuf("pt_lo", [P, HK], F32R)
        ps_s, ps_p = bank("ps_scores", 2, 2), bank("ps_pt", 2)
        ps_x, ps_y = bank("ps_xt", 1), bank("ps_y", 1)
        (xt_ready, s_ready, pt_ready, y_ready, xhi, phi, expd, lnve, lnrs, lndone, xlo, maxd, cent, sumd, recd, plo,
         resd, xbias, normd) = (sem(n) for n in (
             "xt_ready", "scores_ready", "pt_ready", "y_ready", "xt_hi_done", "pt_hi_done", "exp_done", "ln_ve_done", "ln_rstd_done", "ln_done", "xt_lo_done", "max_done", "centred", "sum_done", "recip_done",
             "pt_lo_done", "residual_done", "bias_added", "probs_normed"))

        def wide(a):
            return a.rearrange("p (h o) -> p h o", o=1).broadcast_to([P, H, KV])

        def heads(a):
            return a.rearrange("p (h k) -> p h k", k=KV)

        def turns(eng, stages, first, last):
            def body(i, par):
                for stage, d in stages:
                    if live(i + d):
                        stage(i + d, (par + d) % 2)
            staged(eng, body, first, 6, 12, last)

        with nc.Block() as block:
            @block.tensor
            def _(pe):
                def transpose_probs(t, p):
                    pe.wait_ge(normd, t + 1)
                    for j in range(PAIRS):
                        mm = nc.tensor.transpose(ps_p[:, j // 4, (j % 4) * P:(j % 4 + 1) * P], sc[:, p, j * P:(j + 1) * P], c("ident"))
                        if j % 4 == 3:
                            mm.then_inc(pt_ready, 1)

                def scores(t, p):
                    pe.wait_ge(xlo, t + 1)
                    if not isinstance(t, int) or t > 1:
                        pe.wait_ge(cent, t - 1)
                    for half in range(2):
                        n = 0
                        for k in range(KC):
                            rh, rl = (w[:, k, ds(t // TPB, 1), half * 512:(half + 1) * 512].rearrange("p o n -> p (o n)") for w in (ah, al))
                            for l, r in split3(xh[:, p, k * P:(k + 1) * P], xl[:, p, k * P:(k + 1) * P], rh, rl):
                                mm = nc.tensor.matmul(ps_s[:, p, half, :], l, r, start=(n == 0), stop=(n == KC * PASSES - 1))
                                n += 1
                    mm.then_inc(s_ready, 1)

                def transpose_x(t, p):
                    pe.wait_ge(lndone, t + 1)
                    for k in range(KC):
                        mm = nc.tensor.transpose(ps_x[:, 0, k * P:(k + 1) * P], xn[:, p, k * P:(k + 1) * P], c("ident"))
                    mm.then_inc(xt_ready, 1)

                def outputs(t, p):
                    pe.wait_ge(plo, 2 * t + 2)
                    if not isinstance(t, int) or t > 0:
                        pe.wait_ge(resd, t)
                    n = 0
                    for j in range(PAIRS):
                        rh, rl = (w[:, ds(t // TPB, 1), j, :].rearrange("p o n -> p (o n)") for w in (bh, bl))
                        for l, r in split3(ph[:, j * P:(j + 1) * P], pl[:, j * P:(j + 1) * P], rh, rl):
                            mm = nc.tensor.matmul(ps_y[:, 0, 0:C], l, r, start=(n == 0), stop=(n == PAIRS * PASSES - 1))
                            n += 1
                    mm.then_inc(y_ready, 1)
                turns(pe, ((transpose_probs, -2), (scores, 0), (outputs, -2), (transpose_x, 1)), -1, TILES + 2)

            @block.scalar
            def _(act):
                def exponential(t, p):
                    act.wait_ge(cent, t + 1)
                    act.activation(sc[:, p, :], sc[:, p, :], ACT.Exp).then_inc(expd, 1)

                def probs_high(t, p):
                    for half in range(2):
                        act.wait_ge(pt_ready, 2 * t + half + 1)
                        if half == 0 and (not isinstance(t, int) or t > 0):
                            act.wait_ge(y_ready, t)
                        act.copy(ph[:, half * 512:(half + 1) * 512], ps_p[:, half, :]).then_inc(phi, 1)

                def x_high(t, p):
                    act.wait_ge(xt_ready, t + 1)
                    act.copy(xh[:, p, :], ps_x[:, 0, 0:C]).then_inc(xhi, 1)
                turns(act, ((exponential, -1), (probs_high, -2), (x_high, 1)), -1, TILES + 2)

            @block.gpsimd
            def _(pool):
                def rstd(t, p):
                    pool.wait_ge(lnve, t + 1)
                    pool.tensor_tensor(rs[:, p:p + 1], ve[:, p:p + 1], mhalf[:], ALU.pow).then_inc(lnrs, 1)

                def normalise(t, p):
                    pool.wait_ge(recd, t + 1)
                    pool.tensor_tensor(heads(sc[:, p, :]), heads(sc[:, p, :]), wide(rc[:, p, :]), ALU.mult).then_inc(normd, 1)

                def bias(t, p):
                    pool.wait_ge(s_ready, t + 1)
                    pool.wait_ge(lnrs, 1)
                    xt = xres[:, ds(t, 1), :].rearrange("p o c -> p (o c)")
                    pool.tensor_tensor(xt, xt, bos[:], ALU.add).then_inc(xbias, 1)
                turns(pool, ((normalise, -1), (rstd, 2), (bias, 0)), -2, TILES + 1)

            @block.vector
            def _(dve):
                def tile_of(t):
                    return xres[:, ds(t, 1), :].rearrange("p o c -> p (o c)")

                def stats(t, p):
                    dve.bn_stats(st[:, p, :], tile_of(t))
                    dve.drain()
                    dve.bn_aggr(mv[:, p, :], st[:, p, :])
                    dve.drain()
                    dve.tensor_scalar(ve[:, p:p + 1], mv[:, p, 1:2], EPS, None, ALU.add).then_inc(lnve, 1)

                def layer_norm(t, p):
                    dve.wait_ge(lnrs, t + 1)
                    dve.tensor_scalar(xn[:, p, :], tile_of(t), mv[:, p, 0:1], rs[:, p:p + 1], ALU.subtract, ALU.mult).then_inc(lndone, 1)

                def x_low(t, p):
                    dve.wait_ge(xhi, t + 1)
                    dve.tensor_tensor(xl[:, p, :], ps_x[:, 0, 0:C], xh[:, p, :].bitcast(F32), ALU.subtract).then_inc(xlo, 1)

                def sums(t, p):
                    dve.wait_ge(expd, t + 1)
                    dve.tensor_reduce(sm[:, p, :], heads(sc[:, p, :]), AX.X, ALU.add).then_inc(sumd, 1)
                    dve.wait_ge(sumd, t + 1)
                    dve.reciprocal(rc[:, p, :], sm[:, p, :]).then_inc(recd, 1)

                def probs_low(t, p):
                    for half in range(2):
                        hs = slice(half * 512, (half + 1) * 512)
                        dve.wait_ge(phi, 2 * t + half + 1)
                        dve.tensor_tensor(pl[:, hs], ps_p[:, half, :], ph[:, hs].bitcast(F32), ALU.subtract).then_inc(plo, 1)

                def centre(t, p):
                    dve.wait_ge(s_ready, t + 1)
                    s3 = ps_s[:, p].rearrange("p a (h k) -> p (a h) k", k=KV)
                    dve.tensor_reduce(mx[:, p, :], s3, AX.X, ALU.max).then_inc(maxd, 1)
                    dve.wait_ge(maxd, t + 1)
                    dve.tensor_tensor(heads(sc[:, p, :]), s3, wide(mx[:, p, :]), ALU.subtract).then_inc(cent, 1)

                def residual(t, p):
                    dve.wait_ge(y_ready, t + 1)
                    dve.wait_ge(xbias, t + 1)
                    dve.tensor_tensor(tile_of(t), ps_y[:, 0, 0:C], tile_of(t), ALU.add).then_inc(resd, 1)
                turns(dve, ((sums, -1), (probs_low, -2), (stats, 2), (centre, 0), (residual, -2), (layer_norm, 2), (x_low, 1)), -2, TILES + 2)


def mlp1(nc, c, fwin, fwout, xres, gates, mhalf, out):
    with ExitStack() as ctx:
        def sbuf(name, shape, dt=F32):
            return ctx.enter_context(nc.sbuf_tensor(f"mlp_{name}", shape, dt))

        def sem(name):
            return ctx.enter_context(nc.semaphore(f"mlp_{name}"))

        UN = INNER // 2
        st, mv = sbuf("ln_stats", [P, TILES, 6]), sbuf("ln_mean_var", [P, TILES, 2])
        ve, rs = sbuf("ln_var_eps", [P, TILES]), sbuf("ln_rstd", [P, TILES])
        xn = sbuf("xn", [P, 2, TPB, C])
        xh, xl = sbuf("xt_hi", [P, 2, KC, S], F32R), sbuf("xt_lo", [P, 2, KC, S], F32R)
        wi, wo = ([sbuf(f"{n}_raw", [P, KC, w]), sbuf(f"{n}_hi", [P, KC, w], F32R), sbuf(f"{n}_lo", [P, KC, w], F32R)]
                  for n, w in (("win", P), ("wout", P)))
        wos, bos, ub, t1 = sbuf("wout_gated", [P, KC, P]), sbuf("bout_gated", [P, C]), sbuf("unit_bias", [P, UN]), sbuf("w1_bin", [P, UN])
        hb = sbuf("units", [P, 2, UN, S])
        g = sbuf("g", [P, 2, S])
        gh, gl = sbuf("g_hi", [P, 2, S], F32R), sbuf("g_lo", [P, 2, S], F32R)
        ps_x = ctx.enter_context(nc.psum_tensor("mlp_ps_xt", [P, KC, 512], F32))
        ps_s = ctx.enter_context(nc.psum_tensor("mlp_ps_s", [P, 2, 512], F32))
        ps_y = ctx.enter_context(nc.psum_tensor("mlp_ps_y", [P, 2, 512], F32))
        w_in, gated, whi, wlo, ubias = sem("w_in"), sem("wout_gated_done"), sem("w_hi_done"), sem("w_lo_done"), sem("unit_bias_done")
        (lnst, lnmv, lnve, lnrs, lndone, xt_ready, xhi, xlo, s_ready, relud, acc, ghi, glo, y_ready, resd, xbias, stored) = (sem(n) for n in (
            "ln_stats_done", "ln_mv_done", "ln_ve_done", "ln_rstd_done", "ln_done", "xt_ready", "xt_hi_done", "xt_lo_done",
            "s_ready", "relu_done", "accumulated", "g_hi_done", "g_lo_done", "y_ready", "residual_done", "bias_added", "stored"))

        with nc.Block() as block:
            @block.sync
            def _(sp):
                sp.dma_start(wi[0][:], fwin.rearrange("(k p) n -> p k n", p=P)).then_inc(w_in, 16)
                sp.dma_start(wo[0][:], fwout.rearrange("p (k n) -> p k n", k=KC)).then_inc(w_in, 16)
                for b in range(B):
                    sp.wait_ge(resd, 2 * (b + 1))
                    sp.dma_start(out[b].rearrange("(t p) c -> p t c", p=P), xres[:, b * TPB:(b + 1) * TPB, :]).then_inc(stored, 16)
                sp.wait_ge(stored, 16 * B)

            @block.gpsimd
            def _(pool):
                pool.wait_ge(gated, 3)
                for b in range(B):
                    bt = slice(b * TPB, (b + 1) * TPB)
                    pool.wait_ge(lnve, b + 1)
                    pool.tensor_tensor(rs[:, bt], ve[:, bt], mhalf[:].broadcast_to([P, TPB]), ALU.pow).then_inc(lnrs, 1)
                    pool.wait_ge(lndone, TPB * (b + 1))
                    pool.tensor_tensor(xres[:, bt, :], xres[:, bt, :], bos[:].rearrange("p (o c) -> p o c", o=1).broadcast_to([P, TPB, C]),
                                       ALU.add).then_inc(xbias, 1)

            @block.scalar
            def _(act):
                act.wait_ge(w_in, 32)
                act.copy(wi[1][:], wi[0][:]).then_inc(whi, 1)
                act.wait_ge(gated, 3)
                act.copy(wo[1][:], wos[:]).then_inc(whi, 1)

                def x_high(b):
                    act.wait_ge(xt_ready, b + 1)
                    if b >= 2:
                        act.wait_ge(s_ready, b - 1)
                    act.copy(xh[:, b % 2], ps_x[:]).then_inc(xhi, 1)

                def g_high(b):
                    act.wait_ge(acc, UN * (b + 1))
                    act.copy(gh[:, b % 2, :], g[:, b % 2, :]).then_inc(ghi, 1)
                x_high(0)
                act.wait_ge(ubias, 2)
                for b in range(B):
                    if b + 1 < B:
                        x_high(b + 1)
                    if b >= 1:
                        g_high(b - 1)
                    act.wait_ge(s_ready, b + 1)
                    if b >= 2:
                        act.wait_ge(acc, UN * (b - 1))
                    for u in range(UN):
                        act.activation(hb[:, b % 2, u, :], ps_s[:, b % 2, :], ACT.Relu, bias=ub[:, u:u + 1],
                                       scale=c("fw1")[:, u:u + 1]).then_inc(relud, 1)
                g_high(B - 1)

            @block.vector
            def _(dve):
                dve.tensor_scalar(bos[:], c("fbout"), gates[:, 3:4], None, ALU.mult).then_inc(gated, 1)
                dve.tensor_scalar(t1[:], c("fw1"), c("fbin"), None, ALU.mult).then_inc(ubias, 1)
                dve.wait_ge(ubias, 1)
                dve.tensor_tensor(ub[:], t1[:], c("fb1"), ALU.add).then_inc(ubias, 1)
                dve.wait_ge(w_in, 32)
                dve.tensor_scalar(wos[:], wo[0][:], gates[:, 3:4], None, ALU.mult).then_inc(gated, 2)
                dve.wait_ge(whi, 1)
                dve.tensor_tensor(wi[2][:], wi[0][:], wi[1][:].bitcast(F32), ALU.subtract).then_inc(wlo, 1)
                dve.wait_ge(whi, 2)
                dve.tensor_tensor(wo[2][:], wos[:], wo[1][:].bitcast(F32), ALU.subtract).then_inc(wlo, 1)

                def stats(b):
                    for t in range(b * TPB, (b + 1) * TPB):
                        dve.bn_stats(st[:, t, :], xres[:, t, :]).then_inc(lnst, 1)
                    for t in range(b * TPB, (b + 1) * TPB):
                        dve.wait_ge(lnst, t + 1)
                        dve.bn_aggr(mv[:, t, :], st[:, t, :]).then_inc(lnmv, 1)
                    bt = slice(b * TPB, (b + 1) * TPB)
                    dve.wait_ge(lnmv, TPB * (b + 1))
                    dve.tensor_scalar(ve[:, bt], mv[:, bt, 1], EPS, None, ALU.add).then_inc(lnve, 1)

                def layer_norm(b):
                    dve.wait_ge(lnrs, b + 1)
                    if b >= 2:
                        dve.wait_ge(xt_ready, b - 1)
                    for u in range(TPB):
                        t = b * TPB + u
                        dve.tensor_scalar(xn[:, b % 2, u, :], xres[:, t, :], mv[:, t, 0:1], rs[:, t:t + 1], ALU.subtract, ALU.mult).then_inc(lndone, 1)

                def x_low(b):
                    dve.wait_ge(xhi, b + 1)
                    if b >= 2:
                        dve.wait_ge(s_ready, b - 1)
                    dve.tensor_tensor(xl[:, b % 2], ps_x[:], xh[:, b % 2].bitcast(F32), ALU.subtract).then_inc(xlo, 1)

                def accumulate(b):
                    p = b % 2
                    for u in range(UN):
                        dve.wait_ge(relud, b * UN + u + 1)
                        if u == 0:
                            if b >= 2:
                                dve.wait_ge(glo, b - 1)
                            dve.tensor_scalar(g[:, p, :], hb[:, p, 0, :], c("fw2")[:, 0:1], c("fb2"), ALU.mult, ALU.add).then_inc(acc, 1)
                        else:
                            dve.wait_ge(acc, b * UN + u)
                            dve.scalar_tensor_tensor(out=g[:, p, :], in0=hb[:, p, u, :], scalar=c("fw2")[:, u:u + 1], in1=g[:, p, :],
                                                     op0=ALU.mult, op1=ALU.add).then_inc(acc, 1)

                def g_low(b):
                    dve.wait_ge(ghi, b + 1)
                    dve.tensor_tensor(gl[:, b % 2, :], g[:, b % 2, :], gh[:, b % 2, :].bitcast(F32), ALU.subtract).then_inc(glo, 1)

                def residual(b):
                    dve.wait_ge(xbias, b + 1)
                    for q in range(2):
                        dve.wait_ge(y_ready, 2 * b + q + 1)
                        xt = xres[:, b * TPB + 2 * q:b * TPB + 2 * q + 2, :]
                        dve.tensor_tensor(xt, ps_y[:, q, :].rearrange("p (t c) -> p t c", t=2), xt, ALU.add).then_inc(resd, 1)

                stats(0)
                stats(1)
                layer_norm(0)
                x_low(0)
                for b in range(B):
                    if b + 1 < B:
                        layer_norm(b + 1)
                        x_low(b + 1)
                    if b >= 1:
                        g_low(b - 1)
                    if b + 2 < B:
                        stats(b + 2)
                    accumulate(b)
                    if b >= 1:
                        residual(b - 1)
                g_low(B - 1)
                residual(B - 1)

            @block.tensor
            def _(pe):
                def transpose_x(b):
                    pe.wait_ge(lndone, TPB * (b + 1))
                    for u in range(TPB):
                        for k in range(KC):
                            mm = nc.tensor.transpose(ps_x[:, k, u * P:(u + 1) * P], xn[:, b % 2, u, k * P:(k + 1) * P], c("ident"))
                    mm.then_inc(xt_ready, 1)

                def sums(b):
                    pe.wait_ge(xlo, b + 1)
                    if b >= 2:
                        pe.wait_ge(relud, UN * (b - 1))
                    n = 0
                    for k in range(KC):
                        for l, r in split3(wi[1][:, k, :], wi[2][:, k, :], xh[:, b % 2, k, :], xl[:, b % 2, k, :]):
                            mm = nc.tensor.matmul(ps_s[:, b % 2, :], l, r, start=(n == 0), stop=(n == KC * PASSES - 1))
                            n += 1
                    mm.then_inc(s_ready, 1)

                def outputs(b):
                    pe.wait_ge(glo, b + 1)
                    if b >= 1:
                        pe.wait_ge(resd, 2 * b)
                    for u in range(TPB):
                        us = slice(u * P, (u + 1) * P)
                        rh, rl = (w[:].rearrange("p k n -> p (k n)") for w in wo[1:])
                        for n, (l, r) in enumerate(split3(gh[:, b % 2, us], gl[:, b % 2, us], rh, rl)):
                            mm = nc.tensor.matmul(ps_y[:, u // 2, (u % 2) * C:(u % 2 + 1) * C], l, r, start=(n == 0), stop=(n == PASSES - 1))
                        if u % 2:
                            mm.then_inc(y_ready, 1)

                pe.wait_ge(wlo, 2)
                transpose_x(0)
                sums(0)
                for b in range(B):
                    if b + 1 < B:
                        transpose_x(b + 1)
                        sums(b + 1)
                    if b >= 1:
                        outputs(b - 1)
                outputs(B - 1)


def packed_rows(i):
    f = np.float32
    p = np.arange(P)

    def rep(a):
        return np.broadcast_to(np.reshape(a, (1, -1)), (P, np.size(a)))

    def cols(a):
        return np.reshape(a, (-1, P)).T

    def halves(a):
        return np.concatenate([a[:, :INNER // 2], a[:, INNER // 2:]], axis=0)

    parts = {
        "ident": np.eye(P, dtype=f), "tri": np.triu(np.ones((P, P), f), 1),
        "mask": (p[:, None] // D0 == np.arange(P // D0)[None, :]).astype(f),
        "rev": rep(np.arange(NE, 0, -1, dtype=f)), "item": rep(np.arange(ITEMS, dtype=f)), "ones": np.ones((P, P), f),
        "bq": cols(i["L0_xattn_bq"]), "bk": cols(i["L0_xattn_bk"]), "bv": rep(i["L0_xattn_bv"]), "bo": rep(i["L0_xattn_bo"]),
        "bg": rep(i["L0_ffn_bg"]), "gx": rep(i["g_xattn"]), "gf": rep(i["g_ffn"]), "bout1": rep(i["L1_xattn_b_out"]),
        "fbin": np.reshape(np.concatenate([i["L1_ffn_bin_"]] * 2), (P, 1)),
        "fw1": halves(i["L1_ffn_W1"]), "fb1": halves(i["L1_ffn_b1"]), "fw2": halves(i["L1_ffn_W2"]),
        "fb2": np.reshape(np.concatenate([i["L1_ffn_b2"], np.zeros(M1, f)]), (P, 1)), "fbout": rep(i["L1_ffn_bout"]),
        "scan": rep((np.arange(P) % TILES != 0).astype(f)),
        "place": rep(np.arange(P, dtype=f)), "token": (np.arange(TILES)[None, :] * P + p[:, None]).astype(f),
    }
    return np.concatenate([parts[n] for n, _ in ROWS], axis=1)


def laid_out(i):
    return {
        "x": i["x"], "ctxt": np.reshape(np.transpose(i["ctx_768"], (2, 0, 1)), (CK, B * KV)),
        "wq0": i["L0_xattn_Wq"], "wk0": i["L0_xattn_Wk"], "wv0": i["L0_xattn_Wv"], "wo0": i["L0_xattn_Wo"],
        "wg": np.transpose(i["L0_ffn_Wg"]),
        "w1": np.transpose(i["L0_ffn_w1"], (0, 2, 1)), "w2": np.transpose(i["L0_ffn_w2"], (0, 2, 1)),
        "wqt1": np.transpose(i["L1_xattn_w_q"]), "wk1": i["L1_xattn_w_k"], "wv1": i["L1_xattn_w_v"], "wo1": i["L1_xattn_w_out"],
        "fwin": np.concatenate([i["L1_ffn_Win"]] * 2, axis=1), "fwout": np.concatenate([i["L1_ffn_Wout"]] * 2, axis=0),
        "rows": packed_rows(i),
    }


def kernel(**inputs):
    import concourse.bacc as bacc
    from concourse.bass_utils import run_bass_kernel_spmd

    nc = bacc.Bacc("TRN2", target_bir_lowering=False, num_devices=1)
    arrays, args = {}, []
    for name, a in laid_out({k: np.asarray(v) for k, v in inputs.items()}).items():
        arrays[f"in_{name}"] = np.ascontiguousarray(a)
        args.append(nc.dram_tensor(f"in_{name}", a.shape, mybir.dt.from_np(a.dtype), kind="ExternalInput").ap())
    args.append(nc.dram_tensor("out", (B, S, C), F32, kind="ExternalOutput").ap())
    gated_blocks(nc, *args)
    return run_bass_kernel_spmd(nc, [arrays], core_ids=[0]).results[0]["out"]
```

```python
from contextlib import ExitStack

import numpy as np

import concourse.bass as bass
from concourse import mybir

ALU = mybir.AluOpType
ACT = mybir.ActivationFunctionType
AX = mybir.AxisListType
F32 = mybir.dt.float32
F32R = mybir.dt.float32r
I32 = mybir.dt.int32
U32 = mybir.dt.uint32
ds = bass.ds

P = 128
B, S, C = 4, 512, 256
KV, CK = 64, 192
KP = CK // 2
NTOK = B * S
TILES = NTOK // P
TPB = S // P
KC = C // P
H = 16
PAIRS = H // 2
D0 = C // H
D1 = 64
HK = H * KV
CLAMP = 10000.0
EPS = 1e-5
NE, TOPK = 8, 2
FF = 256
ITEMS = TOPK * NTOK // P + NE
SLOTS = ITEMS * P
M1, INNER = 64, 16
VW = D0 + 1
PASSES = 3

ROWS = [("ident", P), ("tri", P), ("mask", P // D0), ("rev", NE), ("item", ITEMS), ("ones", P),
        ("bq", KC), ("bk", KC), ("bv", C), ("bo", C), ("bg", NE), ("gx", 2), ("gf", 2), ("bout1", C),
        ("fbin", 1), ("fw1", INNER // 2), ("fb1", INNER // 2), ("fw2", INNER // 2), ("fb2", 1), ("fbout", C),
        ("scan", P), ("place", P), ("token", TILES)]
COL, _o = {}, 0
for _n, _w in ROWS:
    COL[_n] = (_o, _o + _w)
    _o += _w
NCOL = _o


def split3(hi_l, lo_l, hi_r, lo_r):
    return ((hi_l, hi_r), (lo_l, hi_r), (hi_l, lo_r))


def live(t):
    return not isinstance(t, int) or 0 <= t < TILES


def staged(eng, body, first, steady, after, last):
    for i in range(first, steady):
        body(i, i % 2)
    with eng.Fori(steady // 2, after // 2) as turn:
        body(2 * turn, 0)
        body(2 * turn + 1, 1)
    for i in range(after, last):
        body(i, i % 2)


def gated_blocks(nc, x, ctxt, wq0, wk0, wv0, wo0, wg, w1, w2, wqt1, wk1, wv1, wo1, fwin, fwout, rows, out):
    top = ExitStack()
    with top:
        def sbuf(name, shape, dt=F32):
            return top.enter_context(nc.sbuf_tensor(name, shape, dt))

        xres = sbuf("xres", [P, TILES, C])
        cst = sbuf("cst", [P, NCOL])
        gates = sbuf("gates", [P, 4])
        mhalf = sbuf("mhalf", [P, 1])
        slots = sbuf("slots", [P, TOPK, TILES], U32)
        wsel = sbuf("wsel", [P, TOPK, TILES])
        xn_dram = nc.dram_tensor("normed_tokens", [NTOK, C], F32).ap()
        ys_dram = nc.dram_tensor("expert_out", [SLOTS, C], F32).ap()

        def c(name):
            return cst[:, COL[name][0]:COL[name][1]]

        with ExitStack() as ffn:
            w1l = ffn.enter_context(nc.sbuf_tensor("ffn0_w1_lo", [P, NE * KC, 2 * FF], F32R))
            w2l = ffn.enter_context(nc.sbuf_tensor("ffn0_w2_lo", [P, NE * 2, C], F32R))
            w_in = ffn.enter_context(nc.semaphore("ffn0_w_in"))
            lg = ffn.enter_context(nc.sbuf_tensor("ffn0_logits", [P, TILES * NE], F32))
            attention0(nc, c, x, ctxt, wq0, wk0, wv0, wo0, rows, xres, xn_dram, cst, gates, mhalf, wg, w1, w2, w1l, w2l, w_in, lg)
            second = SecondWeights(nc, ctxt, wqt1, wk1, wv1, wo1)
            experts(nc, c, w1l, w2l, w_in, lg, xn_dram, ys_dram, gates, slots, wsel, second)
        attention1(nc, c, second, ys_dram, xres, gates, mhalf, slots, wsel)
        mlp1(nc, c, fwin, fwout, xres, gates, mhalf, out)


def attention0(nc, c, x, ctxt, wq0, wk0, wv0, wo0, rows, xres, xn_dram, cst, gates, mhalf, wg, w1, w2, w1l, w2l, w_in, lg):
    with ExitStack() as keep:
        def sbuf(name, shape, dt=F32, on=keep):
            return on.enter_context(nc.sbuf_tensor(f"a0_{name}", shape, dt))

        bkh, bkl = (sbuf(f"blockk_{s}", [P, B, KC, 8 * KV], F32R) for s in ("hi", "lo"))
        bvh, bvl = (sbuf(f"blockv_{s}", [P, B * PAIRS, 2 * VW], F32R) for s in ("hi", "lo"))
        wqh, wql = (sbuf(f"wq_{s}", [P, KC, C], F32R) for s in ("hi", "lo"))
        woh, wol = (sbuf(f"wo_{s}", [P, KC, C], F32R) for s in ("hi", "lo"))
        bos = sbuf("bo_scaled", [P, C])
        wghl = sbuf("wg_hi_lo", [P, KC, 2 * NE], F32R)
        mean, rstd = sbuf("ln_mean_var", [P, TILES, 2]), sbuf("ln_rstd", [P, TILES])
        prepare0(nc, c, x, ctxt, wq0, wk0, wv0, wo0, rows, xres, cst, gates, mhalf,
                 bkh, bkl, bvh, bvl, wqh, wql, woh, wol, bos, wg, wghl, mean, rstd, w1, w2, w1l, w2l, w_in)
        attend0(nc, c, xres, xn_dram, mhalf, bkh, bkl, bvh, bvl, wqh, wql, woh, wol, bos, wghl, mean, rstd, lg)


def prepare0(nc, c, x, ctxt, wq0, wk0, wv0, wo0, rows, xres, cst, gates, mhalf,
             bkh, bkl, bvh, bvl, wqh, wql, woh, wol, bos, wg, wghl, mean, rstd, w1, w2, w1l, w2l, w_in):
    with ExitStack() as ctx:
        def sbuf(name, shape, dt=F32):
            return ctx.enter_context(nc.sbuf_tensor(f"kv0_{name}", shape, dt))

        def sem(name):
            return ctx.enter_context(nc.semaphore(f"kv0_{name}"))

        ctr, cth, ctl = sbuf("ctx_raw", [KP, 2, B * KV]), sbuf("ctx_hi", [KP, 2, B * KV], F32R), sbuf("ctx_lo", [KP, 2, B * KV], F32R)
        dch, dcl = sbuf("ctx2_hi", [KP, 2, B, 2, KV], F32R), sbuf("ctx2_lo", [KP, 2, B, 2, KV], F32R)
        wkr, wkh, wkl = sbuf("wk_raw", [KP, 2, C]), sbuf("wk_hi", [KP, 2, C], F32R), sbuf("wk_lo", [KP, 2, C], F32R)
        wvr, wvh, wvl = sbuf("wv_raw", [KP, 2, C]), sbuf("wv_hi", [KP, 2, C], F32R), sbuf("wv_lo", [KP, 2, C], F32R)
        wqr, wor, wos = sbuf("wq_raw", [P, KC, C]), sbuf("wo_raw", [P, KC, C]), sbuf("wo_scaled", [P, KC, C])
        kf, vf = sbuf("k_full", [P, KC, B * KV]), sbuf("v_full", [P, B, C])
        kh, kl = sbuf("k_hi", [P, KC, B * KV]), sbuf("k_lo", [P, KC, B * KV])
        wgr = sbuf("wg_raw", [P, KC, NE])
        st, ve = sbuf("ln_stats", [P, TILES, 6]), sbuf("ln_var_eps", [P, TILES])
        psk = ctx.enter_context(nc.psum_tensor("kv0_psk", [P, KC, 512], F32))
        psv = ctx.enter_context(nc.psum_tensor("kv0_psv", [P, 2, 512], F32))

        cst_in, ctx_in, wk_in, wv_in, wq_in, wo_in = (sem(n) for n in (
            "cst_in", "ctx_in", "wk_in", "wv_in", "wq_in", "wo_in"))
        x_in = [sem(f"x_in{b}") for b in range(B)]
        gate_done, his, los = sem("gate_done"), sem("his"), sem("los")
        k_ready, v_ready, k_full, v_full = sem("k_ready"), sem("v_ready"), sem("k_full"), sem("v_full")
        kv_hi, kv_lo, wo_scaled = sem("kv_hi"), sem("kv_lo"), sem("wo_scaled_done")
        cleared, wg_in, wg_hi = sem("cleared"), sem("wg_in"), sem("wg_hi_done")
        lnst, lnmv, lnve, lnrs = (sem(n) for n in ("ln_stats_done", "ln_mv_done", "ln_ve_done", "ln_rstd_done"))

        weights = [(ctr, cth, ctl, ctx_in), (wkr, wkh, wkl, wk_in), (wvr, wvh, wvl, wv_in),
                   (wqr, wqh, wql, wq_in), (wos, woh, wol, wo_scaled)]

        with nc.Block() as block:
            @block.sync
            def _(sp):
                sp.dma_start(ctr[:], ctxt.rearrange("(k p) n -> p k n", p=KP)).then_inc(ctx_in, 16)
                sp.dma_start(wkr[:], wk0.rearrange("(k p) n -> p k n", p=KP)).then_inc(wk_in, 16)
                sp.dma_start(cst[:], rows).then_inc(cst_in, 16)
                sp.dma_start(wvr[:], wv0.rearrange("(k p) n -> p k n", p=KP)).then_inc(wv_in, 16)
                sp.dma_start(wqr[:], wq0.rearrange("(k p) n -> p k n", p=P)).then_inc(wq_in, 16)
                sp.dma_start(wor[:], wo0.rearrange("(k p) n -> p k n", p=P)).then_inc(wo_in, 16)
                for b in range(B):
                    sp.dma_start(xres[:, b * TPB:(b + 1) * TPB, :],
                                 x[b].rearrange("(t p) c -> p t c", p=P)).then_inc(x_in[b], 16)
                sp.dma_start(wgr[:], wg.rearrange("(k p) e -> p k e", p=P)).then_inc(wg_in, 16)
                for e in range(NE):
                    sp.dma_start(w1l[:, e * KC:(e + 1) * KC, :].bitcast(F32), w1[e].rearrange("(k p) f -> p k f", p=P)).then_inc(w_in, 16)
                    sp.dma_start(w2l[:, e * 2:(e + 1) * 2, :].bitcast(F32), w2[e].rearrange("(k p) f -> p k f", p=P)).then_inc(w_in, 16)

            @block.gpsimd
            def _(pool):
                pool.memset(mhalf[:], -0.5)
                pool.memset(bvh[:].bitcast(F32), 0.0).then_inc(cleared, 1)
                pool.memset(bvl[:].bitcast(F32), 0.0).then_inc(cleared, 1)
                pool.wait_ge(cleared, 2)
                pool.memset(bvh[0:KV, :, D0:VW].bitcast(F32), 1.0).then_inc(cleared, 1)
                pool.memset(bvh[KV:P, :, VW + D0:2 * VW].bitcast(F32), 1.0).then_inc(cleared, 1)
                pool.wait_ge(cleared, 4)
                for g in range(KC):
                    pool.wait_ge(kv_lo, g + 1)
                    pool.wait_ge(cst_in, 16)
                    pool.tensor_tensor(bkl[:, :, g, :].rearrange("p b (h k) -> p b h k", k=KV),
                                       kl[:, g, :].rearrange("p (b o k) -> p b o k", o=1, k=KV).broadcast_to([P, B, 8, KV]),
                                       c("mask").rearrange("p (o h q) -> p o h q", o=1, q=1).broadcast_to([P, B, 8, KV]),
                                       ALU.mult)
                pool.wait_ge(lnve, 1)
                pool.tensor_tensor(rstd[:], ve[:], mhalf[:].broadcast_to([P, TILES]), ALU.pow).then_inc(lnrs, 1)

            @block.scalar
            def _(act):
                for raw, hi, _, loaded in weights[:2]:
                    act.wait_ge(loaded, 16)
                    act.copy(hi[:], raw[:]).then_inc(his, 1)
                act.wait_ge(cst_in, 16)
                act.activation(gates[:, 0:2], c("gx"), ACT.Tanh).then_inc(gate_done, 1)
                act.activation(gates[:, 2:4], c("gf"), ACT.Tanh).then_inc(gate_done, 1)
                for raw, hi, _, loaded in weights[2:]:
                    act.wait_ge(loaded, 1 if loaded is wo_scaled else 16)
                    act.copy(hi[:], raw[:]).then_inc(his, 1)
                for g in range(KC):
                    act.wait_ge(k_full, g + 1)
                    act.copy(kh[:, g, :].bitcast(F32R), kf[:, g, :]).then_inc(kv_hi, 1)
                act.wait_ge(cleared, 4)
                for h in range(2):
                    act.wait_ge(v_full, 2)
                    act.copy(bvh[h * KV:(h + 1) * KV, :, h * VW:h * VW + D0],
                             vf[h * KV:(h + 1) * KV].rearrange("p b (j h d) -> p (b j) h d", h=2, d=D0)[:, :, h, :]).then_inc(kv_hi, 1)
                act.wait_ge(wg_in, 16)
                act.copy(wghl[:, :, 0:NE], wgr[:]).then_inc(wg_hi, 1)

            @block.vector
            def _(dve):
                for n, (raw, hi, lo, _) in enumerate(weights):
                    if raw is wos:
                        dve.wait_ge(wo_in, 16)
                        dve.wait_ge(gate_done, 2)
                        dve.tensor_scalar(wos[:], wor[:], gates[:, 0:1], None, ALU.mult).then_inc(wo_scaled, 1)
                        dve.tensor_scalar(bos[:], c("bo"), gates[:, 0:1], None, ALU.mult)
                        dve.wait_ge(wo_scaled, 1)
                    dve.wait_ge(his, n + 1)
                    dve.tensor_tensor(lo[:], raw[:], hi[:].bitcast(F32), ALU.subtract).then_inc(los, 1)
                    if raw is ctr:
                        dve.wait_ge(los, 1)
                        for src, dst in ((cth, dch), (ctl, dcl)):
                            for h in range(2):
                                dve.tensor_copy(dst[:, :, :, h, :].rearrange("p k b n -> p k b n"),
                                                src[:].rearrange("p k (b n) -> p k b n", b=B)).then_inc(los, 1)
                for g in range(KC):
                    dve.wait_ge(k_ready, g + 1)
                    dve.wait_ge(cst_in, 16)
                    dve.tensor_scalar(kf[:, g, :], psk[:, g, 0:B * KV], c("bk")[:, g:g + 1], D0 ** -0.5,
                                      ALU.add, ALU.mult).then_inc(k_full, 1)
                for v2 in range(2):
                    dve.wait_ge(v_ready, v2 + 1)
                    dve.tensor_tensor(vf[:, 2 * v2:2 * v2 + 2, :], psv[:, v2, :].rearrange("p (b c) -> p b c", b=2),
                                      c("bv").rearrange("p (o c) -> p o c", o=1).broadcast_to([P, 2, C]), ALU.add).then_inc(v_full, 1)
                for g in range(KC):
                    dve.wait_ge(kv_hi, g + 1)
                    dve.tensor_tensor(kl[:, g, :], kf[:, g, :], kh[:, g, :], ALU.subtract).then_inc(kv_lo, 1)
                    dve.tensor_tensor(bkh[:, :, g, :].rearrange("p b (h k) -> p b h k", k=KV),
                                      kh[:, g, :].rearrange("p (b o k) -> p b o k", o=1, k=KV).broadcast_to([P, B, 8, KV]),
                                      c("mask").rearrange("p (o h q) -> p o h q", o=1, q=1).broadcast_to([P, B, 8, KV]),
                                      ALU.mult)
                dve.wait_ge(cleared, 4)
                for h in range(2):
                    dve.wait_ge(kv_hi, KC + h + 1)
                    rs = slice(h * KV, (h + 1) * KV)
                    dve.tensor_tensor(bvl[rs, :, h * VW:h * VW + D0],
                                      vf[rs].rearrange("p b (j h d) -> p (b j) h d", h=2, d=D0)[:, :, h, :],
                                      bvh[rs, :, h * VW:h * VW + D0].bitcast(F32), ALU.subtract)
                for t in range(TILES):
                    dve.wait_ge(x_in[t // TPB], 16)
                    dve.bn_stats(st[:, t, :], xres[:, t, :]).then_inc(lnst, 1)
                for t in range(TILES):
                    dve.wait_ge(lnst, t + 1)
                    dve.bn_aggr(mean[:, t, :], st[:, t, :]).then_inc(lnmv, 1)
                dve.wait_ge(lnmv, TILES)
                dve.tensor_scalar(ve[:], mean[:, :, 1], EPS, None, ALU.add).then_inc(lnve, 1)
                dve.wait_ge(wg_hi, 1)
                dve.tensor_tensor(wghl[:, :, NE:2 * NE], wgr[:], wghl[:, :, 0:NE].bitcast(F32), ALU.subtract)

            @block.tensor
            def _(pe):
                pe.wait_ge(los, 1 + 4 + 1)
                for g in range(KC):
                    n = 0
                    for k in range(2):
                        m = slice(g * P, (g + 1) * P)
                        for l, r in split3(wkh[:, k, m], wkl[:, k, m], cth[:, k, :], ctl[:, k, :]):
                            mm = nc.tensor.matmul(psk[:, g, 0:B * KV], l, r, start=(n == 0), stop=(n == 2 * PASSES - 1))
                            n += 1
                    mm.then_inc(k_ready, 1)
                pe.wait_ge(los, 1 + 4 + 2)
                for v2 in range(2):
                    for b in (2 * v2, 2 * v2 + 1):
                        n = 0
                        for k in range(2):
                            lh, ll = (t[:, k, b].rearrange("p h n -> p (h n)") for t in (dch, dcl))
                            for l, r in split3(lh, ll, wvh[:, k, :], wvl[:, k, :]):
                                mm = nc.tensor.matmul(psv[:, v2, (b % 2) * C:(b % 2 + 1) * C], l, r,
                                                      start=(n == 0), stop=(n == 2 * PASSES - 1))
                                n += 1
                    mm.then_inc(v_ready, 1)


def attend0(nc, c, xres, xn_dram, mhalf, bkh, bkl, bvh, bvl, wqh, wql, woh, wol, bos, wghl, mean, rstd, lg):
    with ExitStack() as ctx:
        def sbuf(name, shape, dt=F32):
            return ctx.enter_context(nc.sbuf_tensor(f"att0_{name}", shape, dt))

        def sem(name):
            return ctx.enter_context(nc.semaphore(f"att0_{name}"))

        def bank(name, n=1):
            return ctx.enter_context(nc.psum_tensor(f"att0_{name}", [P, n, 512], F32))

        st, mv = sbuf("ln_stats", [P, 2, 6]), sbuf("ln_mean_var", [P, 2, 2])
        ve, rs = sbuf("ln_var_eps", [P, 2]), sbuf("ln_rstd", [P, 2])
        xn = sbuf("xn", [P, 2, 2, C])
        xh, xl = sbuf("xt_hi", [P, 2, 2, C], F32R), sbuf("xt_lo", [P, 2, 2, C], F32R)
        qf = sbuf("q_full", [P, 2, C])
        qh, ql = sbuf("qt_hi", [P, 2, C], F32R), sbuf("qt_lo", [P, 2, C], F32R)
        sc = sbuf("scores", [P, 2, HK])
        mx = sbuf("score_max", [P, 2, H])
        ph, pl = sbuf("pt_hi", [P, 2, HK], F32R), sbuf("pt_lo", [P, 2, HK], F32R)
        rc = sbuf("recip", [P, 2, H])
        on = sbuf("o_norm", [P, 2, C])
        oh, ol = sbuf("ot_hi", [P, 2, C], F32R), sbuf("ot_lo", [P, 2, C], F32R)
        ps_s, ps_p = bank("ps_scores", 2), bank("ps_pt", 2)
        ps_o, ps_x, ps_q, ps_m = bank("ps_pv"), bank("ps_xt"), bank("ps_q"), bank("ps_oy")

        (xt_ready, q_ready, s_ready, pt_ready, pv_ready, ot_ready, y_ready) = (sem(n) for n in (
            "xt_ready", "q_ready", "scores_ready", "pt_ready", "pv_ready", "ot_ready", "y_ready"))
        (xhi, qhi, expd, phi, ohi) = (sem(n) for n in ("xt_hi_done", "q_hi_done", "exp_done", "pt_hi_done", "ot_hi_done"))
        (copied,) = (sem("scores_copied"),)
        (xlo, qsum, clipd, maxd, plo, recd, normd, olo, resd) = (sem(n) for n in (
            "xt_lo_done", "q_biased", "clipped", "max_done", "pt_lo_done", "recip_done", "o_normed", "ot_lo_done", "residual_done"))
        lnve, lndone, lnrs = sem("ln_next_ve"), [sem("ln_out"), sem("ln_next_out")], sem("ln_next_rstd")
        logits, lg_part = sem("logits_ready"), sem("lg_part")
        stored = [sem("xn_next_stored0"), sem("xn_next_stored1")]
        (cent, qlo, xbias) = (sem(n) for n in ("centred", "q_lo_done", "bias_added"))
        ident = c("ident")
        NEXT = 7

        def halves(u):
            return slice(0 if live(u) else 1, 2 if live(u - NEXT) else 1)

        def transposing(u):
            return live(u) or live(u - NEXT)

        with nc.Block() as block:
            @block.sync
            def _(sp):
                def store(t, p):
                    sp.wait_ge(lndone[1], t + 1)
                    sp.dma_start(xn_dram[ds(t * P, P), :], xn[:, (p + NEXT) % 2, 1, :]).then_inc(stored[p], 16)

                def body(i, par):
                    if live(i - 4):
                        store(i - 4, par % 2)
                staged(sp, body, 4, 6, 12, TILES + 4)
                for p in range(2):
                    sp.wait_ge(stored[p], 16 * TILES // 2)

            @block.tensor
            def _(pe):
                def route_logits(t, p):
                    pe.wait_ge(xlo, t + NEXT + 1)
                    steps = ((xh, 0, 2), (xl, 0, 1), (xl, 1, 1), (xh, 1, 2))
                    for n, (lhs, k, w) in enumerate(steps):
                        mm = nc.tensor.matmul(ps_q[:, 0, ds(t * 2 * NE + C, w * NE)], lhs[:, (p + NEXT) % 2, 1, k * P:(k + 1) * P],
                                              wghl[:, k, 0:w * NE], start=(n == 0), stop=(n == len(steps) - 1))
                    mm.then_inc(logits, 1)

                def scores(t, p):
                    pe.wait_ge(qlo, t + 1)
                    if not isinstance(t, int) or t > 0:
                        pe.wait_ge(copied, t)
                    for g in range(KC):
                        gs = slice(g * P, (g + 1) * P)
                        rh, rl = (w[:, ds(t // TPB, 1), g, :].rearrange("p o n -> p (o n)") for w in (bkh, bkl))
                        for n, (l, r) in enumerate(split3(qh[:, p, gs], ql[:, p, gs], rh, rl)):
                            mm = nc.tensor.matmul(ps_s[:, g, :], l, r, start=(n == 0), stop=(n == PASSES - 1))
                    mm.then_inc(s_ready, 1)

                def transpose_probs(t, p):
                    pe.wait_ge(expd, t + 1)
                    for j in range(PAIRS):
                        mm = nc.tensor.transpose(ps_p[:, j // 4, (j % 4) * P:(j % 4 + 1) * P],
                                                 sc[:, p, j * P:(j + 1) * P], ident)
                        if j % 4 == 3:
                            mm.then_inc(pt_ready, 1)

                def transpose_x(u, p):
                    if live(u):
                        pe.wait_ge(lndone[0], u + 1)
                    if live(u - NEXT):
                        pe.wait_ge(lndone[1], u - NEXT + 1)
                    for h in range(2)[halves(u)]:
                        for k in range(KC):
                            mm = nc.tensor.transpose(ps_x[:, 0, h * C + k * P:h * C + (k + 1) * P], xn[:, p, h, k * P:(k + 1) * P], ident)
                    mm.then_inc(xt_ready, 1)

                def transpose_o(t, p):
                    pe.wait_ge(normd, t + 1)
                    if not isinstance(t, int) or t > 0:
                        pe.wait_ge(resd, t)
                    for k in range(KC):
                        mm = nc.tensor.transpose(ps_m[:, 0, k * P:(k + 1) * P], on[:, p, k * P:(k + 1) * P], ident)
                    mm.then_inc(ot_ready, 1)

                def weighted_values(t, p):
                    pe.wait_ge(plo, 2 * t + 2)
                    for j in range(PAIRS):
                        js = slice(j * P, (j + 1) * P)
                        rh, rl = (w[:, ds(t // TPB * PAIRS + j, 1), :].rearrange("p o n -> p (o n)") for w in (bvh, bvl))
                        for n, (l, r) in enumerate(split3(ph[:, p, js], pl[:, p, js], rh, rl)):
                            mm = nc.tensor.matmul(ps_o[:, 0, j * 2 * VW:(j + 1) * 2 * VW], l, r,
                                                  start=(n == 0), stop=(n == PASSES - 1))
                    mm.then_inc(pv_ready, 1)

                def queries(t, p):
                    pe.wait_ge(xlo, t + 1)
                    for m in range(KC):
                        ms, n = slice(m * P, (m + 1) * P), 0
                        for k in range(KC):
                            ks = slice(k * P, (k + 1) * P)
                            for l, r in split3(wqh[:, k, ms], wql[:, k, ms], xh[:, p, 0, ks], xl[:, p, 0, ks]):
                                mm = nc.tensor.matmul(ps_q[:, 0, ms], l, r, start=(n == 0), stop=(n == KC * PASSES - 1))
                                n += 1
                    mm.then_inc(q_ready, 1)

                def project(t, p):
                    pe.wait_ge(olo, t + 1)
                    n = 0
                    for k in range(KC):
                        ks = slice(k * P, (k + 1) * P)
                        for l, r in split3(oh[:, p, ks], ol[:, p, ks], woh[:, k, :], wol[:, k, :]):
                            mm = nc.tensor.matmul(ps_m[:, 0, C:2 * C], l, r, start=(n == 0), stop=(n == KC * PASSES - 1))
                            n += 1
                    mm.then_inc(y_ready, 1)

                def body(i, par):
                    for stage, d in ((transpose_probs, -2), (scores, 0), (transpose_x, 2), (transpose_o, -3),
                                     (weighted_values, -2), (route_logits, -5), (queries, 2), (project, -3)):
                        if live(i + d) or stage is transpose_x and transposing(i + d):
                            stage(i + d, (par + d) % 2)
                staged(pe, body, -2, 6, 12, TILES + 5)

            @block.scalar
            def _(act):
                def copy_scores(t, p):
                    act.wait_ge(s_ready, t + 1)
                    if not isinstance(t, int) or t > 1:
                        act.wait_ge(pt_ready, 2 * t - 2)
                    act.copy(sc[:, p, :].rearrange("p (a n) -> p a n", a=2), ps_s[:]).then_inc(copied, 1)

                def x_high(t, p):
                    act.wait_ge(xt_ready, t + 1)
                    hs = halves(t)
                    act.copy(xh[:, p, hs, :], ps_x[:, 0, :].rearrange("p (h c) -> p h c", h=2)[:, hs, :]).then_inc(xhi, 1)

                def probs_high(t, p):
                    for half in range(2):
                        act.wait_ge(pt_ready, 2 * t + half + 1)
                        act.copy(ph[:, p, half * 512:(half + 1) * 512], ps_p[:, half, :]).then_inc(phi, 1)

                def o_high(t, p):
                    act.wait_ge(ot_ready, t + 1)
                    act.copy(oh[:, p, :], ps_m[:, 0, 0:C]).then_inc(ohi, 1)

                def q_high(t, p):
                    act.wait_ge(qsum, t + 1)
                    act.copy(qh[:, p, :], qf[:, p, :]).then_inc(qhi, 1)

                def exponential(t, p):
                    act.wait_ge(cent, t + 1)
                    act.activation(sc[:, p, :], sc[:, p, :], ACT.Exp).then_inc(expd, 1)

                def body(i, par):
                    for stage, d in ((exponential, -1), (probs_high, -2), (copy_scores, 0), (x_high, 2), (o_high, -3),
                                     (q_high, 2)):
                        if live(i + d) or stage is x_high and transposing(i + d):
                            stage(i + d, (par + d) % 2)
                staged(act, body, -2, 6, 12, TILES + 5)

            @block.gpsimd
            def _(pool):
                def rstd_next(t, p):
                    pool.wait_ge(lnve, t + 1)
                    pool.tensor_tensor(rs[:, p:p + 1], ve[:, p:p + 1], mhalf[:], ALU.pow).then_inc(lnrs, 1)

                def centre(t, p):
                    pool.wait_ge(maxd, t + 1)
                    s3 = sc[:, p, :].rearrange("p (h k) -> p h k", k=KV)
                    pool.tensor_tensor(s3, s3, mx[:, p, :].rearrange("p (h o) -> p h o", o=1).broadcast_to([P, H, KV]),
                                       ALU.subtract).then_inc(cent, 1)
                    xt = xres[:, ds(t, 1), :].rearrange("p o c -> p (o c)")
                    pool.tensor_tensor(xt, xt, bos[:], ALU.add).then_inc(xbias, 1)

                def q_low(t, p):
                    pool.wait_ge(qhi, t + 1)
                    pool.tensor_tensor(ql[:, p, :], qf[:, p, :], qh[:, p, :].bitcast(F32), ALU.subtract).then_inc(qlo, 1)

                def body(i, par):
                    for stage, d in ((centre, 0), (q_low, 2), (rstd_next, -3)):
                        if live(i + d):
                            stage(i + d, (par + d) % 2)
                staged(pool, body, -2, 6, 12, TILES + 3)

            @block.vector
            def _(dve):
                def tile_of(t):
                    return xres[:, ds(t, 1), :].rearrange("p o c -> p (o c)")

                def stats_next(t, p):
                    dve.drain()
                    dve.bn_stats(st[:, p, :], tile_of(t))
                    dve.drain()
                    dve.bn_aggr(mv[:, p, :], st[:, p, :])
                    dve.drain()
                    dve.tensor_scalar(ve[:, p:p + 1], mv[:, p, 1:2], EPS, None, ALU.add).then_inc(lnve, 1)

                def normed(t, p):
                    dve.tensor_scalar(xn[:, p, 0, :], tile_of(t), mean[:, ds(t, 1), 0:1].rearrange("p a b -> p (a b)"),
                                      rstd[:, ds(t, 1)], ALU.subtract, ALU.mult).then_inc(lndone[0], 1)

                def normed_next(t, p):
                    dve.wait_ge(lnrs, t + 1)
                    if not isinstance(t, int) or t > 1:
                        dve.wait_ge(stored[p], (t // 2) * 16)
                    dve.tensor_scalar(xn[:, (p + NEXT) % 2, 1, :], tile_of(t), mv[:, p, 0:1], rs[:, p:p + 1], ALU.subtract, ALU.mult).then_inc(lndone[1], 1)

                def clip_and_max(t, p):
                    dve.wait_ge(copied, t + 1)
                    dve.tensor_scalar(sc[:, p, :], sc[:, p, :], CLAMP, -CLAMP, ALU.min, ALU.max).then_inc(clipd, 1)
                    dve.wait_ge(clipd, t + 1)
                    dve.tensor_reduce(mx[:, p, :], sc[:, p, :].rearrange("p (h k) -> p h k", k=KV), AX.X, ALU.max).then_inc(maxd, 1)

                def probs_low(t, p):
                    for half in range(2):
                        hs = slice(half * 512, (half + 1) * 512)
                        dve.wait_ge(phi, 2 * t + half + 1)
                        dve.tensor_tensor(pl[:, p, hs], ps_p[:, half, :], ph[:, p, hs].bitcast(F32), ALU.subtract).then_inc(plo, 1)

                def x_low(t, p):
                    dve.wait_ge(xhi, t + 1)
                    hs = halves(t)
                    dve.tensor_tensor(xl[:, p, hs, :], ps_x[:, 0, :].rearrange("p (h c) -> p h c", h=2)[:, hs, :],
                                      xh[:, p, hs, :].bitcast(F32), ALU.subtract).then_inc(xlo, 1)

                def o_low(t, p):
                    dve.wait_ge(ohi, t + 1)
                    dve.tensor_tensor(ol[:, p, :], ps_m[:, 0, 0:C], oh[:, p, :].bitcast(F32), ALU.subtract).then_inc(olo, 1)

                def q_bias(t, p):
                    dve.wait_ge(q_ready, t + 1)
                    dve.tensor_tensor(qf[:, p, :].rearrange("p (m n) -> p m n", m=KC), ps_q[:, 0, 0:C].rearrange("p (m n) -> p m n", m=KC),
                                      c("bq").rearrange("p (m o) -> p m o", o=1).broadcast_to([P, KC, P]), ALU.add).then_inc(qsum, 1)

                def normalise_o(t, p):
                    dve.wait_ge(pv_ready, t + 1)
                    o3 = ps_o[:, 0, 0:H * VW].rearrange("p (h v) -> p h v", v=VW)
                    dve.reciprocal(rc[:, p, :], o3[:, :, D0]).then_inc(recd, 1)
                    dve.wait_ge(recd, t + 1)
                    dve.tensor_tensor(on[:, p, :].rearrange("p (h d) -> p h d", d=D0), o3[:, :, 0:D0],
                                      rc[:, p, :].rearrange("p (h o) -> p h o", o=1).broadcast_to([P, H, D0]), ALU.mult).then_inc(normd, 1)

                def residual(t, p):
                    dve.wait_ge(y_ready, t + 1)
                    dve.wait_ge(xbias, t + 1)
                    xt = xres[:, ds(t, 1), :].rearrange("p o c -> p (o c)")
                    dve.tensor_tensor(xt, ps_m[:, 0, C:2 * C], xt, ALU.add).then_inc(resd, 1)

                def body(i, par):
                    for stage, d in ((probs_low, -2), (clip_and_max, 0), (x_low, 2), (o_low, -3), (normed_next, -4),
                                     (q_bias, 2), (normed, 3), (normalise_o, -2), (residual, -3), (stats_next, -3)):
                        if live(i + d) or stage is x_low and transposing(i + d):
                            stage(i + d, (par + d) % 2)
                staged(dve, body, -3, 6, 12, TILES + 5)
                dve.wait_ge(logits, TILES)
                parts = ps_q[:, 0, C:2 * C].rearrange("p (t w e) -> p t w e", w=2, e=NE)
                lg3 = lg[:].rearrange("p (t e) -> p t e", e=NE)
                dve.tensor_tensor(lg3, parts[:, :, 0, :], c("bg").rearrange("p (o e) -> p o e", o=1).broadcast_to([P, TILES, NE]),
                                  ALU.add).then_inc(lg_part, 1)
                dve.wait_ge(lg_part, 1)
                dve.tensor_tensor(lg3, parts[:, :, 1, :], lg3, ALU.add)


def experts(nc, c, w1l, w2l, w_in, lg, xn_dram, ys_dram, gates, slots, wsel, second):
    with ExitStack() as ctx:
        def sbuf(name, shape, dt=F32):
            return ctx.enter_context(nc.sbuf_tensor(f"ffn0_{name}", shape, dt))

        w1h, w2h = sbuf("w1_hi", [P, NE * KC, 2 * FF], F32R), sbuf("w2_hi", [P, NE * 2, C], F32R)
        eid = sbuf("item_expert", [P, ITEMS], I32)
        token = sbuf("token_of_slot", [P, ITEMS], U32)
        route(nc, c, w1h, w1l, w2h, w2l, w_in, eid, token, lg, gates, slots, wsel)
        second.place()
        run_experts(nc, c, w1h, w1l, w2h, w2l, eid, token, xn_dram, ys_dram, second)


def route(nc, c, w1h, w1l, w2h, w2l, w_in, eid, token, lg0, gates, slots, wsel):
    with ExitStack() as ctx:
        def sbuf(name, shape, dt=F32):
            return ctx.enter_context(nc.sbuf_tensor(f"route_{name}", shape, dt))

        def sem(name):
            return ctx.enter_context(nc.semaphore(f"route_{name}"))

        TE, NB = TILES * NE, TOPK * TILES
        CHUNK = 8
        lg = [lg0, sbuf("logits1", [P, TE])]
        key = [sbuf(f"key{n}", [P, TE]) for n in range(2)]
        oneh = [sbuf(f"onehot{n}", [P, TE]) for n in range(2)]
        top = [sbuf(f"top{n}", [P, TILES]) for n in range(2)]
        kmax = [sbuf(f"keymax{n}", [P, TILES]) for n in range(2)]
        maskr = sbuf("chosen", [P, TE], F32R)
        trir, onesr = sbuf("tri_r", [P, P], F32R), sbuf("ones_r", [P, P], F32R)
        tot, incl, base, slot, tmp = (sbuf(n, [P, TE]) for n in ("totals_et", "inclusive", "base", "slot", "slot_picked"))
        cnt = sbuf("counts", [P, NE]); cnti = sbuf("counts_int", [P, NE], I32); ntl = sbuf("tiles_of_expert", [P, NE])
        endt, startt = sbuf("end_tile", [P, NE]), sbuf("start_slot", [P, NE])
        ge = sbuf("item_past_end", [P, ITEMS, NE]); eidf = sbuf("item_expert_f", [P, ITEMS])
        d21, ez, zp1, inv = (sbuf(n, [P, TILES]) for n in ("gap", "gap_exp", "denominator", "inverse"))
        slotf = sbuf("slot_f", [P, NB])
        sloti, itemf, placef = sbuf("slot_item_int", [P, NB], I32), sbuf("slot_item", [P, NB]), sbuf("slot_place", [P, NB])
        is_item, tok_item = sbuf("is_item", [P, NB, ITEMS]), sbuf("token_in_item", [P, NB, ITEMS], F32R)
        is_place = sbuf("is_place", [P, NB, P], F32R)
        ps_r = ctx.enter_context(nc.psum_tensor("route_ps_rank", [P, 512], F32))
        ps_c = ctx.enter_context(nc.psum_tensor("route_ps_totals", [P, 512], F32))
        ps_t = ctx.enter_context(nc.psum_tensor("route_ps_token", [P, 512], F32))

        whi = sem("w_hi_done")
        step, gap, gexp, chosen, rank, placed, inverted = (sem(n) for n in (
            "route_step", "gap_ready", "gap_exp_done", "chosen_ready", "rank_ready", "placed", "inverted"))

        def te(a):
            return a.rearrange("p (t e) -> p t e", e=NE)

        def over_e(a):
            return a.rearrange("p (t o) -> p t o", o=1).broadcast_to([P, TILES, NE])

        def over_t(a):
            return a.rearrange("p (o e) -> p o e", o=1).broadcast_to([P, TILES, NE])

        with nc.Block() as block:
            @block.tensor
            def _(pe):
                pe.wait_ge(chosen, 1)
                nc.tensor.matmul(ps_r[:, 0:TE], trir[:], maskr[:], start=True, stop=True)
                nc.tensor.matmul(ps_c[:, 0:TE], onesr[:], maskr[:], start=True, stop=True).then_inc(rank, 1)
                for n in range(NB):
                    if n % CHUNK == 0:
                        pe.wait_ge(placed, n // CHUNK + 1)
                    mm = nc.tensor.matmul(ps_t[:, 0:ITEMS], is_place[:, n, :], tok_item[:, n, :], start=(n == 0), stop=(n == NB - 1))
                mm.then_inc(inverted, 1)

            @block.scalar
            def _(act):
                act.wait_ge(w_in, 32 * NE)
                for e in range(NE):
                    if e == 2:
                        act.wait_ge(gap, 1)
                        act.activation(ez[:], d21[:], ACT.Exp).then_inc(gexp, 1)
                    act.copy(w1h[:, e * KC:(e + 1) * KC, :], w1l[:, e * KC:(e + 1) * KC, :].bitcast(F32)).then_inc(whi, 1)
                    act.copy(w2h[:, e * 2:(e + 1) * 2, :], w2l[:, e * 2:(e + 1) * 2, :].bitcast(F32)).then_inc(whi, 1)

            @block.gpsimd
            def _(pool):
                for e in range(NE):
                    for n, (hi, lo, w) in enumerate(((w1h, w1l, KC), (w2h, w2l, 2))):
                        es = slice(e * w, (e + 1) * w)
                        pool.wait_ge(whi, 2 * e + n + 1)
                        pool.tensor_tensor(lo[:, es, :], lo[:, es, :].bitcast(F32), hi[:, es, :].bitcast(F32), ALU.subtract)

            @block.vector
            def _(dve):
                steps = [0]

                def link(ins):
                    steps[0] += 1
                    ins.then_inc(step, 1)
                    dve.wait_ge(step, steps[0])

                dve.tensor_copy(trir[:], c("tri"))
                dve.tensor_copy(onesr[:], c("ones"))
                for n in range(TOPK):
                    link(dve.tensor_reduce(top[n][:], te(lg[n][:]), AX.X, ALU.max))
                    link(dve.tensor_tensor(te(key[n][:]), te(lg[n][:]), over_e(top[n][:]), ALU.is_equal))
                    link(dve.tensor_tensor(te(key[n][:]), te(key[n][:]), over_t(c("rev")), ALU.mult))
                    link(dve.tensor_reduce(kmax[n][:], te(key[n][:]), AX.X, ALU.max))
                    link(dve.tensor_tensor(te(oneh[n][:]), over_t(c("rev")), over_e(kmax[n][:]), ALU.is_equal))
                    if n == 0:
                        link(dve.scalar_tensor_tensor(out=lg[1][:], in0=oneh[0][:], scalar=-3e38, in1=lg[0][:], op0=ALU.mult, op1=ALU.add))
                dve.tensor_tensor(maskr[:], oneh[0][:], oneh[1][:], ALU.add).then_inc(chosen, 1)
                dve.tensor_tensor(d21[:], top[1][:], top[0][:], ALU.subtract).then_inc(gap, 1)
                dve.wait_ge(rank, 1)
                link(dve.tensor_copy(tot[:].rearrange("p (e t) -> p t e", e=NE), te(ps_c[:, 0:TE])))
                link(dve.tensor_tensor_scan(incl[:], c("scan"), tot[:], 0.0, ALU.mult, ALU.add))
                link(dve.tensor_scalar(cnt[:], incl[:].rearrange("p (e t) -> p e t", e=NE)[:, :, TILES - 1], float(P - 1), None, ALU.add))
                link(dve.tensor_copy(cnti[:], cnt[:]))
                link(dve.tensor_single_scalar(cnti[:], cnti[:], 7, ALU.arith_shift_right))
                link(dve.tensor_copy(ntl[:], cnti[:]))
                link(dve.tensor_tensor_scan(endt[:], c("ones")[:, 0:NE], ntl[:], 0.0, ALU.mult, ALU.add))
                link(dve.tensor_tensor(startt[:], endt[:], ntl[:], ALU.subtract))
                link(dve.tensor_scalar(startt[:], startt[:], float(P), None, ALU.mult))
                link(dve.tensor_tensor(incl[:], incl[:], tot[:], ALU.subtract))
                link(dve.tensor_tensor(te(base[:]), incl[:].rearrange("p (e t) -> p t e", e=NE), over_t(startt[:]), ALU.add))
                link(dve.tensor_tensor(slot[:], ps_r[:, 0:TE], base[:], ALU.add))
                for n in range(TOPK):
                    link(dve.tensor_tensor(tmp[:], slot[:], oneh[n][:], ALU.mult))
                    link(dve.tensor_reduce(slotf[:, n * TILES:(n + 1) * TILES], te(tmp[:]), AX.X, ALU.add))
                dve.tensor_copy(slots[:].rearrange("p k t -> p (k t)"), slotf[:])
                link(dve.tensor_copy(sloti[:], slotf[:]))
                link(dve.tensor_single_scalar(sloti[:], sloti[:], 7, ALU.arith_shift_right))
                link(dve.tensor_copy(itemf[:], sloti[:]))
                link(dve.scalar_tensor_tensor(out=placef[:], in0=itemf[:], scalar=-float(P), in1=slotf[:], op0=ALU.mult, op1=ALU.add))
                link(dve.tensor_tensor(is_item[:], c("item").rearrange("p (o j) -> p o j", o=1).broadcast_to([P, NB, ITEMS]),
                                       itemf[:].rearrange("p (n o) -> p n o", o=1).broadcast_to([P, NB, ITEMS]), ALU.is_equal))
                for k in range(TOPK):
                    ks = slice(k * TILES, (k + 1) * TILES)
                    link(dve.tensor_tensor(tok_item[:, ks, :], is_item[:, ks, :],
                                           c("token").rearrange("p (t o) -> p t o", o=1).broadcast_to([P, TILES, ITEMS]), ALU.mult))
                for n in range(0, NB, CHUNK):
                    dve.tensor_tensor(is_place[:, n:n + CHUNK, :], c("place").rearrange("p (o r) -> p o r", o=1).broadcast_to([P, CHUNK, P]),
                                      placef[:, n:n + CHUNK].rearrange("p (n o) -> p n o", o=1).broadcast_to([P, CHUNK, P]),
                                      ALU.is_equal).then_inc(placed, 1)
                link(dve.tensor_tensor(ge[:], c("item").rearrange("p (j o) -> p j o", o=1).broadcast_to([P, ITEMS, NE]),
                                       endt[:].rearrange("p (o e) -> p o e", o=1).broadcast_to([P, ITEMS, NE]), ALU.is_ge))
                link(dve.tensor_reduce(eidf[:], ge[:], AX.X, ALU.add))
                link(dve.tensor_scalar(eidf[:], eidf[:], float(NE - 1), None, ALU.min))
                dve.tensor_copy(eid[:], eidf[:])
                dve.wait_ge(inverted, 1)
                dve.tensor_copy(token[:], ps_t[:, 0:ITEMS])
                dve.wait_ge(gexp, 1)
                link(dve.tensor_scalar(zp1[:], ez[:], 1.0, None, ALU.add))
                link(dve.reciprocal(inv[:], zp1[:]))
                link(dve.tensor_scalar(wsel[:, 0, :], inv[:], gates[:, 2:3], None, ALU.mult))
                dve.tensor_tensor(wsel[:, 1, :], wsel[:, 0, :], ez[:], ALU.mult)


def run_experts(nc, c, w1h, w1l, w2h, w2l, eid, token, xn_dram, ys_dram, second):
    with ExitStack() as ctx:
        def sbuf(name, shape, dt=F32):
            return ctx.enter_context(nc.sbuf_tensor(f"moe_{name}", shape, dt))

        def sem(name):
            return ctx.enter_context(nc.semaphore(f"moe_{name}"))

        xg = sbuf("gathered_tile", [P, 2, C])
        xh, xl = sbuf("xt_hi", [P, 2, C], F32R), sbuf("xt_lo", [P, 2, C], F32R)
        sg, act_a = sbuf("silu_gate", [P, 2, FF]), sbuf("hidden", [P, 2, FF])
        ah, al = sbuf("at_hi", [P, 2, FF], F32R), sbuf("at_lo", [P, 2, FF], F32R)
        yo = sbuf("expert_tile", [P, 2, C])
        ps_x = ctx.enter_context(nc.psum_tensor("moe_ps_xt", [P, 2, 512], F32))
        ps_h = ctx.enter_context(nc.psum_tensor("moe_ps_h", [P, 2, 512], F32))
        ps_a = ctx.enter_context(nc.psum_tensor("moe_ps_at", [P, 2, 512], F32))
        ps_y = ctx.enter_context(nc.psum_tensor("moe_ps_y", [P, 2, 512], F32))
        x_in = [sem("x_in0"), sem("x_in1")]
        y_out = [sem("y_out0"), sem("y_out1")]
        (xt_ready, xhi, xlo, h_ready, silud, hidden, at_ready, ahi, alo, y_ready, y_copied) = (sem(n) for n in (
            "xt_ready", "xt_hi_done", "xt_lo_done", "h_ready", "silu_done", "hidden_done", "at_ready", "at_hi_done",
            "at_lo_done", "y_ready", "y_copied"))
        second_cleared, second_in, ctx_in, second_hi, ctx_hi = (sem(n) for n in (
            "second_cleared", "second_in", "second_ctx_in", "second_hi_done", "second_ctx_hi_done"))
        LOADED = 16 * 6
        ROWS2 = 4 * PAIRS
        LAG = 4

        def exists(j):
            return not isinstance(j, int) or 0 <= j < ITEMS

        def later(j, n=0):
            return not isinstance(j, int) or j > n

        def turns(eng, stages, first, last):
            def body(i, par):
                for stage, d in stages:
                    if exists(i + d) and (d != -LAG or not isinstance(i, int) or i + d < ROWS2):
                        stage(i + d, (par + d) % 2)
            staged(eng, body, first, 6, ITEMS - 4, last)

        with nc.Block() as block:
            @block.sync
            def _(sp):
                def store(j, p):
                    sp.wait_ge(y_copied, j + 1)
                    sp.dma_start(ys_dram[ds(j * P, P), :], yo[:, p, :]).then_inc(y_out[p], 16)
                second.load(sp, second_cleared, second_in, ctx_in)
                turns(sp, ((store, -1),), 0, ITEMS + 1)
                for p in range(2):
                    sp.wait_ge(y_out[p], 16 * ITEMS // 2)

            @block.gpsimd
            def _(pool):
                for j in range(ITEMS):
                    if j >= 2:
                        pool.wait_ge(xt_ready, j - 1)
                    pool.indirect_dma_start(xg[:, j % 2, :], None, xn_dram,
                                            bass.IndirectOffsetOnAxis(ap=token[:, j:j + 1], axis=0)).then_inc(x_in[j % 2], 16)
                    if j == 1:
                        for _, _, raw in (second.kq, second.vo):
                            pool.memset(raw[KP:P, 0:PAIRS, :], 0.0).then_inc(second_cleared, 1)
                    r = j - 2 * LAG
                    if r == 0:
                        pool.wait_ge(ctx_hi, 1)
                        pool.tensor_tensor(second.ctl[:], second.ctx_raw[:], second.cth[:].bitcast(F32), ALU.subtract)
                    if r >= 0:
                        hi, lo, raw = (second.kq, second.vo)[r % 2]
                        pool.wait_ge(second_hi, r + 1)
                        pool.tensor_tensor(lo[:, r // 2, :], raw[:, r // 2, :], hi[:, r // 2, :].bitcast(F32), ALU.subtract)

            @block.tensor
            def _(pe):
                expert_down = [pe.alloc_register(f"expert_down{q}") for q in range(2)]
                expert = [pe.alloc_register(f"expert{q}") for q in range(2)]

                def transpose_x(j, p):
                    pe.wait_ge(x_in[p], (j // 2 + 1) * 16)
                    for k in range(KC):
                        mm = nc.tensor.transpose(ps_x[:, p, k * P:(k + 1) * P], xg[:, p, k * P:(k + 1) * P], c("ident"))
                    mm.then_inc(xt_ready, 1)

                def load_expert(j, p):
                    if later(j, 1):
                        pe.reg_load(expert[p], eid[0:1, ds(j, 1)])

                def gate_up(j, p):
                    e, n = pe.snap(expert[p], min_val=0, max_val=NE - 1), 0
                    pe.reg_mov(expert_down[p], expert[p])
                    pe.wait_ge(xlo, j + 1)
                    for k in range(KC):
                        rh, rl = (w[:, ds(e * KC + k, 1), :].rearrange("p o f -> p (o f)") for w in (w1h, w1l))
                        for l, r in split3(xh[:, p, k * P:(k + 1) * P], xl[:, p, k * P:(k + 1) * P], rh, rl):
                            mm = nc.tensor.matmul(ps_h[:, p, :], l, r, start=(n == 0), stop=(n == KC * PASSES - 1))
                            n += 1
                    mm.then_inc(h_ready, 1)

                def transpose_a(j, p):
                    pe.wait_ge(hidden, j + 1)
                    for k in range(2):
                        mm = nc.tensor.transpose(ps_a[:, p, k * P:(k + 1) * P], act_a[:, p, k * P:(k + 1) * P], c("ident"))
                    mm.then_inc(at_ready, 1)

                def down(j, p):
                    e, n = pe.snap(expert_down[p], min_val=0, max_val=NE - 1), 0
                    pe.wait_ge(alo, j + 1)
                    if later(j, 1):
                        pe.wait_ge(y_copied, j - 1)
                    for k in range(2):
                        rh, rl = (w[:, ds(e * 2 + k, 1), :].rearrange("p o f -> p (o f)") for w in (w2h, w2l))
                        for l, r in split3(ah[:, p, k * P:(k + 1) * P], al[:, p, k * P:(k + 1) * P], rh, rl):
                            mm = nc.tensor.matmul(ps_y[:, p, 0:C], l, r, start=(n == 0), stop=(n == 2 * PASSES - 1))
                            n += 1
                    mm.then_inc(y_ready, 1)
                for j in range(2):
                    pe.reg_load(expert[j], eid[0:1, j:j + 1])
                turns(pe, ((down, -2), (transpose_a, -1), (gate_up, 0), (load_expert, 1), (transpose_x, 2)), -2, ITEMS + 2)

            @block.scalar
            def _(act):
                def x_high(j, p):
                    act.wait_ge(xt_ready, j + 1)
                    act.copy(xh[:, p, :], ps_x[:, p, 0:C]).then_inc(xhi, 1)

                def a_high(j, p):
                    act.wait_ge(at_ready, j + 1)
                    act.copy(ah[:, p, :], ps_a[:, p, 0:FF]).then_inc(ahi, 1)

                def silu(j, p):
                    act.wait_ge(h_ready, j + 1)
                    act.activation(sg[:, p, :], ps_h[:, p, 0:FF], ACT.Silu).then_inc(silud, 1)

                def y_copy(j, p):
                    act.wait_ge(y_ready, j + 1)
                    if later(j, 1):
                        act.wait_ge(y_out[p], (j // 2) * 16)
                    act.copy(yo[:, p, :], ps_y[:, p, 0:C]).then_inc(y_copied, 1)

                def second_high(r, p):
                    hi, _, raw = (second.kq, second.vo)[p]
                    if not isinstance(r, int) or r == 0:
                        act.wait_ge(second_in, LOADED)
                        act.wait_ge(second_cleared, 2)
                    if isinstance(r, int) and r == 0:
                        act.wait_ge(ctx_in, 16)
                        act.copy(second.cth[:], second.ctx_raw[:]).then_inc(ctx_hi, 1)
                    act.copy(hi[:, ds(r // 2, 1), :], raw[:, ds(r // 2, 1), :]).then_inc(second_hi, 1)
                turns(act, ((y_copy, -2), (a_high, -1), (second_high, -LAG), (silu, 0), (x_high, 2)), -2, ITEMS + 2)

            @block.vector
            def _(dve):
                def x_low(j, p):
                    dve.wait_ge(xhi, j + 1)
                    dve.tensor_tensor(xl[:, p, :], ps_x[:, p, 0:C], xh[:, p, :].bitcast(F32), ALU.subtract).then_inc(xlo, 1)

                def a_low(j, p):
                    dve.wait_ge(ahi, j + 1)
                    dve.tensor_tensor(al[:, p, :], ps_a[:, p, 0:FF], ah[:, p, :].bitcast(F32), ALU.subtract).then_inc(alo, 1)

                def times_up(j, p):
                    dve.wait_ge(silud, j + 1)
                    dve.tensor_tensor(act_a[:, p, :], ps_h[:, p, FF:2 * FF], sg[:, p, :], ALU.mult).then_inc(hidden, 1)
                turns(dve, ((a_low, -1), (times_up, 0), (x_low, 2)), -2, ITEMS + 1)


def attention1(nc, c, second, ys_dram, xres, gates, mhalf, slots, wsel):
    with ExitStack() as keep:
        def sbuf(name, shape, dt=F32):
            return keep.enter_context(nc.sbuf_tensor(f"a1_{name}", shape, dt))

        bos = sbuf("bo_scaled", [P, C])
        ah, al = (sbuf(f"a_{s}", [P, KC, B, HK], F32R) for s in ("hi", "lo"))
        fold(nc, c, second, second.kq, None, ys_dram, xres, gates, slots, wsel, ah, al, bos)
        second.kq_memory.close()
        bh, bl = (sbuf(f"b_{s}", [P, B, PAIRS, C], F32R) for s in ("hi", "lo"))
        fold(nc, c, second, None, second.vo, ys_dram, xres, gates, slots, wsel, bh, bl, bos)
        second.vo_memory.close()
        attend1(nc, c, xres, mhalf, ah, al, bh, bl, bos)


class SecondWeights:

    def __init__(self, nc, ctxt, wqt1, wk1, wv1, wo1):
        self.nc, self.sources = nc, (ctxt, wqt1, wk1, wv1, wo1)
        self.kq_memory, self.vo_memory = ExitStack(), ExitStack()

    def place(self):
        def sbuf(stack, name, shape, dt=F32R):
            return stack.enter_context(self.nc.sbuf_tensor(f"second_{name}", shape, dt, side="right"))

        def split(stack, name, shape):
            hi, lo = (sbuf(stack, f"{name}_{h}", shape) for h in ("hi", "lo"))
            raw = self.nc.alloc_sbuf_tensor_at(f"second_{name}_raw", shape, F32, offset=self.nc.sbuf_top)
            return hi, lo, raw
        self.cth, self.ctl, self.ctx_raw = split(self.vo_memory, "ctx", [KP, 2, B * KV])
        self.vo = split(self.vo_memory, "vo", [P, 2 * PAIRS, C])
        self.kq = split(self.kq_memory, "kq", [P, 2 * PAIRS, C])

    def load(self, eng, cleared, loaded, loaded_ctx):
        ctxt, wqt1, wk1, wv1, wo1 = self.sources
        eng.dma_start(self.ctx_raw[:], ctxt.rearrange("(k p) n -> p k n", p=KP)).then_inc(loaded_ctx, 16)
        eng.wait_ge(cleared, 2)
        for pair, narrow, wide in ((self.kq, wk1, wqt1), (self.vo, wv1, wo1)):
            raw = pair[2]
            for k in range(2):
                eng.dma_start(raw[0:KP, 0:PAIRS, k * P:(k + 1) * P],
                              narrow[k * KP:(k + 1) * KP, :].rearrange("p (j n) -> p j n", j=PAIRS)).then_inc(loaded, 16)
            eng.dma_start(raw[:, PAIRS:2 * PAIRS, :], wide.rearrange("(j p) n -> p j n", p=P)).then_inc(loaded, 16)


def fold(nc, c, second, kq, vo, ys_dram, xres, gates, slots, wsel, fh, fl, bos):
    keys = kq is not None
    wh, wl, _ = kq if keys else vo
    tag = "foldk" if keys else "foldv"
    with ExitStack() as ctx:
        def sbuf(name, shape, dt=F32):
            return ctx.enter_context(nc.sbuf_tensor(f"{tag}_{name}", shape, dt))

        def sem(name):
            return ctx.enter_context(nc.semaphore(f"{tag}_{name}"))

        DEPTH = 3
        tiles = range(0, TILES // 2) if keys else range(TILES // 2, TILES)
        first = tiles[0]
        yg = sbuf("gathered", [P, DEPTH, TOPK, C])
        th, tl = sbuf("projected_hi", [P, 2, B * P], F32R), sbuf("projected_lo", [P, 2, B * P], F32R)
        ps_kv = ctx.enter_context(nc.psum_tensor(f"{tag}_ps_kv", [P, 2, 512], F32))
        ps_f = ctx.enter_context(nc.psum_tensor(f"{tag}_ps_f", [P, 2, 2, 512], F32))
        g_in = [sem(f"gathered{n}") for n in range(DEPTH)]
        (cleared, kv_ready, kvhi, kvlo, f_ready, fhi, flo, comb) = (sem(n) for n in (
            "cleared", "kv_ready", "kv_hi_done", "kv_lo_done", "f_ready", "f_hi_done", "f_lo_done", "combined"))

        def projected(a, p, h):
            rows = slice(h * D1, (h + 1) * D1)
            return (ps_kv[rows, p, 0:B * KV].rearrange("p (b k) -> p b k", b=B),
                    a[rows, p, :].rearrange("p (b h k) -> p b h k", b=B, h=2)[:, :, h, :])

        def folded(a, j, m):
            ps = ps_f[:, j % 2, m, :]
            if keys:
                return ps.rearrange("p (b n) -> p b n", b=B), a[:, m, :, j * P:(j + 1) * P]
            return ps.rearrange("p (b c) -> p b c", b=2), a[:, 2 * m:2 * m + 2, j, :]

        with nc.Block() as block:
            @block.gpsimd
            def _(pool):
                for i, t in enumerate(tiles):
                    if i >= DEPTH:
                        pool.wait_ge(comb, TOPK * (i - DEPTH + 1))
                    for n in range(TOPK):
                        pool.indirect_dma_start(yg[:, i % DEPTH, n, :], None, ys_dram,
                                                bass.IndirectOffsetOnAxis(ap=slots[:, n, t:t + 1], axis=0)).then_inc(g_in[i % DEPTH], 16)

            @block.scalar
            def _(act):
                def projected_high(j):
                    if j == 0:
                        act.wait_ge(cleared, 2)
                    act.wait_ge(kv_ready, j + 1)
                    if j >= 2:
                        act.wait_ge(f_ready, 2 * (j - 1))
                    for h in range(2):
                        src, dst = projected(th, j % 2, h)
                        act.activation(dst, src, ACT.Copy, scale=D1 ** -0.5 if keys else 1.0).then_inc(kvhi, 1)

                def folded_high(j):
                    for m in range(2):
                        act.wait_ge(f_ready, 2 * j + m + 1)
                        src, dst = folded(fh, j, m)
                        if keys:
                            act.copy(dst, src).then_inc(fhi, 1)
                        else:
                            act.activation(dst, src, ACT.Identity, scale=gates[:, 1:2]).then_inc(fhi, 1)
                projected_high(0)
                for j in range(PAIRS):
                    if j + 1 < PAIRS:
                        projected_high(j + 1)
                    folded_high(j)

            @block.vector
            def _(dve):
                dve.memset(th[:].bitcast(F32), 0.0).then_inc(cleared, 1)
                dve.memset(tl[:].bitcast(F32), 0.0).then_inc(cleared, 1)
                if keys:
                    dve.tensor_scalar(bos[:], c("bout1"), gates[:, 1:2], None, ALU.mult)
                dve.wait_ge(cleared, 2)

                def projected_low(j):
                    for h in range(2):
                        dve.wait_ge(kvhi, 2 * j + h + 1)
                        src, dst = projected(tl, j % 2, h)
                        _, hi = projected(th, j % 2, h)
                        dve.scalar_tensor_tensor(out=dst, in0=src, scalar=D1 ** -0.5 if keys else 1.0, in1=hi.bitcast(F32),
                                                 op0=ALU.mult, op1=ALU.subtract).then_inc(kvlo, 1)

                def folded_low(j):
                    for m in range(2):
                        dve.wait_ge(fhi, 2 * j + m + 1)
                        src, dst = folded(fl, j, m)
                        _, hi = folded(fh, j, m)
                        if keys:
                            dve.tensor_tensor(dst, src, hi.bitcast(F32), ALU.subtract).then_inc(flo, 1)
                        else:
                            dve.scalar_tensor_tensor(out=dst, in0=src, scalar=gates[:, 1:2], in1=hi.bitcast(F32),
                                                     op0=ALU.mult, op1=ALU.subtract).then_inc(flo, 1)

                def combine(i, n):
                    t = first + i
                    dve.wait_ge(g_in[i % DEPTH], 16 * TOPK * (i // DEPTH + 1))
                    if n:
                        dve.wait_ge(comb, TOPK * i + 1)
                    dve.scalar_tensor_tensor(out=xres[:, t, :], in0=yg[:, i % DEPTH, n, :], scalar=wsel[:, n, t:t + 1],
                                             in1=xres[:, t, :], op0=ALU.mult, op1=ALU.add).then_inc(comb, 1)

                projected_low(0)
                for j in range(PAIRS):
                    if j + 1 < PAIRS:
                        projected_low(j + 1)
                    combine(j, 0)
                    folded_low(j)
                    combine(j, 1)

            @block.tensor
            def _(pe):
                def project(j):
                    if j >= 2:
                        pe.wait_ge(kvlo, 2 * (j - 1))
                    q = 0
                    for k in range(2):
                        ks = slice(k * P, (k + 1) * P)
                        for l, r in split3(wh[0:KP, j, ks], wl[0:KP, j, ks], second.cth[:, k, :], second.ctl[:, k, :]):
                            mm = nc.tensor.matmul(ps_kv[:, j % 2, 0:B * KV], l, r, start=(q == 0), stop=(q == 2 * PASSES - 1))
                            q += 1
                    mm.then_inc(kv_ready, 1)

                def banks_free(j):
                    if j >= 2:
                        pe.wait_ge(flo, 2 * (j - 1))

                def fold_keys(j):
                    p, row = j % 2, PAIRS + j
                    pe.wait_ge(kvlo, 2 * (j + 1))
                    banks_free(j)
                    for m in range(KC):
                        ms = slice(m * P, (m + 1) * P)
                        for n, (l, r) in enumerate(split3(wh[:, row, ms], wl[:, row, ms], th[:, p, :], tl[:, p, :])):
                            mm = nc.tensor.matmul(ps_f[:, p, m, :], l, r, start=(n == 0), stop=(n == PASSES - 1))
                        mm.then_inc(f_ready, 1)

                def fold_values(j):
                    p, row = j % 2, PAIRS + j
                    pe.wait_ge(kvlo, 2 * (j + 1))
                    banks_free(j)
                    for b in range(B):
                        bs = slice(b * P, (b + 1) * P)
                        for n, (l, r) in enumerate(split3(th[:, p, bs], tl[:, p, bs], wh[:, row, :], wl[:, row, :])):
                            mm = nc.tensor.matmul(ps_f[:, p, b // 2, (b % 2) * C:(b % 2 + 1) * C], l, r, start=(n == 0), stop=(n == PASSES - 1))
                        if b % 2:
                            mm.then_inc(f_ready, 1)

                project(0)
                project(1)
                for j in range(PAIRS):
                    fold_keys(j) if keys else fold_values(j)
                    if j + 2 < PAIRS:
                        project(j + 2)


def attend1(nc, c, xres, mhalf, ah, al, bh, bl, bos):
    with ExitStack() as ctx:
        def sbuf(name, shape, dt=F32):
            return ctx.enter_context(nc.sbuf_tensor(f"att1_{name}", shape, dt))

        def sem(name):
            return ctx.enter_context(nc.semaphore(f"att1_{name}"))

        def bank(name, *n):
            return ctx.enter_context(nc.psum_tensor(f"att1_{name}", [P, *n, 512], F32))

        st, mv = sbuf("ln_stats", [P, 2, 6]), sbuf("ln_mean_var", [P, 2, 2])
        ve, rs = sbuf("ln_var_eps", [P, 2]), sbuf("ln_rstd", [P, 2])
        xn = sbuf("xn", [P, 2, C])
        xh, xl = sbuf("xt_hi", [P, 2, C], F32R), sbuf("xt_lo", [P, 2, C], F32R)
        sc = sbuf("scores", [P, 2, HK])
        mx, sm, rc = (sbuf(n, [P, 2, H]) for n in ("score_max", "exp_sum", "recip"))
        ph, pl = sbuf("pt_hi", [P, HK], F32R), sbuf("pt_lo", [P, HK], F32R)
        ps_s, ps_p = bank("ps_scores", 2, 2), bank("ps_pt", 2)
        ps_x, ps_y = bank("ps_xt", 1), bank("ps_y", 1)
        (xt_ready, s_ready, pt_ready, y_ready, xhi, phi, expd, lnve, lnrs, lndone, xlo, maxd, cent, sumd, recd, plo,
         resd, xbias, normd, copied) = (sem(n) for n in (
             "xt_ready", "scores_ready", "pt_ready", "y_ready", "xt_hi_done", "pt_hi_done", "exp_done", "ln_ve_done", "ln_rstd_done", "ln_done", "xt_lo_done", "max_done", "centred", "sum_done", "recip_done",
             "pt_lo_done", "residual_done", "bias_added", "probs_normed", "scores_copied"))

        def wide(a):
            return a.rearrange("p (h o) -> p h o", o=1).broadcast_to([P, H, KV])

        def heads(a):
            return a.rearrange("p (h k) -> p h k", k=KV)

        def turns(eng, stages, first, last):
            def body(i, par):
                for stage, d in stages:
                    if live(i + d):
                        stage(i + d, (par + d) % 2)
            staged(eng, body, first, 6, 12, last)

        with nc.Block() as block:
            @block.tensor
            def _(pe):
                def transpose_probs(t, p):
                    pe.wait_ge(normd, t + 1)
                    for j in range(PAIRS):
                        mm = nc.tensor.transpose(ps_p[:, j // 4, (j % 4) * P:(j % 4 + 1) * P], sc[:, p, j * P:(j + 1) * P], c("ident"))
                        if j % 4 == 3:
                            mm.then_inc(pt_ready, 1)

                def scores(t, p):
                    pe.wait_ge(xlo, t + 1)
                    if not isinstance(t, int) or t > 1:
                        pe.wait_ge(copied, t - 1)
                    for half in range(2):
                        n = 0
                        for k in range(KC):
                            rh, rl = (w[:, k, ds(t // TPB, 1), half * 512:(half + 1) * 512].rearrange("p o n -> p (o n)") for w in (ah, al))
                            for l, r in split3(xh[:, p, k * P:(k + 1) * P], xl[:, p, k * P:(k + 1) * P], rh, rl):
                                mm = nc.tensor.matmul(ps_s[:, p, half, :], l, r, start=(n == 0), stop=(n == KC * PASSES - 1))
                                n += 1
                    mm.then_inc(s_ready, 1)

                def transpose_x(t, p):
                    pe.wait_ge(lndone, t + 1)
                    for k in range(KC):
                        mm = nc.tensor.transpose(ps_x[:, 0, k * P:(k + 1) * P], xn[:, p, k * P:(k + 1) * P], c("ident"))
                    mm.then_inc(xt_ready, 1)

                def outputs(t, p):
                    pe.wait_ge(plo, 2 * t + 2)
                    if not isinstance(t, int) or t > 0:
                        pe.wait_ge(resd, t)
                    n = 0
                    for j in range(PAIRS):
                        rh, rl = (w[:, ds(t // TPB, 1), j, :].rearrange("p o n -> p (o n)") for w in (bh, bl))
                        for l, r in split3(ph[:, j * P:(j + 1) * P], pl[:, j * P:(j + 1) * P], rh, rl):
                            mm = nc.tensor.matmul(ps_y[:, 0, 0:C], l, r, start=(n == 0), stop=(n == PAIRS * PASSES - 1))
                            n += 1
                    mm.then_inc(y_ready, 1)
                turns(pe, ((transpose_probs, -2), (scores, 0), (outputs, -2), (transpose_x, 2)), -2, TILES + 2)

            @block.scalar
            def _(act):
                def copy_scores(t, p):
                    act.wait_ge(s_ready, t + 1)
                    if not isinstance(t, int) or t > 1:
                        act.wait_ge(pt_ready, 2 * t - 2)
                    act.copy(sc[:, p, :].rearrange("p (a n) -> p a n", a=2), ps_s[:, p]).then_inc(copied, 1)

                def exponential(t, p):
                    act.wait_ge(cent, t + 1)
                    act.activation(sc[:, p, :], sc[:, p, :], ACT.Exp).then_inc(expd, 1)

                def probs_high(t, p):
                    for half in range(2):
                        act.wait_ge(pt_ready, 2 * t + half + 1)
                        if half == 0 and (not isinstance(t, int) or t > 0):
                            act.wait_ge(y_ready, t)
                        act.copy(ph[:, half * 512:(half + 1) * 512], ps_p[:, half, :]).then_inc(phi, 1)

                def x_high(t, p):
                    act.wait_ge(xt_ready, t + 1)
                    act.copy(xh[:, p, :], ps_x[:, 0, 0:C]).then_inc(xhi, 1)
                turns(act, ((x_high, 1), (probs_high, -2), (exponential, -1), (copy_scores, 0)), -1, TILES + 2)

            @block.gpsimd
            def _(pool):
                def rstd(t, p):
                    pool.wait_ge(lnve, t + 1)
                    pool.tensor_tensor(rs[:, p:p + 1], ve[:, p:p + 1], mhalf[:], ALU.pow).then_inc(lnrs, 1)

                def normalise(t, p):
                    pool.wait_ge(recd, t + 1)
                    pool.tensor_tensor(heads(sc[:, p, :]), heads(sc[:, p, :]), wide(rc[:, p, :]), ALU.mult).then_inc(normd, 1)

                def centre(t, p):
                    pool.wait_ge(maxd, t + 1)
                    pool.tensor_tensor(heads(sc[:, p, :]), heads(sc[:, p, :]), wide(mx[:, p, :]), ALU.subtract).then_inc(cent, 1)

                def bias(t, p):
                    pool.wait_ge(s_ready, t + 1)
                    pool.wait_ge(lnrs, 1)
                    xt = xres[:, ds(t, 1), :].rearrange("p o c -> p (o c)")
                    pool.tensor_tensor(xt, xt, bos[:], ALU.add).then_inc(xbias, 1)
                turns(pool, ((normalise, -1), (centre, 0), (rstd, 3), (bias, 0)), -3, TILES + 1)

            @block.vector
            def _(dve):
                def tile_of(t):
                    return xres[:, ds(t, 1), :].rearrange("p o c -> p (o c)")

                def stats(t, p):
                    dve.bn_stats(st[:, p, :], tile_of(t))
                    dve.drain()
                    dve.bn_aggr(mv[:, p, :], st[:, p, :])
                    dve.drain()
                    dve.tensor_scalar(ve[:, p:p + 1], mv[:, p, 1:2], EPS, None, ALU.add).then_inc(lnve, 1)

                def layer_norm(t, p):
                    dve.wait_ge(lnrs, t + 1)
                    dve.tensor_scalar(xn[:, p, :], tile_of(t), mv[:, p, 0:1], rs[:, p:p + 1], ALU.subtract, ALU.mult).then_inc(lndone, 1)

                def x_low(t, p):
                    dve.wait_ge(xhi, t + 1)
                    dve.tensor_tensor(xl[:, p, :], ps_x[:, 0, 0:C], xh[:, p, :].bitcast(F32), ALU.subtract).then_inc(xlo, 1)

                def sums(t, p):
                    dve.wait_ge(expd, t + 1)
                    dve.tensor_reduce(sm[:, p, :], heads(sc[:, p, :]), AX.X, ALU.add).then_inc(sumd, 1)
                    dve.wait_ge(sumd, t + 1)
                    dve.reciprocal(rc[:, p, :], sm[:, p, :]).then_inc(recd, 1)

                def probs_low(t, p):
                    for half in range(2):
                        hs = slice(half * 512, (half + 1) * 512)
                        dve.wait_ge(phi, 2 * t + half + 1)
                        dve.tensor_tensor(pl[:, hs], ps_p[:, half, :], ph[:, hs].bitcast(F32), ALU.subtract).then_inc(plo, 1)

                def maxima(t, p):
                    dve.wait_ge(copied, t + 1)
                    dve.tensor_reduce(mx[:, p, :], heads(sc[:, p, :]), AX.X, ALU.max).then_inc(maxd, 1)

                def residual(t, p):
                    dve.wait_ge(y_ready, t + 1)
                    dve.wait_ge(xbias, t + 1)
                    dve.tensor_tensor(tile_of(t), ps_y[:, 0, 0:C], tile_of(t), ALU.add).then_inc(resd, 1)
                turns(dve, ((residual, -3), (x_low, 1), (probs_low, -2), (layer_norm, 2), (sums, -1), (maxima, 0), (stats, 3)), -3, TILES + 3)


def mlp1(nc, c, fwin, fwout, xres, gates, mhalf, out):
    with ExitStack() as ctx:
        def sbuf(name, shape, dt=F32):
            return ctx.enter_context(nc.sbuf_tensor(f"mlp_{name}", shape, dt))

        def sem(name):
            return ctx.enter_context(nc.semaphore(f"mlp_{name}"))

        UN = INNER // 2
        UP = 2
        UV = UN - UP
        PSTEPS = 2 * UP - 1
        HALF = S // 2
        st, mv = sbuf("ln_stats", [P, TILES, 6]), sbuf("ln_mean_var", [P, TILES, 2])
        ve, rs, shift = sbuf("ln_var_eps", [P, TILES]), sbuf("ln_rstd", [P, TILES]), sbuf("ln_shift", [P, TILES])
        xn = sbuf("xn", [P, 2, TPB, C])
        xh, xl = sbuf("xt_hi", [P, 2, KC, S], F32R), sbuf("xt_lo", [P, 2, KC, S], F32R)
        wi, wo = ([sbuf(f"{n}_raw", [P, KC, w]), sbuf(f"{n}_hi", [P, KC, w], F32R), sbuf(f"{n}_lo", [P, KC, w], F32R)]
                  for n, w in (("win", P), ("wout", P)))
        wos, bos, ub, t1 = sbuf("wout_gated", [P, KC, P]), sbuf("bout_gated", [P, C]), sbuf("unit_bias", [P, UN]), sbuf("w1_bin", [P, UN])
        hb = sbuf("units", [P, 2, UN, S])
        g, gp = sbuf("g", [P, 2, S]), sbuf("g_of_gpsimd", [P, 2, S])
        gh, gl = sbuf("g_hi", [P, 2, S], F32R), sbuf("g_lo", [P, 2, S], F32R)
        ps_x = ctx.enter_context(nc.psum_tensor("mlp_ps_xt", [P, KC, 512], F32))
        ps_s = ctx.enter_context(nc.psum_tensor("mlp_ps_s", [P, 2, 512], F32))
        ps_y = ctx.enter_context(nc.psum_tensor("mlp_ps_y", [P, 2, 512], F32))
        w_in, gated, whi, wlo, ubias = sem("w_in"), sem("wout_gated_done"), sem("w_hi_done"), sem("w_lo_done"), sem("unit_bias_done")
        (lnst, lnmv, lnve, lnrs, lndone, xt_ready, xhi, xlo, s_ready, relud, acc, ghi, glo, y_ready, resd, xbias, stored) = (sem(n) for n in (
            "ln_stats_done", "ln_mv_done", "ln_ve_done", "ln_rstd_done", "ln_done", "xt_ready", "xt_hi_done", "xt_lo_done",
            "s_ready", "relu_done", "accumulated", "g_hi_done", "g_lo_done", "y_ready", "residual_done", "bias_added", "stored"))
        pacc, summed, lnshift = sem("accumulated_on_gpsimd"), sem("g_summed"), sem("ln_shift_done")

        with nc.Block() as block:
            @block.sync
            def _(sp):
                sp.dma_start(wi[0][:], fwin.rearrange("(k p) n -> p k n", p=P)).then_inc(w_in, 16)
                sp.dma_start(wo[0][:], fwout.rearrange("p (k n) -> p k n", k=KC)).then_inc(w_in, 16)
                for b in range(B):
                    sp.wait_ge(resd, 2 * (b + 1))
                    sp.dma_start(out[b].rearrange("(t p) c -> p t c", p=P), xres[:, b * TPB:(b + 1) * TPB, :]).then_inc(stored, 16)
                sp.wait_ge(stored, 16 * B)

            @block.gpsimd
            def _(pool):
                pool.wait_ge(gated, 3)

                def rstd(b):
                    bt = slice(b * TPB, (b + 1) * TPB)
                    pool.wait_ge(lnve, b + 1)
                    pool.tensor_tensor(rs[:, bt], ve[:, bt], mhalf[:].broadcast_to([P, TPB]), ALU.pow).then_inc(lnrs, 1)

                def bias(b):
                    bt = slice(b * TPB, (b + 1) * TPB)
                    pool.wait_ge(lndone, TPB * (b + 1))
                    pool.tensor_tensor(xres[:, bt, :], xres[:, bt, :], bos[:].rearrange("p (o c) -> p o c", o=1).broadcast_to([P, TPB, C]),
                                       ALU.add).then_inc(xbias, 1)

                def accumulate(b):
                    p = b % 2
                    for n in range(UP):
                        pool.wait_ge(relud, b * UN + n + 1)
                        if n == 0 and b >= 2:
                            pool.wait_ge(summed, 2 * (b - 1))
                        dst = gp[:, p, :] if n == 0 else hb[:, p, n, :]
                        pool.tensor_tensor(dst, hb[:, p, n, :], c("fw2")[:, n:n + 1].broadcast_to([P, S]), ALU.mult).then_inc(pacc, 1)
                        if n:
                            pool.wait_ge(pacc, b * PSTEPS + 2 * n)
                            pool.tensor_tensor(gp[:, p, :], gp[:, p, :], hb[:, p, n, :], ALU.add).then_inc(pacc, 1)
                for b in range(3):
                    rstd(b)
                for b in range(B):
                    bias(b)
                    accumulate(b)
                    if b + 3 < B:
                        rstd(b + 3)

            @block.scalar
            def _(act):
                act.wait_ge(w_in, 32)
                act.copy(wi[1][:], wi[0][:]).then_inc(whi, 1)
                act.wait_ge(gated, 3)
                act.copy(wo[1][:], wos[:]).then_inc(whi, 1)

                def x_high(b):
                    act.wait_ge(xt_ready, b + 1)
                    if b >= 2:
                        act.wait_ge(s_ready, b - 1)
                    act.copy(xh[:, b % 2], ps_x[:]).then_inc(xhi, 1)

                def layer_norm(b):
                    act.wait_ge(lnshift, b + 1)
                    if b >= 2:
                        act.wait_ge(xt_ready, b - 1)
                    for u in range(TPB):
                        t = b * TPB + u
                        act.activation(xn[:, b % 2, u, :], xres[:, t, :], ACT.Identity, bias=shift[:, t:t + 1], scale=rs[:, t:t + 1]).then_inc(lndone, 1)

                def g_high(b):
                    act.wait_ge(summed, 2 * (b + 1))
                    act.copy(gh[:, b % 2, :], g[:, b % 2, :]).then_inc(ghi, 1)

                layer_norm(0)
                x_high(0)
                layer_norm(1)
                act.wait_ge(ubias, 2)
                for b in range(B):
                    act.wait_ge(s_ready, b + 1)
                    if b >= 2:
                        act.wait_ge(acc, 2 * UV * (b - 1))
                        act.wait_ge(pacc, PSTEPS * (b - 1))
                    for u in range(UN):
                        act.activation(hb[:, b % 2, u, :], ps_s[:, b % 2, :], ACT.Relu, bias=ub[:, u:u + 1],
                                       scale=c("fw1")[:, u:u + 1]).then_inc(relud, 1)
                        if u == 1 and b >= 1:
                            g_high(b - 1)
                        if u == 3 and b + 1 < B:
                            x_high(b + 1)
                    if b + 2 < B:
                        layer_norm(b + 2)
                g_high(B - 1)

            @block.vector
            def _(dve):
                dve.tensor_scalar(bos[:], c("fbout"), gates[:, 3:4], None, ALU.mult).then_inc(gated, 1)
                dve.tensor_scalar(t1[:], c("fw1"), c("fbin"), None, ALU.mult).then_inc(ubias, 1)
                dve.wait_ge(ubias, 1)
                dve.tensor_tensor(ub[:], t1[:], c("fb1"), ALU.add).then_inc(ubias, 1)
                dve.wait_ge(w_in, 32)
                dve.tensor_scalar(wos[:], wo[0][:], gates[:, 3:4], None, ALU.mult).then_inc(gated, 2)
                dve.wait_ge(whi, 1)
                dve.tensor_tensor(wi[2][:], wi[0][:], wi[1][:].bitcast(F32), ALU.subtract).then_inc(wlo, 1)
                dve.wait_ge(whi, 2)
                dve.tensor_tensor(wo[2][:], wos[:], wo[1][:].bitcast(F32), ALU.subtract).then_inc(wlo, 1)

                def stats(b):
                    for t in range(b * TPB, (b + 1) * TPB):
                        dve.bn_stats(st[:, t, :], xres[:, t, :]).then_inc(lnst, 1)
                    for t in range(b * TPB, (b + 1) * TPB):
                        dve.wait_ge(lnst, t + 1)
                        dve.bn_aggr(mv[:, t, :], st[:, t, :]).then_inc(lnmv, 1)
                    bt = slice(b * TPB, (b + 1) * TPB)
                    dve.wait_ge(lnmv, TPB * (b + 1))
                    dve.tensor_scalar(ve[:, bt], mv[:, bt, 1], EPS, None, ALU.add).then_inc(lnve, 1)

                def shifts(b):
                    bt = slice(b * TPB, (b + 1) * TPB)
                    dve.wait_ge(lnrs, b + 1)
                    dve.scalar_tensor_tensor(out=shift[:, bt], in0=mv[:, bt, 0], scalar=-1.0, in1=rs[:, bt],
                                             op0=ALU.mult, op1=ALU.mult).then_inc(lnshift, 1)

                def x_low(b):
                    dve.wait_ge(xhi, b + 1)
                    if b >= 2:
                        dve.wait_ge(s_ready, b - 1)
                    dve.tensor_tensor(xl[:, b % 2], ps_x[:], xh[:, b % 2].bitcast(F32), ALU.subtract).then_inc(xlo, 1)

                def accumulate(b, units):
                    p = b % 2
                    for u in units:
                        dve.wait_ge(relud, b * UN + u + 1)
                        for h in range(2):
                            hs = slice(h * HALF, (h + 1) * HALF)
                            if u == UP:
                                if b >= 2:
                                    dve.wait_ge(glo, b - 1)
                                dve.tensor_scalar(g[:, p, hs], hb[:, p, u, hs], c("fw2")[:, u:u + 1], c("fb2"), ALU.mult, ALU.add).then_inc(acc, 1)
                            else:
                                dve.wait_ge(acc, 2 * (b * UV + u - UP - 1) + h + 1)
                                dve.scalar_tensor_tensor(out=g[:, p, hs], in0=hb[:, p, u, hs], scalar=c("fw2")[:, u:u + 1], in1=g[:, p, hs],
                                                         op0=ALU.mult, op1=ALU.add).then_inc(acc, 1)

                def sum_parts(b):
                    p = b % 2
                    dve.wait_ge(pacc, PSTEPS * (b + 1))
                    for h in range(2):
                        hs = slice(h * HALF, (h + 1) * HALF)
                        dve.wait_ge(acc, 2 * UV * (b + 1) - 1 + h)
                        dve.tensor_tensor(g[:, p, hs], g[:, p, hs], gp[:, p, hs], ALU.add).then_inc(summed, 1)

                def g_low(b):
                    dve.wait_ge(ghi, b + 1)
                    dve.tensor_tensor(gl[:, b % 2, :], g[:, b % 2, :], gh[:, b % 2, :].bitcast(F32), ALU.subtract).then_inc(glo, 1)

                def residual(b):
                    dve.wait_ge(xbias, b + 1)
                    for q in range(2):
                        dve.wait_ge(y_ready, 2 * b + q + 1)
                        xt = xres[:, b * TPB + 2 * q:b * TPB + 2 * q + 2, :]
                        dve.tensor_tensor(xt, ps_y[:, q, :].rearrange("p (t c) -> p t c", t=2), xt, ALU.add).then_inc(resd, 1)

                stats(0)
                stats(1)
                shifts(0)
                stats(2)
                shifts(1)
                x_low(0)
                shifts(2)
                for b in range(B):
                    if b >= 1:
                        g_low(b - 1)
                    accumulate(b, range(UP, UP + 1))
                    if b + 1 < B:
                        x_low(b + 1)
                    accumulate(b, range(UP + 1, UN))
                    if b + 3 < B:
                        stats(b + 3)
                    if b >= 1:
                        residual(b - 1)
                    sum_parts(b)
                    if b + 3 < B:
                        shifts(b + 3)
                g_low(B - 1)
                residual(B - 1)

            @block.tensor
            def _(pe):
                def transpose_x(b):
                    pe.wait_ge(lndone, TPB * (b + 1))
                    for u in range(TPB):
                        for k in range(KC):
                            mm = nc.tensor.transpose(ps_x[:, k, u * P:(u + 1) * P], xn[:, b % 2, u, k * P:(k + 1) * P], c("ident"))
                    mm.then_inc(xt_ready, 1)

                def sums(b):
                    pe.wait_ge(xlo, b + 1)
                    if b >= 2:
                        pe.wait_ge(relud, UN * (b - 1))
                    n = 0
                    for k in range(KC):
                        for l, r in split3(wi[1][:, k, :], wi[2][:, k, :], xh[:, b % 2, k, :], xl[:, b % 2, k, :]):
                            mm = nc.tensor.matmul(ps_s[:, b % 2, :], l, r, start=(n == 0), stop=(n == KC * PASSES - 1))
                            n += 1
                    mm.then_inc(s_ready, 1)

                def outputs(b):
                    pe.wait_ge(glo, b + 1)
                    if b >= 1:
                        pe.wait_ge(resd, 2 * b)
                    for u in range(TPB):
                        us = slice(u * P, (u + 1) * P)
                        rh, rl = (w[:].rearrange("p k n -> p (k n)") for w in wo[1:])
                        for n, (l, r) in enumerate(split3(gh[:, b % 2, us], gl[:, b % 2, us], rh, rl)):
                            mm = nc.tensor.matmul(ps_y[:, u // 2, (u % 2) * C:(u % 2 + 1) * C], l, r, start=(n == 0), stop=(n == PASSES - 1))
                        if u % 2:
                            mm.then_inc(y_ready, 1)

                transpose_x(0)
                pe.wait_ge(wlo, 2)
                sums(0)
                transpose_x(1)
                for b in range(B):
                    if b >= 1:
                        outputs(b - 1)
                    if b + 1 < B:
                        sums(b + 1)
                    if b + 2 < B:
                        transpose_x(b + 2)
                outputs(B - 1)


def packed_rows(i):
    f = np.float32
    p = np.arange(P)

    def rep(a):
        return np.broadcast_to(np.reshape(a, (1, -1)), (P, np.size(a)))

    def cols(a):
        return np.reshape(a, (-1, P)).T

    def halves(a):
        return np.concatenate([a[:, :INNER // 2], a[:, INNER // 2:]], axis=0)

    parts = {
        "ident": np.eye(P, dtype=f), "tri": np.triu(np.ones((P, P), f), 1),
        "mask": (p[:, None] // D0 == np.arange(P // D0)[None, :]).astype(f),
        "rev": rep(np.arange(NE, 0, -1, dtype=f)), "item": rep(np.arange(ITEMS, dtype=f)), "ones": np.ones((P, P), f),
        "bq": cols(i["L0_xattn_bq"]), "bk": cols(i["L0_xattn_bk"]), "bv": rep(i["L0_xattn_bv"]), "bo": rep(i["L0_xattn_bo"]),
        "bg": rep(i["L0_ffn_bg"]), "gx": rep(i["g_xattn"]), "gf": rep(i["g_ffn"]), "bout1": rep(i["L1_xattn_b_out"]),
        "fbin": np.reshape(np.concatenate([i["L1_ffn_bin_"]] * 2), (P, 1)),
        "fw1": halves(i["L1_ffn_W1"]), "fb1": halves(i["L1_ffn_b1"]), "fw2": halves(i["L1_ffn_W2"]),
        "fb2": np.reshape(np.concatenate([i["L1_ffn_b2"], np.zeros(M1, f)]), (P, 1)), "fbout": rep(i["L1_ffn_bout"]),
        "scan": rep((np.arange(P) % TILES != 0).astype(f)),
        "place": rep(np.arange(P, dtype=f)), "token": (np.arange(TILES)[None, :] * P + p[:, None]).astype(f),
    }
    return np.concatenate([parts[n] for n, _ in ROWS], axis=1)


def laid_out(i):
    return {
        "x": i["x"], "ctxt": np.reshape(np.transpose(i["ctx_768"], (2, 0, 1)), (CK, B * KV)),
        "wq0": i["L0_xattn_Wq"], "wk0": i["L0_xattn_Wk"], "wv0": i["L0_xattn_Wv"], "wo0": i["L0_xattn_Wo"],
        "wg": np.transpose(i["L0_ffn_Wg"]),
        "w1": np.transpose(i["L0_ffn_w1"], (0, 2, 1)), "w2": np.transpose(i["L0_ffn_w2"], (0, 2, 1)),
        "wqt1": np.transpose(i["L1_xattn_w_q"]), "wk1": i["L1_xattn_w_k"], "wv1": i["L1_xattn_w_v"], "wo1": i["L1_xattn_w_out"],
        "fwin": np.concatenate([i["L1_ffn_Win"]] * 2, axis=1), "fwout": np.concatenate([i["L1_ffn_Wout"]] * 2, axis=0),
        "rows": packed_rows(i),
    }


def kernel(**inputs):
    import concourse.bacc as bacc
    from concourse.bass_utils import run_bass_kernel_spmd

    nc = bacc.Bacc("TRN2", target_bir_lowering=False, num_devices=1)
    arrays, args = {}, []
    for name, a in laid_out({k: np.asarray(v) for k, v in inputs.items()}).items():
        arrays[f"in_{name}"] = np.ascontiguousarray(a)
        args.append(nc.dram_tensor(f"in_{name}", a.shape, mybir.dt.from_np(a.dtype), kind="ExternalInput").ap())
    args.append(nc.dram_tensor("out", (B, S, C), F32, kind="ExternalOutput").ap())
    gated_blocks(nc, *args)
    return run_bass_kernel_spmd(nc, [arrays], core_ids=[0]).results[0]["out"]
```

```python
from contextlib import ExitStack

import numpy as np

import concourse.bass as bass
from concourse import mybir

ALU = mybir.AluOpType
ACT = mybir.ActivationFunctionType
AX = mybir.AxisListType
F32 = mybir.dt.float32
F32R = mybir.dt.float32r
I32 = mybir.dt.int32
U32 = mybir.dt.uint32
ds = bass.ds

P = 128
B, S, C = 4, 512, 256
KV, CK = 64, 192
KP = CK // 2
NTOK = B * S
TILES = NTOK // P
TPB = S // P
KC = C // P
H = 16
PAIRS = H // 2
D0 = C // H
D1 = 64
HK = H * KV
CLAMP = 10000.0
EPS = 1e-5
NE, TOPK = 8, 2
FF = 256
ITEMS = TOPK * NTOK // P + NE
SLOTS = ITEMS * P
M1, INNER = 64, 16
PASSES = 3

ROWS = [("ident", P), ("tri", P), ("mask", P // D0), ("rev", NE), ("item", ITEMS), ("ones", P),
        ("bq", KC), ("bk", KC), ("bv", KC), ("bo", C), ("bg", NE), ("gx", 2), ("gf", 2), ("bout1", C),
        ("fbin", 1), ("fw1", INNER // 2), ("fb1", INNER // 2), ("fw2", INNER // 2), ("fb2", 1), ("fbout", C),
        ("scan", P), ("place", P), ("token", TILES)]
COL, _o = {}, 0
for _n, _w in ROWS:
    COL[_n] = (_o, _o + _w)
    _o += _w
NCOL = _o


def split3(hi_l, lo_l, hi_r, lo_r):
    return ((hi_l, hi_r), (lo_l, hi_r), (hi_l, lo_r))


def keep_warm(nc, bank, operand, count):
    for _ in range(count):
        nc.tensor.matmul(bank, operand[:, 0:P], operand, start=True, stop=True)


def live(t):
    return not isinstance(t, int) or 0 <= t < TILES


def staged(eng, body, first, steady, after, last, unroll=2):
    for i in range(first, steady):
        body(i, i % unroll)
    with eng.Fori(steady // unroll, after // unroll) as turn:
        for q in range(unroll):
            body(unroll * turn + q, q)
    for i in range(after, last):
        body(i, i % unroll)


def gated_blocks(nc, x, ctxt, wq0, wk0, wv0, wo0, wg, w1, w2, wqt1, wk1, wv1, wo1, fwin, fwout, rows, out):
    top = ExitStack()
    with top:
        def sbuf(name, shape, dt=F32):
            return top.enter_context(nc.sbuf_tensor(name, shape, dt))

        xres = sbuf("xres", [P, TILES, C])
        cst = sbuf("cst", [P, NCOL])
        gates = sbuf("gates", [P, 4])
        mhalf = sbuf("mhalf", [P, 1])
        slots = sbuf("slots", [P, TOPK, TILES], U32)
        wsel = sbuf("wsel", [P, TOPK, TILES])
        xn_dram = nc.dram_tensor("normed_tokens", [NTOK, C], F32).ap()
        ys_dram = nc.dram_tensor("expert_out", [SLOTS, C], F32).ap()
        ys_stored = [top.enter_context(nc.semaphore(f"ys_stored{p}")) for p in range(2)]

        def c(name):
            return cst[:, COL[name][0]:COL[name][1]]

        with ExitStack() as ffn:
            lg = ffn.enter_context(nc.sbuf_tensor("ffn0_logits", [P, TILES * NE], F32))
            w1l, w2l, w_in = attention0(nc, c, x, ctxt, wq0, wk0, wv0, wo0, rows, xres, xn_dram, cst, gates, mhalf,
                                        wg, w1, w2, ffn, lg)
            second = SecondWeights(nc, ctxt, wqt1, wk1, wv1, wo1)
            experts(nc, c, w1l, w2l, w_in, lg, xn_dram, ys_dram, ys_stored, gates, slots, wsel, second)
        attention1(nc, c, second, ys_dram, ys_stored, xres, gates, mhalf, slots, wsel)
        mlp1(nc, c, fwin, fwout, xres, gates, mhalf, out)


def attention0(nc, c, x, ctxt, wq0, wk0, wv0, wo0, rows, xres, xn_dram, cst, gates, mhalf, wg, w1, w2, ffn, lg):
    with ExitStack() as keep:
        def sbuf(name, shape, dt=F32, on=keep):
            return on.enter_context(nc.sbuf_tensor(f"a0_{name}", shape, dt, side="right"))

        bkh, bkl = (sbuf(f"blockk_{s}", [P, B, KC, 8 * KV], F32R) for s in ("hi", "lo"))
        bh, bl = (sbuf(f"b_{s}", [P, B, PAIRS, C], F32R) for s in ("hi", "lo"))
        wqh, wql = (sbuf(f"wq_{s}", [P, KC, C], F32R) for s in ("hi", "lo"))
        bos = sbuf("bo_scaled", [P, C])
        wghl = sbuf("wg_hi_lo", [P, KC, 2 * NE], F32R)
        shift, rstd = sbuf("ln_shift", [P, TILES]), sbuf("ln_rstd", [P, TILES])
        bqs = sbuf("bq_guarded", [P, KC])
        prepare0(nc, c, x, ctxt, wq0, wk0, wv0, wo0, rows, xres, cst, gates, mhalf, bkh, bkl, bh, bl, wqh, wql, bos,
                 wg, wghl, shift, rstd, bqs)
        w1l = ffn.enter_context(nc.sbuf_tensor("ffn0_w1_lo", [P, NE * KC, 2 * FF], F32R))
        w2l = ffn.enter_context(nc.sbuf_tensor("ffn0_w2_lo", [P, NE * 2, C], F32R))
        w_in = ffn.enter_context(nc.semaphore("ffn0_w_in"))
        attend0(nc, c, xres, xn_dram, mhalf, bkh, bkl, bh, bl, wqh, wql, bos, wghl, shift, rstd, bqs, lg, w1, w2, w1l, w2l, w_in)
    return w1l, w2l, w_in


def prepare0(nc, c, x, ctxt, wq0, wk0, wv0, wo0, rows, xres, cst, gates, mhalf, bkh, bkl, bh, bl, wqh, wql, bos,
             wg, wghl, shift, rstd, bqs):
    with ExitStack() as ctx:
        def sbuf(name, shape, dt=F32):
            return ctx.enter_context(nc.sbuf_tensor(f"kv0_{name}", shape, dt))

        def sem(name):
            return ctx.enter_context(nc.semaphore(f"kv0_{name}"))

        ctr, cth, ctl = sbuf("ctx_raw", [KP, 2, B * KV]), sbuf("ctx_hi", [KP, 2, B * KV], F32R), sbuf("ctx_lo", [KP, 2, B * KV], F32R)
        wkr, wkh, wkl = sbuf("wk_raw", [KP, 2, C]), sbuf("wk_hi", [KP, 2, C], F32R), sbuf("wk_lo", [KP, 2, C], F32R)
        wvr, wvh, wvl = sbuf("wv_raw", [KP, 2, C]), sbuf("wv_hi", [KP, 2, C], F32R), sbuf("wv_lo", [KP, 2, C], F32R)
        wor, woh, wol = sbuf("wo_raw", [P, KC, C]), sbuf("wo_hi", [P, KC, C], F32R), sbuf("wo_lo", [P, KC, C], F32R)
        wqr, wqs = sbuf("wq_raw", [P, KC, C]), sbuf("wq_guarded", [P, KC, C])
        unguarded = sbuf("k_unguarded", [P, KC, B * KV])
        NCHECK = 4
        checked, bad = sbuf("nan_sums", [P, NCHECK]), sbuf("nan_found", [P, NCHECK])
        nbad, clean = sbuf("nan_count", [P, 1]), sbuf("no_nan", [P, 1])
        full, high, low = (sbuf(n, [P, 2, KC, B * KV]) for n in ("vk_full", "vk_hi", "vk_lo"))
        bvh, bvl = (sbuf(f"blockv_{h}", [P, B, KC, 8 * KV], F32R) for h in ("hi", "lo"))
        wgr = sbuf("wg_raw", [P, KC, NE])
        st, mv, ve = sbuf("ln_stats", [P, TILES, 6]), sbuf("ln_mean_var", [P, TILES, 2]), sbuf("ln_var_eps", [P, TILES])
        ps_vk = ctx.enter_context(nc.psum_tensor("kv0_ps_vk", [P, 2, KC, 512], F32))
        ps_f = ctx.enter_context(nc.psum_tensor("kv0_ps_fold", [P, 2, 2, 512], F32))

        cst_in, ctx_in, wk_in, wv_in, wq_in, wo_in = (sem(n) for n in (
            "cst_in", "ctx_in", "wk_in", "wv_in", "wq_in", "wo_in"))
        x_in = [sem(f"x_in{b}") for b in range(B)]
        gate_done, his, los, vk_ready, vk_full, vk_hi, vk_lo, vblock_lo, f_ready, fhi, flo = (sem(n) for n in (
            "gate_done", "his", "los", "vk_ready", "vk_full_done", "vk_hi_done", "vk_lo_done", "vblock_lo_done", "fold_ready",
            "fold_hi_done", "fold_lo_done"))
        wg_in, wg_hi = sem("wg_in"), sem("wg_hi_done")
        vblock_hi = sem("vblock_hi_done")
        guard, nan_ready, nan_counted, wq_guarded = (sem(n) for n in ("guard_step", "nan_found_ready", "nan_counted", "wq_guarded_done"))
        lnst, lnmv, lnve, lnrs = (sem(n) for n in ("ln_stats_done", "ln_mv_done", "ln_ve_done", "ln_rstd_done"))

        weights = [(ctr, cth, ctl, ctx_in), (wvr, wvh, wvl, wv_in), (wkr, wkh, wkl, wk_in), (wor, woh, wol, wo_in),
                   (wqs, wqh, wql, wq_guarded)]

        def spread(a, w, g):
            return a[:, w, g, :].rearrange("p (b o k) -> p b o k", o=1, k=KV).broadcast_to([P, B, 8, KV])

        def block(a, g):
            return a[:, :, g, :].rearrange("p b (h k) -> p b h k", k=KV)

        ps_bad = ps_vk[:, 0, 0, B * KV:B * KV + NCHECK]
        mask = c("mask").rearrange("p (o h q) -> p o h q", o=1, q=1).broadcast_to([P, B, 8, KV])

        def folded(a, j, m):
            return ps_f[:, j % 2, m, :].rearrange("p (b c) -> p b c", b=2), a[:, 2 * m:2 * m + 2, j, :]

        with nc.Block() as block_:
            @block_.sync
            def _(sp):
                sp.dma_start(ctr[:], ctxt.rearrange("(k p) n -> p k n", p=KP)).then_inc(ctx_in, 16)
                sp.dma_start(wvr[:], wv0.rearrange("(k p) n -> p k n", p=KP)).then_inc(wv_in, 16)
                sp.dma_start(cst[:], rows).then_inc(cst_in, 16)
                sp.dma_start(wkr[:], wk0.rearrange("(k p) n -> p k n", p=KP)).then_inc(wk_in, 16)
                sp.dma_start(wor[:], wo0.rearrange("(k p) n -> p k n", p=P)).then_inc(wo_in, 16)
                sp.dma_start(wqr[:], wq0.rearrange("(k p) n -> p k n", p=P)).then_inc(wq_in, 16)
                for b in range(B):
                    sp.dma_start(xres[:, b * TPB:(b + 1) * TPB, :],
                                 x[b].rearrange("(t p) c -> p t c", p=P)).then_inc(x_in[b], 16)
                sp.dma_start(wgr[:], wg.rearrange("(k p) e -> p k e", p=P)).then_inc(wg_in, 16)

            @block_.gpsimd
            def _(pool):
                pool.wait_ge(cst_in, 16)
                for g in range(KC):
                    pool.wait_ge(vk_lo, g + 1)
                    pool.tensor_tensor(block(bvl, g), spread(low, 0, g), mask, ALU.mult).then_inc(vblock_lo, 1)
                pool.wait_ge(lnve, 1)
                pool.tensor_tensor(rstd[:], ve[:], mhalf[:].broadcast_to([P, TILES]), ALU.pow).then_inc(lnrs, 1)
                for g in range(KC):
                    pool.wait_ge(vk_lo, KC + g + 1)
                    pool.tensor_tensor(block(bkl, g), spread(low, 1, g), mask, ALU.mult)
                pool.tensor_tensor(block(bkh, 1), spread(high, 1, 1), mask, ALU.mult)

            @block_.scalar
            def _(act):
                def weight_high(n):
                    raw, hi, _, loaded = weights[n]
                    act.wait_ge(loaded, 1 if loaded is wq_guarded else 16)
                    act.copy(hi[:], raw[:]).then_inc(his, 1)

                def block_high(w, g, wait):
                    act.wait_ge(vk_hi, wait)
                    for h in range(8):
                        act.activation(block((bvh, bkh)[w], g)[:, :, h, :], high[:, w, g, :].rearrange("p (b k) -> p b k", b=B),
                                       ACT.Copy, scale=c("mask")[:, h:h + 1]).then_inc(vblock_hi, 1)

                def high_part(w, g):
                    act.wait_ge(vk_full, KC * w + g + 1)
                    act.copy(high[:, w, g, :].bitcast(F32R), full[:, w, g, :]).then_inc(vk_hi, 1)

                weight_high(0)
                weight_high(1)
                act.wait_ge(cst_in, 16)
                act.activation(gates[:, 0:2], c("gx"), ACT.Tanh).then_inc(gate_done, 1)
                act.activation(gates[:, 2:4], c("gf"), ACT.Tanh).then_inc(gate_done, 1)
                weight_high(2)
                weight_high(3)
                for g in range(KC):
                    high_part(0, g)
                for g in range(KC):
                    block_high(0, g, g + 1)
                act.wait_ge(gate_done, 2)
                for j in range(PAIRS):
                    if j in (2, 3):
                        high_part(1, j - 2)
                    if j == 5:
                        block_high(1, 0, KC + 1)
                    if j == 4:
                        weight_high(4)
                    for m in range(2):
                        act.wait_ge(f_ready, 2 * j + m + 1)
                        src, dst = folded(bh, j, m)
                        act.activation(dst, src, ACT.Identity, scale=gates[:, 0:1]).then_inc(fhi, 1)
                act.wait_ge(wg_in, 16)
                act.copy(wghl[:, :, 0:NE], wgr[:]).then_inc(wg_hi, 1)

            @block_.vector
            def _(dve):
                def weight_low(n):
                    raw, hi, lo, _ = weights[n]
                    dve.wait_ge(his, n + 1)
                    dve.tensor_tensor(lo[:], raw[:], hi[:].bitcast(F32), ALU.subtract).then_inc(los, 1)

                def biased(w, g):
                    dve.wait_ge(vk_ready, KC * w + g + 1)
                    dve.tensor_scalar((full[:, 0], unguarded)[w][:, g, :], ps_vk[:, w, g, 0:B * KV], c(("bv", "bk")[w])[:, g:g + 1],
                                      (1.0, D0 ** -0.5)[w], ALU.add, ALU.mult).then_inc((vk_full, guard)[w], 1)

                def low_part(w, g):
                    dve.wait_ge(vk_hi, KC * w + g + 1)
                    dve.tensor_tensor(low[:, w, g, :], full[:, w, g, :], high[:, w, g, :], ALU.subtract).then_inc(vk_lo, 1)

                def statistics():
                    for t in range(TILES):
                        dve.wait_ge(x_in[t // TPB], 16)
                        dve.bn_stats(st[:, t, :], xres[:, t, :]).then_inc(lnst, 1)
                    for t in range(TILES):
                        dve.wait_ge(lnst, t + 1)
                        dve.bn_aggr(mv[:, t, :], st[:, t, :]).then_inc(lnmv, 1)
                    dve.wait_ge(lnmv, TILES)
                    dve.tensor_scalar(ve[:], mv[:, :, 1], EPS, None, ALU.add).then_inc(lnve, 1)

                def check_for_nan():
                    dve.wait_ge(wq_in, 16)
                    dve.wait_ge(guard, KC)
                    for n, a in enumerate((mv[:].rearrange("p t s -> p (t s)"), unguarded[:].rearrange("p g n -> p (g n)"),
                                           wqr[:].rearrange("p k n -> p (k n)"), c("bq"))):
                        dve.tensor_reduce(checked[:, n:n + 1], a, AX.X, ALU.add).then_inc(guard, 1)
                    dve.wait_ge(guard, KC + NCHECK)
                    dve.tensor_tensor(bad[:], checked[:], checked[:], ALU.not_equal).then_inc(nan_ready, 1)

                def apply_guard():
                    dve.memset(wqs[:], 0.0)
                    dve.memset(bqs[:], 0.0)
                    dve.memset(full[:, 1], 0.0).then_inc(guard, 1)
                    dve.wait_ge(nan_counted, 1)
                    dve.tensor_reduce(nbad[:], ps_bad, AX.X, ALU.add).then_inc(guard, 1)
                    dve.wait_ge(guard, KC + NCHECK + 2)
                    dve.tensor_single_scalar(clean[:], nbad[:], 0.0, ALU.is_equal).then_inc(guard, 1)
                    dve.wait_ge(guard, KC + NCHECK + 3)
                    for g in range(KC):
                        dve.copy_predicated(full[:, 1, g, :], clean[:].bitcast(U32).broadcast_to([P, B * KV]), unguarded[:, g, :]).then_inc(vk_full, 1)
                    for k in range(KC):
                        ins = dve.copy_predicated(wqs[:, k, :], clean[:].bitcast(U32).broadcast_to([P, C]), wqr[:, k, :])
                    ins.then_inc(wq_guarded, 1)
                    dve.copy_predicated(bqs[:], clean[:].bitcast(U32).broadcast_to([P, KC]), c("bq"))

                def folded_low(j):
                    for m in range(2):
                        dve.wait_ge(fhi, 2 * j + m + 1)
                        src, dst = folded(bl, j, m)
                        _, hi = folded(bh, j, m)
                        dve.scalar_tensor_tensor(out=dst, in0=src, scalar=gates[:, 0:1], in1=hi.bitcast(F32),
                                                 op0=ALU.mult, op1=ALU.subtract).then_inc(flo, 1)

                dve.memset(mhalf[:], -0.5)
                weight_low(0)
                weight_low(1)
                weight_low(2)
                dve.wait_ge(cst_in, 16)
                biased(0, 0)
                biased(0, 1)
                weight_low(3)
                for g in range(KC):
                    low_part(0, g)
                biased(1, 0)
                biased(1, 1)
                statistics()
                check_for_nan()
                dve.wait_ge(gate_done, 2)
                for j in range(PAIRS):
                    if j == 2:
                        dve.tensor_scalar(bos[:], c("bo"), gates[:, 0:1], None, ALU.mult)
                        apply_guard()
                    if j in (3, 4):
                        low_part(1, j - 3)
                    if j == 5:
                        weight_low(4)
                    folded_low(j)
                dve.wait_ge(wg_hi, 1)
                dve.tensor_tensor(wghl[:, :, NE:2 * NE], wgr[:], wghl[:, :, 0:NE].bitcast(F32), ALU.subtract)
                dve.wait_ge(lnrs, 1)
                dve.scalar_tensor_tensor(out=shift[:], in0=mv[:, :, 0], scalar=-1.0, in1=rstd[:], op0=ALU.mult, op1=ALU.mult)

            @block_.tensor
            def _(pe):
                for w, (wh, wl) in enumerate(((wvh, wvl), (wkh, wkl))):
                    pe.wait_ge(los, w + 2)
                    for g in range(KC):
                        n = 0
                        for k in range(2):
                            m = slice(g * P, (g + 1) * P)
                            for l, r in split3(wh[:, k, m], wl[:, k, m], cth[:, k, :], ctl[:, k, :]):
                                mm = nc.tensor.matmul(ps_vk[:, w, g, 0:B * KV], l, r, start=(n == 0), stop=(n == 2 * PASSES - 1))
                                n += 1
                        mm.then_inc(vk_ready, 1)
                pe.wait_ge(los, 4)
                for j in range(PAIRS):
                    if j % 4 == 0:
                        pe.wait_ge(vblock_hi, 8 * (j // 4 + 1))
                        pe.wait_ge(vblock_lo, j // 4 + 1)
                    if j == 2:
                        pe.wait_ge(nan_ready, 1)
                        nc.tensor.matmul(ps_bad, c("ones"), bad[:], start=True, stop=True).then_inc(nan_counted, 1)
                    if j >= 2:
                        pe.wait_ge(flo, 2 * (j - 1))
                    g, hk = j // 4, slice(j % 4 * P, (j % 4 + 1) * P)
                    for b in range(B):
                        for n, (l, r) in enumerate(split3(bvh[:, b, g, hk], bvl[:, b, g, hk], woh[:, g, :], wol[:, g, :])):
                            mm = nc.tensor.matmul(ps_f[:, j % 2, b // 2, (b % 2) * C:(b % 2 + 1) * C], l, r, start=(n == 0), stop=(n == PASSES - 1))
                        if b % 2:
                            mm.then_inc(f_ready, 1)


def attend0(nc, c, xres, xn_dram, mhalf, bkh, bkl, bh, bl, wqh, wql, bos, wghl, shift, rstd, bqs, lg, w1, w2, w1l, w2l, w_in):
    with ExitStack() as ctx:
        def sbuf(name, shape, dt=F32):
            return ctx.enter_context(nc.sbuf_tensor(f"att0_{name}", shape, dt))

        def sem(name):
            return ctx.enter_context(nc.semaphore(f"att0_{name}"))

        def bank(name, n=1):
            return ctx.enter_context(nc.psum_tensor(f"att0_{name}", [P, n, 512], F32))

        st, mv = sbuf("ln_stats", [P, 2, 6]), sbuf("ln_mean_var", [P, 2, 2])
        ve, rs = sbuf("ln_var_eps", [P, 2]), sbuf("ln_rstd", [P, 2])
        xn = sbuf("xn", [P, 2, 2, C])
        xh, xl = sbuf("xt_hi", [P, 2, 2, C], F32R), sbuf("xt_lo", [P, 2, 2, C], F32R)
        qf = sbuf("q_full", [P, 2, C])
        qh, ql = sbuf("qt_hi", [P, 2, C], F32R), sbuf("qt_lo", [P, 2, C], F32R)
        sc = sbuf("scores", [P, 2, HK])
        mx, sm, rc = (sbuf(n, [P, 2, H]) for n in ("score_max", "exp_sum", "recip"))
        ph, pl = sbuf("pt_hi", [P, HK], F32R), sbuf("pt_lo", [P, HK], F32R)
        ps_s, ps_p = bank("ps_scores", 2), bank("ps_pt", 2)
        ps_x, ps_q, ps_y = bank("ps_xt"), bank("ps_q"), bank("ps_y")

        (xt_ready, q_ready, s_ready, pt_ready, y_ready, logits) = (sem(n) for n in (
            "xt_ready", "q_ready", "scores_ready", "pt_ready", "y_ready", "logits_ready"))
        (xhi, qsum, qhi, copied, expd, phi) = (sem(n) for n in (
            "xt_hi_done", "q_biased", "q_hi_done", "scores_copied", "exp_done", "pt_hi_done"))
        (xlo, clipd, maxd, plo, sumd, recd, resd, lnve, lg_part) = (sem(n) for n in (
            "xt_lo_done", "clipped", "max_done", "pt_lo_done", "sum_done", "recip_done", "residual_done", "ln_next_ve", "lg_part"))
        (cent, qlo, xbias, normd, lnrs) = (sem(n) for n in ("centred", "q_lo_done", "bias_added", "probs_normed", "ln_next_rstd"))
        lndone = [sem("ln_out"), sem("ln_next_out")]
        stored = [sem("xn_next_stored0"), sem("xn_next_stored1")]
        ident = c("ident")
        NEXT = 7

        def halves(u):
            return slice(0 if live(u) else 1, 2 if live(u - NEXT) else 1)

        def transposing(u):
            return live(u) or live(u - NEXT)

        def wide(a):
            return a.rearrange("p (h o) -> p h o", o=1).broadcast_to([P, H, KV])

        def heads(a):
            return a.rearrange("p (h k) -> p h k", k=KV)

        def tile_of(t):
            return xres[:, ds(t, 1), :].rearrange("p o c -> p (o c)")

        def later(t, n=0):
            return not isinstance(t, int) or t > n

        def turns(eng, stages, first, last):
            def body(i, par):
                for stage, d in stages:
                    if live(i + d) or stage.__name__ in ("transpose_x", "x_high", "x_low") and transposing(i + d):
                        stage(i + d, (par + d) % 2)
            staged(eng, body, first, 6, 12, last)

        with nc.Block() as block:
            @block.sync
            def _(sp):
                for e in range(NE):
                    sp.dma_start(w1l[:, e * KC:(e + 1) * KC, :].bitcast(F32), w1[e].rearrange("(k p) f -> p k f", p=P)).then_inc(w_in, 16)
                    sp.dma_start(w2l[:, e * 2:(e + 1) * 2, :].bitcast(F32), w2[e].rearrange("(k p) f -> p k f", p=P)).then_inc(w_in, 16)

                def store(t, p):
                    sp.wait_ge(lndone[1], t + 1)
                    sp.dma_start(xn_dram[ds(t * P, P), :], xn[:, (p + NEXT) % 2, 1, :]).then_inc(stored[p], 16)
                turns(sp, ((store, -4),), 4, TILES + 4)
                for p in range(2):
                    sp.wait_ge(stored[p], 16 * TILES // 2)

            @block.tensor
            def _(pe):
                def transpose_probs(t, p):
                    pe.wait_ge(normd, t + 1)
                    for j in range(PAIRS):
                        mm = nc.tensor.transpose(ps_p[:, j // 4, (j % 4) * P:(j % 4 + 1) * P],
                                                 sc[:, p, j * P:(j + 1) * P], ident)
                        if j % 4 == 3:
                            mm.then_inc(pt_ready, 1)

                def scores(t, p):
                    pe.wait_ge(qlo, t + 1)
                    if later(t):
                        pe.wait_ge(copied, t)
                    for g in range(KC):
                        gs = slice(g * P, (g + 1) * P)
                        rh, rl = (w[:, ds(t // TPB, 1), g, :].rearrange("p o n -> p (o n)") for w in (bkh, bkl))
                        for n, (l, r) in enumerate(split3(qh[:, p, gs], ql[:, p, gs], rh, rl)):
                            mm = nc.tensor.matmul(ps_s[:, g, :], l, r, start=(n == 0), stop=(n == PASSES - 1))
                    mm.then_inc(s_ready, 1)

                def outputs(t, p):
                    pe.wait_ge(plo, 2 * t + 2)
                    if later(t):
                        pe.wait_ge(resd, t)
                    n = 0
                    for j in range(PAIRS):
                        rh, rl = (w[:, ds(t // TPB, 1), j, :].rearrange("p o n -> p (o n)") for w in (bh, bl))
                        for l, r in split3(ph[:, j * P:(j + 1) * P], pl[:, j * P:(j + 1) * P], rh, rl):
                            mm = nc.tensor.matmul(ps_y[:, 0, 0:C], l, r, start=(n == 0), stop=(n == PAIRS * PASSES - 1))
                            n += 1
                    mm.then_inc(y_ready, 1)

                def route_logits(t, p):
                    pe.wait_ge(xlo, t + NEXT + 1)
                    steps = ((xh, 0, 2), (xl, 0, 1), (xl, 1, 1), (xh, 1, 2))
                    for n, (lhs, k, w) in enumerate(steps):
                        mm = nc.tensor.matmul(ps_q[:, 0, ds(t * 2 * NE + C, w * NE)], lhs[:, (p + NEXT) % 2, 1, k * P:(k + 1) * P],
                                              wghl[:, k, 0:w * NE], start=(n == 0), stop=(n == len(steps) - 1))
                    mm.then_inc(logits, 1)

                def queries(t, p):
                    pe.wait_ge(xlo, t + 1)
                    for m in range(KC):
                        ms, n = slice(m * P, (m + 1) * P), 0
                        for k in range(KC):
                            ks = slice(k * P, (k + 1) * P)
                            for l, r in split3(wqh[:, k, ms], wql[:, k, ms], xh[:, p, 0, ks], xl[:, p, 0, ks]):
                                mm = nc.tensor.matmul(ps_q[:, 0, ms], l, r, start=(n == 0), stop=(n == KC * PASSES - 1))
                                n += 1
                    mm.then_inc(q_ready, 1)

                def transpose_x(u, p):
                    if live(u):
                        pe.wait_ge(lndone[0], u + 1)
                    if live(u - NEXT):
                        pe.wait_ge(lndone[1], u - NEXT + 1)
                    if not isinstance(u, int) or u > 0:
                        pe.wait_ge(xlo, u)
                    for h in range(2)[halves(u)]:
                        for k in range(KC):
                            mm = nc.tensor.transpose(ps_x[:, 0, h * C + k * P:h * C + (k + 1) * P], xn[:, p, h, k * P:(k + 1) * P], ident)
                    mm.then_inc(xt_ready, 1)
                turns(pe, ((transpose_probs, -2), (scores, 0), (route_logits, -5), (queries, 2), (transpose_x, 3), (outputs, -2)),
                      -3, TILES + 5)

            @block.scalar
            def _(act):
                def q_bias(t, p):
                    act.wait_ge(q_ready, t + 1)
                    for m in range(KC):
                        ms = slice(m * P, (m + 1) * P)
                        act.activation(qf[:, p, ms], ps_q[:, 0, ms], ACT.Identity, bias=bqs[:, m:m + 1]).then_inc(qsum, 1)
                    act.wait_ge(qsum, KC * (t + 1))
                    act.copy(qh[:, p, :], qf[:, p, :]).then_inc(qhi, 1)

                def x_high(t, p):
                    act.wait_ge(xt_ready, t + 1)
                    hs = halves(t)
                    act.copy(xh[:, p, hs, :], ps_x[:, 0, :].rearrange("p (h c) -> p h c", h=2)[:, hs, :]).then_inc(xhi, 1)

                def normed(t, p):
                    act.activation(xn[:, p, 0, :], tile_of(t), ACT.Identity, bias=shift[:, ds(t, 1)],
                                   scale=rstd[:, ds(t, 1)]).then_inc(lndone[0], 1)

                def probs_high(t, p):
                    for half in range(2):
                        act.wait_ge(pt_ready, 2 * t + half + 1)
                        if half == 0 and later(t):
                            act.wait_ge(y_ready, t)
                        act.copy(ph[:, half * 512:(half + 1) * 512], ps_p[:, half, :]).then_inc(phi, 1)

                def exponential(t, p):
                    act.wait_ge(cent, t + 1)
                    act.activation(sc[:, p, :], sc[:, p, :], ACT.Exp).then_inc(expd, 1)

                def copy_scores(t, p):
                    act.wait_ge(s_ready, t + 1)
                    if later(t, 1):
                        act.wait_ge(pt_ready, 2 * t - 2)
                    act.copy(sc[:, p, :].rearrange("p (a n) -> p a n", a=2), ps_s[:]).then_inc(copied, 1)
                turns(act, ((probs_high, -2), (exponential, -1), (copy_scores, 0), (q_bias, 2), (x_high, 3), (normed, 4)),
                      -4, TILES + 4)

            @block.gpsimd
            def _(pool):
                def q_low(t, p):
                    pool.wait_ge(qhi, t + 1)
                    pool.tensor_tensor(ql[:, p, :], qf[:, p, :], qh[:, p, :].bitcast(F32), ALU.subtract).then_inc(qlo, 1)

                def normalise(t, p):
                    pool.wait_ge(recd, t + 1)
                    pool.tensor_tensor(heads(sc[:, p, :]), heads(sc[:, p, :]), wide(rc[:, p, :]), ALU.mult).then_inc(normd, 1)

                def centre(t, p):
                    pool.wait_ge(maxd, t + 1)
                    pool.tensor_tensor(heads(sc[:, p, :]), heads(sc[:, p, :]), wide(mx[:, p, :]), ALU.subtract).then_inc(cent, 1)
                    pool.tensor_tensor(tile_of(t), tile_of(t), bos[:], ALU.add).then_inc(xbias, 1)

                def rstd_next(t, p):
                    pool.wait_ge(lnve, t + 1)
                    pool.tensor_tensor(rs[:, p:p + 1], ve[:, p:p + 1], mhalf[:], ALU.pow).then_inc(lnrs, 1)
                turns(pool, ((rstd_next, -3), (normalise, -1), (q_low, 2), (centre, 0)), -2, TILES + 3)

            @block.vector
            def _(dve):
                def normed_next(t, p):
                    dve.wait_ge(lnrs, t + 1)
                    if later(t, 1):
                        dve.wait_ge(stored[p], (t // 2) * 16)
                    dve.tensor_scalar(xn[:, (p + NEXT) % 2, 1, :], tile_of(t), mv[:, p, 0:1], rs[:, p:p + 1], ALU.subtract, ALU.mult).then_inc(lndone[1], 1)

                def residual(t, p):
                    dve.wait_ge(y_ready, t + 1)
                    dve.wait_ge(xbias, t + 1)
                    dve.tensor_tensor(tile_of(t), ps_y[:, 0, 0:C], tile_of(t), ALU.add).then_inc(resd, 1)

                def x_low(t, p):
                    dve.wait_ge(xhi, t + 1)
                    hs = halves(t)
                    dve.tensor_tensor(xl[:, p, hs, :], ps_x[:, 0, :].rearrange("p (h c) -> p h c", h=2)[:, hs, :],
                                      xh[:, p, hs, :].bitcast(F32), ALU.subtract).then_inc(xlo, 1)

                def probs_low(t, p):
                    for half in range(2):
                        hs = slice(half * 512, (half + 1) * 512)
                        dve.wait_ge(phi, 2 * t + half + 1)
                        dve.tensor_tensor(pl[:, hs], ps_p[:, half, :], ph[:, hs].bitcast(F32), ALU.subtract).then_inc(plo, 1)

                def sums(t, p):
                    dve.wait_ge(expd, t + 1)
                    dve.tensor_reduce(sm[:, p, :], heads(sc[:, p, :]), AX.X, ALU.add).then_inc(sumd, 1)
                    dve.wait_ge(sumd, t + 1)
                    dve.reciprocal(rc[:, p, :], sm[:, p, :]).then_inc(recd, 1)

                def clip_and_max(t, p):
                    dve.wait_ge(copied, t + 1)
                    dve.tensor_scalar(sc[:, p, :], sc[:, p, :], CLAMP, -CLAMP, ALU.min, ALU.max).then_inc(clipd, 1)
                    dve.wait_ge(clipd, t + 1)
                    dve.tensor_reduce(mx[:, p, :], heads(sc[:, p, :]), AX.X, ALU.max).then_inc(maxd, 1)

                def stats_next(t, p):
                    dve.drain()
                    dve.bn_stats(st[:, p, :], tile_of(t))
                    dve.drain()
                    dve.bn_aggr(mv[:, p, :], st[:, p, :])
                    dve.drain()
                    dve.tensor_scalar(ve[:, p:p + 1], mv[:, p, 1:2], EPS, None, ALU.add).then_inc(lnve, 1)
                turns(dve, ((normed_next, -4), (residual, -3), (stats_next, -3), (probs_low, -2), (sums, -1), (clip_and_max, 0),
                            (x_low, 3)), -3, TILES + 4)
                dve.wait_ge(logits, TILES)
                parts = ps_q[:, 0, C:2 * C].rearrange("p (t w e) -> p t w e", w=2, e=NE)
                lg3 = lg[:].rearrange("p (t e) -> p t e", e=NE)
                dve.tensor_tensor(lg3, parts[:, :, 0, :], c("bg").rearrange("p (o e) -> p o e", o=1).broadcast_to([P, TILES, NE]),
                                  ALU.add).then_inc(lg_part, 1)
                dve.wait_ge(lg_part, 1)
                dve.tensor_tensor(lg3, parts[:, :, 1, :], lg3, ALU.add)


def experts(nc, c, w1l, w2l, w_in, lg, xn_dram, ys_dram, ys_stored, gates, slots, wsel, second):
    with ExitStack() as ctx:
        def sbuf(name, shape, dt=F32):
            return ctx.enter_context(nc.sbuf_tensor(f"ffn0_{name}", shape, dt))

        w1h, w2h = sbuf("w1_hi", [P, NE * KC, 2 * FF], F32R), sbuf("w2_hi", [P, NE * 2, C], F32R)
        eid = sbuf("item_expert", [P, ITEMS], I32)
        token = sbuf("token_of_slot", [P, ITEMS], U32)
        second.place_vo()
        route(nc, c, w1h, w1l, w2h, w2l, w_in, eid, token, lg, gates, slots, wsel, second)
        second.place_kq()
        run_experts(nc, c, w1h, w1l, w2h, w2l, eid, token, xn_dram, ys_dram, ys_stored, second)


def route(nc, c, w1h, w1l, w2h, w2l, w_in, eid, token, lg0, gates, slots, wsel, second):
    with ExitStack() as ctx:
        def sbuf(name, shape, dt=F32):
            return ctx.enter_context(nc.sbuf_tensor(f"route_{name}", shape, dt))

        def sem(name):
            return ctx.enter_context(nc.semaphore(f"route_{name}"))

        TE, NB = TILES * NE, TOPK * TILES
        CHUNK = 8
        lg = [lg0, sbuf("logits1", [P, TE])]
        key = [sbuf(f"key{n}", [P, TE]) for n in range(2)]
        oneh = [sbuf(f"onehot{n}", [P, TE]) for n in range(2)]
        top = [sbuf(f"top{n}", [P, TILES]) for n in range(2)]
        kmax = [sbuf(f"keymax{n}", [P, TILES]) for n in range(2)]
        maskr = sbuf("chosen", [P, TE], F32R)
        trir, onesr = sbuf("tri_r", [P, P], F32R), sbuf("ones_r", [P, P], F32R)
        tot, incl, base, slot, tmp = (sbuf(n, [P, TE]) for n in ("totals_et", "inclusive", "base", "slot", "slot_picked"))
        cnt = sbuf("counts", [P, NE]); cnti = sbuf("counts_int", [P, NE], I32); ntl = sbuf("tiles_of_expert", [P, NE])
        endt, startt = sbuf("end_tile", [P, NE]), sbuf("start_slot", [P, NE])
        ge = sbuf("item_past_end", [P, ITEMS, NE]); eidf = sbuf("item_expert_f", [P, ITEMS])
        d21, ez, zp1, inv = (sbuf(n, [P, TILES]) for n in ("gap", "gap_exp", "denominator", "inverse"))
        slotf = sbuf("slot_f", [P, NB])
        sloti, itemf, placef = sbuf("slot_item_int", [P, NB], I32), sbuf("slot_item", [P, NB]), sbuf("slot_place", [P, NB])
        is_item, tok_item = sbuf("is_item", [P, NB, ITEMS]), sbuf("token_in_item", [P, NB, ITEMS], F32R)
        is_place = sbuf("is_place", [P, NB, P], F32R)
        ps_r = ctx.enter_context(nc.psum_tensor("route_ps_rank", [P, 512], F32))
        ps_c = ctx.enter_context(nc.psum_tensor("route_ps_totals", [P, 512], F32))
        ps_t = ctx.enter_context(nc.psum_tensor("route_ps_token", [P, 512], F32))
        ps_w = ctx.enter_context(nc.psum_tensor("route_ps_unread", [P, 512], F32))

        whi = sem("w_hi_done")
        step, gap, gexp, chosen, rank, placed, inverted = (sem(n) for n in (
            "route_step", "gap_ready", "gap_exp_done", "chosen_ready", "rank_ready", "placed", "inverted"))

        def te(a):
            return a.rearrange("p (t e) -> p t e", e=NE)

        def over_e(a):
            return a.rearrange("p (t o) -> p t o", o=1).broadcast_to([P, TILES, NE])

        def over_t(a):
            return a.rearrange("p (o e) -> p o e", o=1).broadcast_to([P, TILES, NE])

        POOL_W2 = 2

        def low_parts(eng, hi, lo, e):
            es = slice(e * KC, (e + 1) * KC)
            eng.tensor_tensor(lo[:, es, :], lo[:, es, :].bitcast(F32), hi[:, es, :].bitcast(F32), ALU.subtract)

        with nc.Block() as block:
            @block.sync
            def _(sp):
                second.load_vo(sp)

            @block.tensor
            def _(pe):
                pe.wait_ge(chosen, 1)
                nc.tensor.matmul(ps_r[:, 0:TE], trir[:], maskr[:], start=True, stop=True)
                nc.tensor.matmul(ps_c[:, 0:TE], onesr[:], maskr[:], start=True, stop=True).then_inc(rank, 1)
                pe.wait_ge(whi, 1)
                keep_warm(nc, ps_w[:], w1h[:, 0, :], 24)
                for n in range(NB):
                    if n % CHUNK == 0:
                        pe.wait_ge(placed, n // CHUNK + 1)
                    mm = nc.tensor.matmul(ps_t[:, 0:ITEMS], is_place[:, n, :], tok_item[:, n, :], start=(n == 0), stop=(n == NB - 1))
                mm.then_inc(inverted, 1)

            @block.scalar
            def _(act):
                act.wait_ge(w_in, 32 * NE)
                for e in range(NE):
                    if e == 2:
                        act.wait_ge(gap, 1)
                        act.activation(ez[:], d21[:], ACT.Exp).then_inc(gexp, 1)
                    act.copy(w1h[:, e * KC:(e + 1) * KC, :], w1l[:, e * KC:(e + 1) * KC, :].bitcast(F32)).then_inc(whi, 1)
                    act.copy(w2h[:, e * 2:(e + 1) * 2, :], w2l[:, e * 2:(e + 1) * 2, :].bitcast(F32)).then_inc(whi, 1)

            @block.gpsimd
            def _(pool):
                for e in range(NE):
                    pool.wait_ge(whi, 2 * e + 1)
                    low_parts(pool, w1h, w1l, e)
                pool.wait_ge(whi, 2 * NE)
                for e in range(NE - POOL_W2, NE):
                    low_parts(pool, w2h, w2l, e)

            @block.vector
            def _(dve):
                steps = [0]

                def link(ins):
                    steps[0] += 1
                    ins.then_inc(step, 1)
                    dve.wait_ge(step, steps[0])

                dve.tensor_copy(trir[:], c("tri"))
                dve.tensor_copy(onesr[:], c("ones"))
                for n in range(TOPK):
                    link(dve.tensor_reduce(top[n][:], te(lg[n][:]), AX.X, ALU.max))
                    link(dve.tensor_tensor(te(key[n][:]), te(lg[n][:]), over_e(top[n][:]), ALU.is_equal))
                    link(dve.tensor_tensor(te(key[n][:]), te(key[n][:]), over_t(c("rev")), ALU.mult))
                    link(dve.tensor_reduce(kmax[n][:], te(key[n][:]), AX.X, ALU.max))
                    link(dve.tensor_tensor(te(oneh[n][:]), over_t(c("rev")), over_e(kmax[n][:]), ALU.is_equal))
                    if n == 0:
                        link(dve.scalar_tensor_tensor(out=lg[1][:], in0=oneh[0][:], scalar=-3e38, in1=lg[0][:], op0=ALU.mult, op1=ALU.add))
                dve.tensor_tensor(maskr[:], oneh[0][:], oneh[1][:], ALU.add).then_inc(chosen, 1)
                dve.tensor_tensor(d21[:], top[1][:], top[0][:], ALU.subtract).then_inc(gap, 1)
                dve.wait_ge(rank, 1)
                link(dve.tensor_copy(tot[:].rearrange("p (e t) -> p t e", e=NE), te(ps_c[:, 0:TE])))
                link(dve.tensor_tensor_scan(incl[:], c("scan"), tot[:], 0.0, ALU.mult, ALU.add))
                link(dve.tensor_scalar(cnt[:], incl[:].rearrange("p (e t) -> p e t", e=NE)[:, :, TILES - 1], float(P - 1), None, ALU.add))
                link(dve.tensor_copy(cnti[:], cnt[:]))
                link(dve.tensor_single_scalar(cnti[:], cnti[:], 7, ALU.arith_shift_right))
                link(dve.tensor_copy(ntl[:], cnti[:]))
                link(dve.tensor_tensor_scan(endt[:], c("ones")[:, 0:NE], ntl[:], 0.0, ALU.mult, ALU.add))
                link(dve.tensor_tensor(startt[:], endt[:], ntl[:], ALU.subtract))
                link(dve.tensor_scalar(startt[:], startt[:], float(P), None, ALU.mult))
                link(dve.tensor_tensor(incl[:], incl[:], tot[:], ALU.subtract))
                link(dve.tensor_tensor(te(base[:]), incl[:].rearrange("p (e t) -> p t e", e=NE), over_t(startt[:]), ALU.add))
                link(dve.tensor_tensor(slot[:], ps_r[:, 0:TE], base[:], ALU.add))
                for n in range(TOPK):
                    link(dve.tensor_tensor(tmp[:], slot[:], oneh[n][:], ALU.mult))
                    link(dve.tensor_reduce(slotf[:, n * TILES:(n + 1) * TILES], te(tmp[:]), AX.X, ALU.add))
                dve.tensor_copy(slots[:].rearrange("p k t -> p (k t)"), slotf[:])
                link(dve.tensor_copy(sloti[:], slotf[:]))
                link(dve.tensor_single_scalar(sloti[:], sloti[:], 7, ALU.arith_shift_right))
                link(dve.tensor_copy(itemf[:], sloti[:]))
                link(dve.scalar_tensor_tensor(out=placef[:], in0=itemf[:], scalar=-float(P), in1=slotf[:], op0=ALU.mult, op1=ALU.add))
                link(dve.tensor_tensor(is_item[:], c("item").rearrange("p (o j) -> p o j", o=1).broadcast_to([P, NB, ITEMS]),
                                       itemf[:].rearrange("p (n o) -> p n o", o=1).broadcast_to([P, NB, ITEMS]), ALU.is_equal))
                for k in range(TOPK):
                    ks = slice(k * TILES, (k + 1) * TILES)
                    link(dve.tensor_tensor(tok_item[:, ks, :], is_item[:, ks, :],
                                           c("token").rearrange("p (t o) -> p t o", o=1).broadcast_to([P, TILES, ITEMS]), ALU.mult))
                for n in range(0, NB, CHUNK):
                    dve.tensor_tensor(is_place[:, n:n + CHUNK, :], c("place").rearrange("p (o r) -> p o r", o=1).broadcast_to([P, CHUNK, P]),
                                      placef[:, n:n + CHUNK].rearrange("p (n o) -> p n o", o=1).broadcast_to([P, CHUNK, P]),
                                      ALU.is_equal).then_inc(placed, 1)
                link(dve.tensor_tensor(ge[:], c("item").rearrange("p (j o) -> p j o", o=1).broadcast_to([P, ITEMS, NE]),
                                       endt[:].rearrange("p (o e) -> p o e", o=1).broadcast_to([P, ITEMS, NE]), ALU.is_ge))
                link(dve.tensor_reduce(eidf[:], ge[:], AX.X, ALU.add))
                link(dve.tensor_scalar(eidf[:], eidf[:], float(NE - 1), None, ALU.min))
                dve.tensor_copy(eid[:], eidf[:])
                dve.wait_ge(whi, 2 * NE)
                for e in range(NE - POOL_W2):
                    low_parts(dve, w2h, w2l, e)
                dve.wait_ge(inverted, 1)
                dve.tensor_copy(token[:], ps_t[:, 0:ITEMS])
                dve.wait_ge(gexp, 1)
                link(dve.tensor_scalar(zp1[:], ez[:], 1.0, None, ALU.add))
                link(dve.reciprocal(inv[:], zp1[:]))
                link(dve.tensor_scalar(wsel[:, 0, :], inv[:], gates[:, 2:3], None, ALU.mult))
                dve.tensor_tensor(wsel[:, 1, :], wsel[:, 0, :], ez[:], ALU.mult)


def run_experts(nc, c, w1h, w1l, w2h, w2l, eid, token, xn_dram, ys_dram, ys_stored, second):
    with ExitStack() as ctx:
        def sbuf(name, shape, dt=F32):
            return ctx.enter_context(nc.sbuf_tensor(f"moe_{name}", shape, dt))

        def sem(name):
            return ctx.enter_context(nc.semaphore(f"moe_{name}"))

        xg = sbuf("gathered_tile", [P, 2, C])
        xh, xl = sbuf("xt_hi", [P, 2, C], F32R), sbuf("xt_lo", [P, 2, C], F32R)
        sg, act_a = sbuf("silu_gate", [P, 2, FF]), sbuf("hidden", [P, 2, FF])
        ah, al = sbuf("at_hi", [P, 2, FF], F32R), sbuf("at_lo", [P, 2, FF], F32R)
        yo = sbuf("expert_tile", [P, 2, C])
        unread = sbuf("unread", [P, 1])
        ps_x = ctx.enter_context(nc.psum_tensor("moe_ps_xt", [P, 2, 512], F32))
        ps_h = ctx.enter_context(nc.psum_tensor("moe_ps_h", [P, 2, 512], F32))
        ps_a = ctx.enter_context(nc.psum_tensor("moe_ps_at", [P, 2, 512], F32))
        ps_y = ctx.enter_context(nc.psum_tensor("moe_ps_y", [P, 2, 512], F32))
        x_in = [sem("x_in0"), sem("x_in1")]
        y_out = ys_stored
        (xt_ready, xhi, xlo, h_ready, silud, hidden, at_ready, ahi, alo, y_ready, y_copied) = (sem(n) for n in (
            "xt_ready", "xt_hi_done", "xt_lo_done", "h_ready", "silu_done", "hidden_done", "at_ready", "at_hi_done",
            "at_lo_done", "y_ready", "y_copied"))
        second_hi, ctx_hi = sem("second_hi_done"), sem("second_ctx_hi_done")
        ROWS2 = 4 * PAIRS
        UNROLL = 4
        LAG = 8

        def exists(j):
            return not isinstance(j, int) or 0 <= j < ITEMS

        def later(j, n=0):
            return not isinstance(j, int) or j > n

        def turns(eng, stages, first, last):
            def body(i, par):
                for stage, d in stages:
                    last_turns = stage.__name__ == "gate_up" and isinstance(i, int) and i in (ITEMS, ITEMS + 1)
                    if (exists(i + d) or last_turns) and (d != -LAG or not isinstance(i, int) or i + d < ROWS2):
                        stage(i + d, (par + d) % (UNROLL if d == -LAG else 2))
            staged(eng, body, first, LAG + UNROLL, ITEMS - 4, last, UNROLL)

        with nc.Block() as block:
            @block.sync
            def _(sp):
                def store(j, p):
                    sp.wait_ge(y_copied, j + 1)
                    sp.dma_start(ys_dram[ds(j * P, P), :], yo[:, p, :]).then_inc(y_out[p], 16)
                second.load_kq(sp)
                turns(sp, ((store, -1),), 0, ITEMS + 1)

            @block.gpsimd
            def _(pool):
                for j in range(ROWS2 + LAG + 4):
                    if j < ITEMS:
                        if j >= 2:
                            pool.wait_ge(xt_ready, j - 1)
                        pool.indirect_dma_start(xg[:, j % 2, :], None, xn_dram,
                                                bass.IndirectOffsetOnAxis(ap=token[:, j:j + 1], axis=0)).then_inc(x_in[j % 2], 16)
                    r = j - LAG - 4
                    if r == 0:
                        pool.wait_ge(ctx_hi, 1)
                        pool.tensor_tensor(second.ctl[:], second.ctx_raw[:], second.cth[:].bitcast(F32), ALU.subtract)
                    if r >= 0:
                        (hi, lo, raw), rows, first = second.part(r % 4)
                        row = r // 4 + first
                        pool.wait_ge(second_hi, r + 1)
                        pool.tensor_tensor(lo[rows, row, :], raw[rows, row, :], hi[rows, row, :].bitcast(F32), ALU.subtract)

            @block.tensor
            def _(pe):
                expert_down = [pe.alloc_register(f"expert_down{q}") for q in range(2)]
                expert = [pe.alloc_register(f"expert{q}") for q in range(2)]

                def transpose_x(j, p):
                    pe.wait_ge(x_in[p], (j // 2 + 1) * 16)
                    for k in range(KC):
                        mm = nc.tensor.transpose(ps_x[:, p, k * P:(k + 1) * P], xg[:, p, k * P:(k + 1) * P], c("ident"))
                    mm.then_inc(xt_ready, 1)

                def load_expert(j, p):
                    if later(j, 1):
                        pe.reg_load(expert[p], eid[0:1, ds(j, 1)])

                def transpose_a(j, p):
                    pe.wait_ge(hidden, j + 1)
                    for k in range(2):
                        mm = nc.tensor.transpose(ps_a[:, p, k * P:(k + 1) * P], act_a[:, p, k * P:(k + 1) * P], c("ident"))
                    mm.then_inc(at_ready, 1)

                def between(j, p):
                    if exists(j - 2):
                        down(j - 2, p)
                    if exists(j - 1):
                        transpose_a(j - 1, 1 - p)

                def gate_up(j, p):
                    if not exists(j):
                        between(j, p)
                        return
                    e, n = pe.snap(expert[p], min_val=0, max_val=NE - 1), 0
                    pe.wait_ge(xlo, j + 1)
                    for k in range(KC):
                        if k == 1:
                            between(j, p)
                            pe.reg_mov(expert_down[p], expert[p])
                        rh, rl = (w[:, ds(e * KC + k, 1), :].rearrange("p o f -> p (o f)") for w in (w1h, w1l))
                        for l, r in split3(xh[:, p, k * P:(k + 1) * P], xl[:, p, k * P:(k + 1) * P], rh, rl):
                            mm = nc.tensor.matmul(ps_h[:, p, :], l, r, start=(n == 0), stop=(n == KC * PASSES - 1))
                            n += 1
                    mm.then_inc(h_ready, 1)

                def down(j, p):
                    e, n = pe.snap(expert_down[p], min_val=0, max_val=NE - 1), 0
                    pe.wait_ge(alo, j + 1)
                    if later(j, 1):
                        pe.wait_ge(y_copied, j - 1)
                    for k in range(2):
                        rh, rl = (w[:, ds(e * 2 + k, 1), :].rearrange("p o f -> p (o f)") for w in (w2h, w2l))
                        for l, r in split3(ah[:, p, k * P:(k + 1) * P], al[:, p, k * P:(k + 1) * P], rh, rl):
                            mm = nc.tensor.matmul(ps_y[:, p, 0:C], l, r, start=(n == 0), stop=(n == 2 * PASSES - 1))
                            n += 1
                    mm.then_inc(y_ready, 1)
                keep_warm(nc, ps_y[:, 0, :], w1h[:, 0, :], 6)
                for j in range(2):
                    pe.reg_load(expert[j], eid[0:1, j:j + 1])
                turns(pe, ((gate_up, 0), (load_expert, 1), (transpose_x, 2)), -2, ITEMS + 2)

            @block.scalar
            def _(act):
                def x_high(j, p):
                    act.wait_ge(xt_ready, j + 1)
                    act.copy(xh[:, p, :], ps_x[:, p, 0:C]).then_inc(xhi, 1)

                def a_high(j, p):
                    act.wait_ge(at_ready, j + 1)
                    act.copy(ah[:, p, :], ps_a[:, p, 0:FF]).then_inc(ahi, 1)

                def silu(j, p):
                    act.wait_ge(h_ready, j + 1)
                    act.activation(sg[:, p, :], ps_h[:, p, 0:FF], ACT.Silu).then_inc(silud, 1)

                def y_copy(j, p):
                    act.wait_ge(y_ready, j + 1)
                    if later(j, 1):
                        act.wait_ge(y_out[p], (j // 2) * 16)
                    act.copy(yo[:, p, :], ps_y[:, p, 0:C]).then_inc(y_copied, 1)

                def second_high(r, p):
                    (hi, _, raw), rows, first = second.part(p)
                    if not isinstance(r, int) or r == 0:
                        act.wait_ge(second.loaded, second.all_loads)
                    if isinstance(r, int) and r == 0:
                        act.copy(second.cth[:], second.ctx_raw[:]).then_inc(ctx_hi, 1)
                    act.copy(hi[rows, ds(r // 4 + first, 1), :], raw[rows, ds(r // 4 + first, 1), :]).then_inc(second_hi, 1)
                act.activation(unread[:], c("ident")[:, 0:1], ACT.Silu)
                turns(act, ((y_copy, -2), (a_high, -1), (second_high, -LAG), (silu, 0), (x_high, 2)), -2, ITEMS + 2)

            @block.vector
            def _(dve):
                def x_low(j, p):
                    dve.wait_ge(xhi, j + 1)
                    dve.tensor_tensor(xl[:, p, :], ps_x[:, p, 0:C], xh[:, p, :].bitcast(F32), ALU.subtract).then_inc(xlo, 1)

                def a_low(j, p):
                    dve.wait_ge(ahi, j + 1)
                    dve.tensor_tensor(al[:, p, :], ps_a[:, p, 0:FF], ah[:, p, :].bitcast(F32), ALU.subtract).then_inc(alo, 1)

                def times_up(j, p):
                    dve.wait_ge(silud, j + 1)
                    dve.tensor_tensor(act_a[:, p, :], ps_h[:, p, FF:2 * FF], sg[:, p, :], ALU.mult).then_inc(hidden, 1)
                turns(dve, ((a_low, -1), (times_up, 0), (x_low, 2)), -2, ITEMS + 1)


def attention1(nc, c, second, ys_dram, ys_stored, xres, gates, mhalf, slots, wsel):
    with ExitStack() as keep:
        def sbuf(name, shape, dt=F32):
            return keep.enter_context(nc.sbuf_tensor(f"a1_{name}", shape, dt))

        bos = sbuf("bo_scaled", [P, C])
        ah, al = (sbuf(f"a_{s}", [P, KC, B, HK], F32R) for s in ("hi", "lo"))
        fold(nc, c, second, second.kq, None, ys_dram, ys_stored, xres, gates, slots, wsel, ah, al, bos)
        second.kq_memory.close()
        bh, bl = (sbuf(f"b_{s}", [P, B, PAIRS, C], F32R) for s in ("hi", "lo"))
        fold(nc, c, second, None, second.vo, ys_dram, ys_stored, xres, gates, slots, wsel, bh, bl, bos)
        second.vo_memory.close()
        attend1(nc, c, xres, mhalf, ah, al, bh, bl, bos)


class SecondWeights:

    def __init__(self, nc, ctxt, wqt1, wk1, wv1, wo1):
        self.nc, self.sources = nc, (ctxt, wqt1, wk1, wv1, wo1)
        self.kq_memory, self.vo_memory = ExitStack(), ExitStack()

        self.loaded = self.vo_memory.enter_context(nc.semaphore("second_loaded"))
        self.all_loads = 16 * (1 + 4 * PAIRS)

    def split(self, stack, name, shape):
        hi, lo = (stack.enter_context(self.nc.sbuf_tensor(f"second_{name}_{h}", shape, F32R, side="right")) for h in ("hi", "lo"))
        raw = self.nc.alloc_sbuf_tensor_at(f"second_{name}_raw", shape, F32, offset=self.nc.sbuf_top)
        return hi, lo, raw

    def place_vo(self):
        self.cth, self.ctl, self.ctx_raw = self.split(self.vo_memory, "ctx", [KP, 2, B * KV])
        self.vo = self.split(self.vo_memory, "vo", [P, 2 * PAIRS, C])

    def place_kq(self):
        self.kq = self.split(self.kq_memory, "kq", [P, 2 * PAIRS, C])

    def part(self, p):
        return (self.kq, self.vo)[p // 2], slice(0, P if p % 2 else KP), PAIRS * (p % 2)

    def load_pairs(self, eng, raw, narrow, wide):
        for j in range(PAIRS):
            cols = slice(j * P, (j + 1) * P)
            eng.dma_start(raw[0:KP, j, :].rearrange("p (k n) -> p k n", k=2),
                          narrow[:, cols].rearrange("(k p) n -> p k n", p=KP)).then_inc(self.loaded, 16)
            eng.dma_start(raw[:, PAIRS + j, :], wide[cols, :]).then_inc(self.loaded, 16)

    def load_vo(self, eng):
        ctxt, _, _, wv1, wo1 = self.sources
        eng.dma_start(self.ctx_raw[:], ctxt.rearrange("(k p) n -> p k n", p=KP)).then_inc(self.loaded, 16)
        self.load_pairs(eng, self.vo[2], wv1, wo1)

    def load_kq(self, eng):
        _, wqt1, wk1, _, _ = self.sources
        self.load_pairs(eng, self.kq[2], wk1, wqt1)


def fold(nc, c, second, kq, vo, ys_dram, ys_stored, xres, gates, slots, wsel, fh, fl, bos):
    keys = kq is not None
    wh, wl, _ = kq if keys else vo
    tag = "foldk" if keys else "foldv"
    with ExitStack() as ctx:
        def sbuf(name, shape, dt=F32):
            return ctx.enter_context(nc.sbuf_tensor(f"{tag}_{name}", shape, dt))

        def sem(name):
            return ctx.enter_context(nc.semaphore(f"{tag}_{name}"))

        DEPTH = 3
        tiles = range(0, TILES // 2) if keys else range(TILES // 2, TILES)
        first = tiles[0]
        yg = sbuf("gathered", [P, DEPTH, TOPK, C])
        th, tl = sbuf("projected_hi", [P, 2, B * P], F32R), sbuf("projected_lo", [P, 2, B * P], F32R)
        ps_kv = ctx.enter_context(nc.psum_tensor(f"{tag}_ps_kv", [P, 2, 512], F32))
        ps_f = ctx.enter_context(nc.psum_tensor(f"{tag}_ps_f", [P, 2, 2, 512], F32))
        g_in = [sem(f"gathered{n}") for n in range(DEPTH)]
        (cleared, kv_ready, kvhi, kvlo, f_ready, fhi, flo, comb) = (sem(n) for n in (
            "cleared", "kv_ready", "kv_hi_done", "kv_lo_done", "f_ready", "f_hi_done", "f_lo_done", "combined"))

        def projected(a, p, h):
            rows = slice(h * D1, (h + 1) * D1)
            return (ps_kv[rows, p, 0:B * KV].rearrange("p (b k) -> p b k", b=B),
                    a[rows, p, :].rearrange("p (b h k) -> p b h k", b=B, h=2)[:, :, h, :])

        def folded(a, j, m):
            ps = ps_f[:, j % 2, m, :]
            if keys:
                return ps.rearrange("p (b n) -> p b n", b=B), a[:, m, :, j * P:(j + 1) * P]
            return ps.rearrange("p (b c) -> p b c", b=2), a[:, 2 * m:2 * m + 2, j, :]

        with nc.Block() as block:
            @block.gpsimd
            def _(pool):
                if keys:
                    for p in range(2):
                        pool.wait_ge(ys_stored[p], 16 * ITEMS // 2)
                for i, t in enumerate(tiles):
                    if i >= DEPTH:
                        pool.wait_ge(comb, TOPK * (i - DEPTH + 1))
                    for n in range(TOPK):
                        pool.indirect_dma_start(yg[:, i % DEPTH, n, :], None, ys_dram,
                                                bass.IndirectOffsetOnAxis(ap=slots[:, n, t:t + 1], axis=0)).then_inc(g_in[i % DEPTH], 16)

            @block.scalar
            def _(act):
                def projected_high(j):
                    if j < 2:
                        act.wait_ge(cleared, 2 * (j + 1))
                    act.wait_ge(kv_ready, j + 1)
                    if j >= 2:
                        act.wait_ge(f_ready, 2 * (j - 1))
                    for h in range(2):
                        src, dst = projected(th, j % 2, h)
                        act.activation(dst, src, ACT.Copy, scale=D1 ** -0.5 if keys else 1.0).then_inc(kvhi, 1)

                def folded_high(j):
                    for m in range(2):
                        act.wait_ge(f_ready, 2 * j + m + 1)
                        src, dst = folded(fh, j, m)
                        if keys:
                            act.copy(dst, src).then_inc(fhi, 1)
                        else:
                            act.activation(dst, src, ACT.Identity, scale=gates[:, 1:2]).then_inc(fhi, 1)
                projected_high(0)
                for j in range(PAIRS):
                    if j + 1 < PAIRS:
                        projected_high(j + 1)
                    folded_high(j)

            @block.vector
            def _(dve):
                for p in range(2):
                    for a in (th, tl):
                        dve.memset(a[:, p].bitcast(F32), 0.0).then_inc(cleared, 1)
                if keys:
                    dve.tensor_scalar(bos[:], c("bout1"), gates[:, 1:2], None, ALU.mult)
                dve.wait_ge(cleared, 4)

                def projected_low(j):
                    for h in range(2):
                        dve.wait_ge(kvhi, 2 * j + h + 1)
                        src, dst = projected(tl, j % 2, h)
                        _, hi = projected(th, j % 2, h)
                        dve.scalar_tensor_tensor(out=dst, in0=src, scalar=D1 ** -0.5 if keys else 1.0, in1=hi.bitcast(F32),
                                                 op0=ALU.mult, op1=ALU.subtract).then_inc(kvlo, 1)

                def folded_low(j):
                    for m in range(2):
                        dve.wait_ge(fhi, 2 * j + m + 1)
                        src, dst = folded(fl, j, m)
                        _, hi = folded(fh, j, m)
                        if keys:
                            dve.tensor_tensor(dst, src, hi.bitcast(F32), ALU.subtract).then_inc(flo, 1)
                        else:
                            dve.scalar_tensor_tensor(out=dst, in0=src, scalar=gates[:, 1:2], in1=hi.bitcast(F32),
                                                     op0=ALU.mult, op1=ALU.subtract).then_inc(flo, 1)

                def combine(i, n):
                    t = first + i
                    dve.wait_ge(g_in[i % DEPTH], 16 * TOPK * (i // DEPTH + 1))
                    if n:
                        dve.wait_ge(comb, TOPK * i + 1)
                    dve.scalar_tensor_tensor(out=xres[:, t, :], in0=yg[:, i % DEPTH, n, :], scalar=wsel[:, n, t:t + 1],
                                             in1=xres[:, t, :], op0=ALU.mult, op1=ALU.add).then_inc(comb, 1)

                projected_low(0)
                for j in range(PAIRS):
                    if j + 1 < PAIRS:
                        projected_low(j + 1)
                    combine(j, 0)
                    folded_low(j)
                    combine(j, 1)

            @block.tensor
            def _(pe):
                def project(j):
                    if j >= 2:
                        pe.wait_ge(kvlo, 2 * (j - 1))
                    q = 0
                    for k in range(2):
                        ks = slice(k * P, (k + 1) * P)
                        for l, r in split3(wh[0:KP, j, ks], wl[0:KP, j, ks], second.cth[:, k, :], second.ctl[:, k, :]):
                            mm = nc.tensor.matmul(ps_kv[:, j % 2, 0:B * KV], l, r, start=(q == 0), stop=(q == 2 * PASSES - 1))
                            q += 1
                    mm.then_inc(kv_ready, 1)

                def banks_free(j):
                    if j >= 2:
                        pe.wait_ge(flo, 2 * (j - 1))

                def fold_keys(j):
                    p, row = j % 2, PAIRS + j
                    pe.wait_ge(kvlo, 2 * (j + 1))
                    banks_free(j)
                    for m in range(KC):
                        ms = slice(m * P, (m + 1) * P)
                        for n, (l, r) in enumerate(split3(wh[:, row, ms], wl[:, row, ms], th[:, p, :], tl[:, p, :])):
                            mm = nc.tensor.matmul(ps_f[:, p, m, :], l, r, start=(n == 0), stop=(n == PASSES - 1))
                        mm.then_inc(f_ready, 1)

                def fold_values(j):
                    p, row = j % 2, PAIRS + j
                    pe.wait_ge(kvlo, 2 * (j + 1))
                    banks_free(j)
                    for b in range(B):
                        bs = slice(b * P, (b + 1) * P)
                        for n, (l, r) in enumerate(split3(th[:, p, bs], tl[:, p, bs], wh[:, row, :], wl[:, row, :])):
                            mm = nc.tensor.matmul(ps_f[:, p, b // 2, (b % 2) * C:(b % 2 + 1) * C], l, r, start=(n == 0), stop=(n == PASSES - 1))
                        if b % 2:
                            mm.then_inc(f_ready, 1)

                project(0)
                project(1)
                for j in range(PAIRS):
                    fold_keys(j) if keys else fold_values(j)
                    if j + 2 < PAIRS:
                        project(j + 2)


def attend1(nc, c, xres, mhalf, ah, al, bh, bl, bos):
    with ExitStack() as ctx:
        def sbuf(name, shape, dt=F32):
            return ctx.enter_context(nc.sbuf_tensor(f"att1_{name}", shape, dt))

        def sem(name):
            return ctx.enter_context(nc.semaphore(f"att1_{name}"))

        def bank(name, *n):
            return ctx.enter_context(nc.psum_tensor(f"att1_{name}", [P, *n, 512], F32))

        st, mv = sbuf("ln_stats", [P, 2, 6]), sbuf("ln_mean_var", [P, 2, 2])
        ve, rs = sbuf("ln_var_eps", [P, 2]), sbuf("ln_rstd", [P, 2])
        xn = sbuf("xn", [P, 2, C])
        xh, xl = sbuf("xt_hi", [P, 2, C], F32R), sbuf("xt_lo", [P, 2, C], F32R)
        sc = sbuf("scores", [P, 2, HK])
        mx, sm, rc = (sbuf(n, [P, 2, H]) for n in ("score_max", "exp_sum", "recip"))
        ph, pl = sbuf("pt_hi", [P, HK], F32R), sbuf("pt_lo", [P, HK], F32R)
        ps_s, ps_p = bank("ps_scores", 2, 2), bank("ps_pt", 2)
        ps_x, ps_y = bank("ps_xt", 1), bank("ps_y", 1)
        (xt_ready, s_ready, pt_ready, y_ready, xhi, phi, expd, lnve, lnrs, lndone, xlo, maxd, cent, sumd, recd, plo,
         resd, xbias, normd, copied) = (sem(n) for n in (
             "xt_ready", "scores_ready", "pt_ready", "y_ready", "xt_hi_done", "pt_hi_done", "exp_done", "ln_ve_done", "ln_rstd_done", "ln_done", "xt_lo_done", "max_done", "centred", "sum_done", "recip_done",
             "pt_lo_done", "residual_done", "bias_added", "probs_normed", "scores_copied"))

        def wide(a):
            return a.rearrange("p (h o) -> p h o", o=1).broadcast_to([P, H, KV])

        def heads(a):
            return a.rearrange("p (h k) -> p h k", k=KV)

        def turns(eng, stages, first, last):
            def body(i, par):
                for stage, d in stages:
                    if live(i + d):
                        stage(i + d, (par + d) % 2)
            staged(eng, body, first, 6, 12, last)

        with nc.Block() as block:
            @block.tensor
            def _(pe):
                def transpose_probs(t, p):
                    pe.wait_ge(normd, t + 1)
                    for j in range(PAIRS):
                        mm = nc.tensor.transpose(ps_p[:, j // 4, (j % 4) * P:(j % 4 + 1) * P], sc[:, p, j * P:(j + 1) * P], c("ident"))
                        if j % 4 == 3:
                            mm.then_inc(pt_ready, 1)

                def scores(t, p):
                    pe.wait_ge(xlo, t + 1)
                    if not isinstance(t, int) or t > 1:
                        pe.wait_ge(copied, t - 1)
                    for half in range(2):
                        n = 0
                        for k in range(KC):
                            rh, rl = (w[:, k, ds(t // TPB, 1), half * 512:(half + 1) * 512].rearrange("p o n -> p (o n)") for w in (ah, al))
                            for l, r in split3(xh[:, p, k * P:(k + 1) * P], xl[:, p, k * P:(k + 1) * P], rh, rl):
                                mm = nc.tensor.matmul(ps_s[:, p, half, :], l, r, start=(n == 0), stop=(n == KC * PASSES - 1))
                                n += 1
                    mm.then_inc(s_ready, 1)

                def transpose_x(t, p):
                    pe.wait_ge(lndone, t + 1)
                    for k in range(KC):
                        mm = nc.tensor.transpose(ps_x[:, 0, k * P:(k + 1) * P], xn[:, p, k * P:(k + 1) * P], c("ident"))
                    mm.then_inc(xt_ready, 1)

                def outputs(t, p):
                    pe.wait_ge(plo, 2 * t + 2)
                    if not isinstance(t, int) or t > 0:
                        pe.wait_ge(resd, t)
                    n = 0
                    for j in range(PAIRS):
                        rh, rl = (w[:, ds(t // TPB, 1), j, :].rearrange("p o n -> p (o n)") for w in (bh, bl))
                        for l, r in split3(ph[:, j * P:(j + 1) * P], pl[:, j * P:(j + 1) * P], rh, rl):
                            mm = nc.tensor.matmul(ps_y[:, 0, 0:C], l, r, start=(n == 0), stop=(n == PAIRS * PASSES - 1))
                            n += 1
                    mm.then_inc(y_ready, 1)
                turns(pe, ((transpose_probs, -2), (scores, 0), (outputs, -2), (transpose_x, 2)), -2, TILES + 2)

            @block.scalar
            def _(act):
                def copy_scores(t, p):
                    act.wait_ge(s_ready, t + 1)
                    if not isinstance(t, int) or t > 1:
                        act.wait_ge(pt_ready, 2 * t - 2)
                    act.copy(sc[:, p, :].rearrange("p (a n) -> p a n", a=2), ps_s[:, p]).then_inc(copied, 1)

                def exponential(t, p):
                    act.wait_ge(cent, t + 1)
                    act.activation(sc[:, p, :], sc[:, p, :], ACT.Exp).then_inc(expd, 1)

                def probs_high(t, p):
                    for half in range(2):
                        act.wait_ge(pt_ready, 2 * t + half + 1)
                        if half == 0 and (not isinstance(t, int) or t > 0):
                            act.wait_ge(y_ready, t)
                        act.copy(ph[:, half * 512:(half + 1) * 512], ps_p[:, half, :]).then_inc(phi, 1)

                def x_high(t, p):
                    act.wait_ge(xt_ready, t + 1)
                    act.copy(xh[:, p, :], ps_x[:, 0, 0:C]).then_inc(xhi, 1)
                turns(act, ((x_high, 1), (probs_high, -2), (exponential, -1), (copy_scores, 0)), -1, TILES + 2)

            @block.gpsimd
            def _(pool):
                def rstd(t, p):
                    pool.wait_ge(lnve, t + 1)
                    pool.tensor_tensor(rs[:, p:p + 1], ve[:, p:p + 1], mhalf[:], ALU.pow).then_inc(lnrs, 1)

                def normalise(t, p):
                    pool.wait_ge(recd, t + 1)
                    pool.tensor_tensor(heads(sc[:, p, :]), heads(sc[:, p, :]), wide(rc[:, p, :]), ALU.mult).then_inc(normd, 1)

                def centre(t, p):
                    pool.wait_ge(maxd, t + 1)
                    pool.tensor_tensor(heads(sc[:, p, :]), heads(sc[:, p, :]), wide(mx[:, p, :]), ALU.subtract).then_inc(cent, 1)

                def bias(t, p):
                    pool.wait_ge(s_ready, t + 1)
                    pool.wait_ge(lnrs, 1)
                    xt = xres[:, ds(t, 1), :].rearrange("p o c -> p (o c)")
                    pool.tensor_tensor(xt, xt, bos[:], ALU.add).then_inc(xbias, 1)
                turns(pool, ((normalise, -1), (centre, 0), (rstd, 3), (bias, 0)), -3, TILES + 1)

            @block.vector
            def _(dve):
                def tile_of(t):
                    return xres[:, ds(t, 1), :].rearrange("p o c -> p (o c)")

                def stats(t, p):
                    dve.bn_stats(st[:, p, :], tile_of(t))
                    dve.drain()
                    dve.bn_aggr(mv[:, p, :], st[:, p, :])
                    dve.drain()
                    dve.tensor_scalar(ve[:, p:p + 1], mv[:, p, 1:2], EPS, None, ALU.add).then_inc(lnve, 1)

                def layer_norm(t, p):
                    dve.wait_ge(lnrs, t + 1)
                    dve.tensor_scalar(xn[:, p, :], tile_of(t), mv[:, p, 0:1], rs[:, p:p + 1], ALU.subtract, ALU.mult).then_inc(lndone, 1)

                def x_low(t, p):
                    dve.wait_ge(xhi, t + 1)
                    dve.tensor_tensor(xl[:, p, :], ps_x[:, 0, 0:C], xh[:, p, :].bitcast(F32), ALU.subtract).then_inc(xlo, 1)

                def sums(t, p):
                    dve.wait_ge(expd, t + 1)
                    dve.tensor_reduce(sm[:, p, :], heads(sc[:, p, :]), AX.X, ALU.add).then_inc(sumd, 1)
                    dve.wait_ge(sumd, t + 1)
                    dve.reciprocal(rc[:, p, :], sm[:, p, :]).then_inc(recd, 1)

                def probs_low(t, p):
                    for half in range(2):
                        hs = slice(half * 512, (half + 1) * 512)
                        dve.wait_ge(phi, 2 * t + half + 1)
                        dve.tensor_tensor(pl[:, hs], ps_p[:, half, :], ph[:, hs].bitcast(F32), ALU.subtract).then_inc(plo, 1)

                def maxima(t, p):
                    dve.wait_ge(copied, t + 1)
                    dve.tensor_reduce(mx[:, p, :], heads(sc[:, p, :]), AX.X, ALU.max).then_inc(maxd, 1)

                def residual(t, p):
                    dve.wait_ge(y_ready, t + 1)
                    dve.wait_ge(xbias, t + 1)
                    dve.tensor_tensor(tile_of(t), ps_y[:, 0, 0:C], tile_of(t), ALU.add).then_inc(resd, 1)
                turns(dve, ((residual, -3), (x_low, 1), (probs_low, -2), (layer_norm, 2), (sums, -1), (maxima, 0), (stats, 3)), -3, TILES + 3)


def mlp1(nc, c, fwin, fwout, xres, gates, mhalf, out):
    with ExitStack() as ctx:
        def sbuf(name, shape, dt=F32):
            return ctx.enter_context(nc.sbuf_tensor(f"mlp_{name}", shape, dt))

        def sem(name):
            return ctx.enter_context(nc.semaphore(f"mlp_{name}"))

        UN = INNER // 2
        UP = 3
        UV = UN - UP
        PSTEPS = 2 * UP - 1
        HALF = S // 2
        st, mv = sbuf("ln_stats", [P, TILES, 6]), sbuf("ln_mean_var", [P, TILES, 2])
        ve, rs, shift = sbuf("ln_var_eps", [P, TILES]), sbuf("ln_rstd", [P, TILES]), sbuf("ln_shift", [P, TILES])
        xn = sbuf("xn", [P, 2, TPB, C])
        xh, xl = sbuf("xt_hi", [P, 2, KC, S], F32R), sbuf("xt_lo", [P, 2, KC, S], F32R)
        wi, wo = ([sbuf(f"{n}_raw", [P, KC, w]), sbuf(f"{n}_hi", [P, KC, w], F32R), sbuf(f"{n}_lo", [P, KC, w], F32R)]
                  for n, w in (("win", P), ("wout", P)))
        wos, bos, ub, t1 = sbuf("wout_gated", [P, KC, P]), sbuf("bout_gated", [P, C]), sbuf("unit_bias", [P, UN]), sbuf("w1_bin", [P, UN])
        hb = sbuf("units", [P, 2, UN, S])
        g, gp = sbuf("g", [P, 2, S]), sbuf("g_of_gpsimd", [P, 2, S])
        gh, gl = sbuf("g_hi", [P, 2, S], F32R), sbuf("g_lo", [P, 2, S], F32R)
        ps_x = ctx.enter_context(nc.psum_tensor("mlp_ps_xt", [P, KC, 512], F32))
        ps_s = ctx.enter_context(nc.psum_tensor("mlp_ps_s", [P, 2, 512], F32))
        ps_y = ctx.enter_context(nc.psum_tensor("mlp_ps_y", [P, 2, 512], F32))
        w_in, gated, whi, wlo, ubias = sem("w_in"), sem("wout_gated_done"), sem("w_hi_done"), sem("w_lo_done"), sem("unit_bias_done")
        (lnst, lnmv, lnve, lnrs, lndone, xt_ready, xhi, xlo, s_ready, relud, acc, ghi, glo, y_ready, resd, xbias, stored) = (sem(n) for n in (
            "ln_stats_done", "ln_mv_done", "ln_ve_done", "ln_rstd_done", "ln_done", "xt_ready", "xt_hi_done", "xt_lo_done",
            "s_ready", "relu_done", "accumulated", "g_hi_done", "g_lo_done", "y_ready", "residual_done", "bias_added", "stored"))
        pacc, summed, lnshift = sem("accumulated_on_gpsimd"), sem("g_summed"), sem("ln_shift_done")

        with nc.Block() as block:
            @block.sync
            def _(sp):
                sp.dma_start(wi[0][:], fwin.rearrange("(k p) n -> p k n", p=P)).then_inc(w_in, 16)
                sp.dma_start(wo[0][:], fwout.rearrange("p (k n) -> p k n", k=KC)).then_inc(w_in, 16)
                for b in range(B):
                    for q in range(2):
                        sp.wait_ge(resd, 2 * b + q + 1)
                        sp.dma_start(out[b][q * HALF:(q + 1) * HALF].rearrange("(t p) c -> p t c", p=P),
                                     xres[:, b * TPB + 2 * q:b * TPB + 2 * q + 2, :]).then_inc(stored, 16)
                sp.wait_ge(stored, 32 * B)

            @block.gpsimd
            def _(pool):
                def rstd(b):
                    bt = slice(b * TPB, (b + 1) * TPB)
                    pool.wait_ge(lnve, b + 1)
                    pool.tensor_tensor(rs[:, bt], ve[:, bt], mhalf[:].broadcast_to([P, TPB]), ALU.pow).then_inc(lnrs, 1)

                def bias(b):
                    bt = slice(b * TPB, (b + 1) * TPB)
                    pool.wait_ge(lndone, TPB * (b + 1))
                    pool.tensor_tensor(xres[:, bt, :], xres[:, bt, :], bos[:].rearrange("p (o c) -> p o c", o=1).broadcast_to([P, TPB, C]),
                                       ALU.add).then_inc(xbias, 1)

                def accumulate(b):
                    p = b % 2
                    for n in range(UP):
                        pool.wait_ge(relud, b * UN + n + 1)
                        if n == 0 and b >= 2:
                            pool.wait_ge(summed, 2 * (b - 1))
                        dst = gp[:, p, :] if n == 0 else hb[:, p, n, :]
                        pool.tensor_tensor(dst, hb[:, p, n, :], c("fw2")[:, n:n + 1].broadcast_to([P, S]), ALU.mult).then_inc(pacc, 1)
                        if n:
                            pool.wait_ge(pacc, b * PSTEPS + 2 * n)
                            pool.tensor_tensor(gp[:, p, :], gp[:, p, :], hb[:, p, n, :], ALU.add).then_inc(pacc, 1)
                for b in range(3):
                    rstd(b)
                pool.wait_ge(gated, 3)
                for b in range(B):
                    bias(b)
                    accumulate(b)
                    if b + 3 < B:
                        rstd(b + 3)

            @block.scalar
            def _(act):
                def x_high(b):
                    act.wait_ge(xt_ready, b + 1)
                    if b >= 2:
                        act.wait_ge(s_ready, b - 1)
                    act.copy(xh[:, b % 2], ps_x[:]).then_inc(xhi, 1)

                def layer_norm(b):
                    act.wait_ge(lnshift, b + 1)
                    if b >= 2:
                        act.wait_ge(xt_ready, b - 1)
                    for u in range(TPB):
                        t = b * TPB + u
                        act.activation(xn[:, b % 2, u, :], xres[:, t, :], ACT.Identity, bias=shift[:, t:t + 1], scale=rs[:, t:t + 1]).then_inc(lndone, 1)

                def g_high(b):
                    act.wait_ge(summed, 2 * (b + 1))
                    act.copy(gh[:, b % 2, :], g[:, b % 2, :]).then_inc(ghi, 1)

                layer_norm(0)
                act.wait_ge(w_in, 32)
                act.copy(wi[1][:], wi[0][:]).then_inc(whi, 1)
                x_high(0)
                act.wait_ge(gated, 3)
                act.copy(wo[1][:], wos[:]).then_inc(whi, 1)
                layer_norm(1)
                act.wait_ge(ubias, 2)
                for b in range(B):
                    act.wait_ge(s_ready, b + 1)
                    if b >= 2:
                        act.wait_ge(acc, 2 * UV * (b - 1))
                        act.wait_ge(pacc, PSTEPS * (b - 1))
                    for u in range(UN):
                        act.activation(hb[:, b % 2, u, :], ps_s[:, b % 2, :], ACT.Relu, bias=ub[:, u:u + 1],
                                       scale=c("fw1")[:, u:u + 1]).then_inc(relud, 1)
                        if u == 1 and b >= 1:
                            g_high(b - 1)
                        if u == 3 and b + 1 < B:
                            x_high(b + 1)
                    if b + 2 < B:
                        layer_norm(b + 2)
                g_high(B - 1)

            @block.vector
            def _(dve):
                def stats(b):
                    for t in range(b * TPB, (b + 1) * TPB):
                        dve.bn_stats(st[:, t, :], xres[:, t, :]).then_inc(lnst, 1)
                    for t in range(b * TPB, (b + 1) * TPB):
                        dve.wait_ge(lnst, t + 1)
                        dve.bn_aggr(mv[:, t, :], st[:, t, :]).then_inc(lnmv, 1)
                    bt = slice(b * TPB, (b + 1) * TPB)
                    dve.wait_ge(lnmv, TPB * (b + 1))
                    dve.tensor_scalar(ve[:, bt], mv[:, bt, 1], EPS, None, ALU.add).then_inc(lnve, 1)

                def shifts(b):
                    bt = slice(b * TPB, (b + 1) * TPB)
                    dve.wait_ge(lnrs, b + 1)
                    dve.scalar_tensor_tensor(out=shift[:, bt], in0=mv[:, bt, 0], scalar=-1.0, in1=rs[:, bt],
                                             op0=ALU.mult, op1=ALU.mult).then_inc(lnshift, 1)

                def x_low(b):
                    dve.wait_ge(xhi, b + 1)
                    if b >= 2:
                        dve.wait_ge(s_ready, b - 1)
                    dve.tensor_tensor(xl[:, b % 2], ps_x[:], xh[:, b % 2].bitcast(F32), ALU.subtract).then_inc(xlo, 1)

                def accumulate(b, units):
                    p = b % 2
                    for u in units:
                        dve.wait_ge(relud, b * UN + u + 1)
                        for h in range(2):
                            hs = slice(h * HALF, (h + 1) * HALF)
                            if u == UP:
                                if b >= 2:
                                    dve.wait_ge(glo, b - 1)
                                dve.tensor_scalar(g[:, p, hs], hb[:, p, u, hs], c("fw2")[:, u:u + 1], c("fb2"), ALU.mult, ALU.add).then_inc(acc, 1)
                            else:
                                dve.wait_ge(acc, 2 * (b * UV + u - UP - 1) + h + 1)
                                dve.scalar_tensor_tensor(out=g[:, p, hs], in0=hb[:, p, u, hs], scalar=c("fw2")[:, u:u + 1], in1=g[:, p, hs],
                                                         op0=ALU.mult, op1=ALU.add).then_inc(acc, 1)

                def sum_parts(b):
                    p = b % 2
                    dve.wait_ge(pacc, PSTEPS * (b + 1))
                    for h in range(2):
                        hs = slice(h * HALF, (h + 1) * HALF)
                        dve.wait_ge(acc, 2 * UV * (b + 1) - 1 + h)
                        dve.tensor_tensor(g[:, p, hs], g[:, p, hs], gp[:, p, hs], ALU.add).then_inc(summed, 1)

                def g_low(b):
                    dve.wait_ge(ghi, b + 1)
                    dve.tensor_tensor(gl[:, b % 2, :], g[:, b % 2, :], gh[:, b % 2, :].bitcast(F32), ALU.subtract).then_inc(glo, 1)

                def residual(b):
                    dve.wait_ge(xbias, b + 1)
                    for q in range(2):
                        dve.wait_ge(y_ready, 2 * b + q + 1)
                        xt = xres[:, b * TPB + 2 * q:b * TPB + 2 * q + 2, :]
                        dve.tensor_tensor(xt, ps_y[:, q, :].rearrange("p (t c) -> p t c", t=2), xt, ALU.add).then_inc(resd, 1)

                stats(0)
                dve.tensor_scalar(bos[:], c("fbout"), gates[:, 3:4], None, ALU.mult).then_inc(gated, 1)
                dve.tensor_scalar(t1[:], c("fw1"), c("fbin"), None, ALU.mult).then_inc(ubias, 1)
                dve.wait_ge(ubias, 1)
                dve.tensor_tensor(ub[:], t1[:], c("fb1"), ALU.add).then_inc(ubias, 1)
                dve.wait_ge(w_in, 32)
                dve.tensor_scalar(wos[:], wo[0][:], gates[:, 3:4], None, ALU.mult).then_inc(gated, 2)
                shifts(0)
                stats(1)
                dve.wait_ge(whi, 1)
                dve.tensor_tensor(wi[2][:], wi[0][:], wi[1][:].bitcast(F32), ALU.subtract).then_inc(wlo, 1)
                x_low(0)
                shifts(1)
                dve.wait_ge(whi, 2)
                dve.tensor_tensor(wo[2][:], wos[:], wo[1][:].bitcast(F32), ALU.subtract).then_inc(wlo, 1)
                stats(2)
                shifts(2)
                for b in range(B):
                    if b >= 1:
                        g_low(b - 1)
                    accumulate(b, range(UP, UP + 1))
                    if b + 1 < B:
                        x_low(b + 1)
                    accumulate(b, range(UP + 1, UN))
                    if b + 3 < B:
                        stats(b + 3)
                    if b >= 1:
                        residual(b - 1)
                    sum_parts(b)
                    if b + 3 < B:
                        shifts(b + 3)
                g_low(B - 1)
                residual(B - 1)

            @block.tensor
            def _(pe):
                def transpose_x(b):
                    pe.wait_ge(lndone, TPB * (b + 1))
                    for u in range(TPB):
                        for k in range(KC):
                            mm = nc.tensor.transpose(ps_x[:, k, u * P:(u + 1) * P], xn[:, b % 2, u, k * P:(k + 1) * P], c("ident"))
                    mm.then_inc(xt_ready, 1)

                def sums(b):
                    pe.wait_ge(xlo, b + 1)
                    if b >= 2:
                        pe.wait_ge(relud, UN * (b - 1))
                    n = 0
                    for k in range(KC):
                        for l, r in split3(wi[1][:, k, :], wi[2][:, k, :], xh[:, b % 2, k, :], xl[:, b % 2, k, :]):
                            mm = nc.tensor.matmul(ps_s[:, b % 2, :], l, r, start=(n == 0), stop=(n == KC * PASSES - 1))
                            n += 1
                    mm.then_inc(s_ready, 1)

                def outputs(b):
                    pe.wait_ge(wlo, 2)
                    pe.wait_ge(glo, b + 1)
                    if b >= 1:
                        pe.wait_ge(resd, 2 * b)
                    for u in range(TPB):
                        us = slice(u * P, (u + 1) * P)
                        rh, rl = (w[:].rearrange("p k n -> p (k n)") for w in wo[1:])
                        for n, (l, r) in enumerate(split3(gh[:, b % 2, us], gl[:, b % 2, us], rh, rl)):
                            mm = nc.tensor.matmul(ps_y[:, u // 2, (u % 2) * C:(u % 2 + 1) * C], l, r, start=(n == 0), stop=(n == PASSES - 1))
                        if u % 2:
                            mm.then_inc(y_ready, 1)

                transpose_x(0)
                pe.wait_ge(wlo, 1)
                sums(0)
                transpose_x(1)
                for b in range(B):
                    if b >= 1:
                        outputs(b - 1)
                    if b + 1 < B:
                        sums(b + 1)
                    if b + 2 < B:
                        transpose_x(b + 2)
                outputs(B - 1)


def packed_rows(i):
    f = np.float32
    p = np.arange(P)

    def rep(a):
        return np.broadcast_to(np.reshape(a, (1, -1)), (P, np.size(a)))

    def cols(a):
        return np.reshape(a, (-1, P)).T

    def halves(a):
        return np.concatenate([a[:, :INNER // 2], a[:, INNER // 2:]], axis=0)

    parts = {
        "ident": np.eye(P, dtype=f), "tri": np.triu(np.ones((P, P), f), 1),
        "mask": (p[:, None] // D0 == np.arange(P // D0)[None, :]).astype(f),
        "rev": rep(np.arange(NE, 0, -1, dtype=f)), "item": rep(np.arange(ITEMS, dtype=f)), "ones": np.ones((P, P), f),
        "bq": cols(i["L0_xattn_bq"]), "bk": cols(i["L0_xattn_bk"]), "bv": cols(i["L0_xattn_bv"]), "bo": rep(i["L0_xattn_bo"]),
        "bg": rep(i["L0_ffn_bg"]), "gx": rep(i["g_xattn"]), "gf": rep(i["g_ffn"]), "bout1": rep(i["L1_xattn_b_out"]),
        "fbin": np.reshape(np.concatenate([i["L1_ffn_bin_"]] * 2), (P, 1)),
        "fw1": halves(i["L1_ffn_W1"]), "fb1": halves(i["L1_ffn_b1"]), "fw2": halves(i["L1_ffn_W2"]),
        "fb2": np.reshape(np.concatenate([i["L1_ffn_b2"], np.zeros(M1, f)]), (P, 1)), "fbout": rep(i["L1_ffn_bout"]),
        "scan": rep((np.arange(P) % TILES != 0).astype(f)),
        "place": rep(np.arange(P, dtype=f)), "token": (np.arange(TILES)[None, :] * P + p[:, None]).astype(f),
    }
    return np.concatenate([parts[n] for n, _ in ROWS], axis=1)


def laid_out(i):
    return {
        "x": i["x"], "ctxt": np.reshape(np.transpose(i["ctx_768"], (2, 0, 1)), (CK, B * KV)),
        "wq0": i["L0_xattn_Wq"], "wk0": i["L0_xattn_Wk"], "wv0": i["L0_xattn_Wv"], "wo0": i["L0_xattn_Wo"],
        "wg": np.transpose(i["L0_ffn_Wg"]),
        "w1": np.transpose(i["L0_ffn_w1"], (0, 2, 1)), "w2": np.transpose(i["L0_ffn_w2"], (0, 2, 1)),
        "wqt1": np.transpose(i["L1_xattn_w_q"]), "wk1": i["L1_xattn_w_k"], "wv1": i["L1_xattn_w_v"], "wo1": i["L1_xattn_w_out"],
        "fwin": np.concatenate([i["L1_ffn_Win"]] * 2, axis=1), "fwout": np.concatenate([i["L1_ffn_Wout"]] * 2, axis=0),
        "rows": packed_rows(i),
    }


def kernel(**inputs):
    import concourse.bacc as bacc
    from concourse.bass_utils import run_bass_kernel_spmd

    nc = bacc.Bacc("TRN2", target_bir_lowering=False, num_devices=1)
    arrays, args = {}, []
    for name, a in laid_out({k: np.asarray(v) for k, v in inputs.items()}).items():
        arrays[f"in_{name}"] = np.ascontiguousarray(a)
        args.append(nc.dram_tensor(f"in_{name}", a.shape, mybir.dt.from_np(a.dtype), kind="ExternalInput").ap())
    args.append(nc.dram_tensor("out", (B, S, C), F32, kind="ExternalOutput").ap())
    gated_blocks(nc, *args)
    return run_bass_kernel_spmd(nc, [arrays], core_ids=[0]).results[0]["out"]
```
